# Optimizing a Trainium2 kernel written in Bass

```python
import numpy as np
import jax
import jax.numpy as jnp

def _softmax(x, axis=-1):
    return jax.nn.softmax(x, axis=axis)

def _gelu(x):
    return jax.nn.gelu(x, approximate=True)

def _silu(x):
    return jax.nn.silu(x)

def _sigmoid(x):
    return jax.nn.sigmoid(x)

def _layernorm(x, axis=-1, eps=1e-05):
    m = jnp.mean(x, axis=axis, keepdims=True)
    v = jnp.var(x, axis=axis, keepdims=True)
    return (x - m) / jnp.sqrt(v + eps)

def _scatter_add(tgt, idx, src, axis=0):
    return tgt.at[idx].add(src)

def _segment_sum(src, seg, n):
    return jax.ops.segment_sum(src, seg, n)
kernel_name = 'mk_early_fusion_d1_tok_img1024_r4_447c3b'

def setup_inputs(seed: int=0):
    np.random.seed(seed)
    _w = jnp.asarray

    def _rec_inputs():
        import jax
        import jax.numpy as jnp
        _rk = jax.random.key(seed)
        x = -0.000125008 + 0.999885 * jax.random.normal(jax.random.fold_in(_rk, 1), (16, 512, 256, 4), jnp.float32)
        txt = -8.03667e-05 + 0.656214 * jax.random.normal(jax.random.fold_in(_rk, 2), (16, 128, 256), jnp.float32)
        return (x, txt)
    x, txt = _rec_inputs()

    def _L0_tok_setup():
        import jax, jax.numpy as jnp
        import numpy as np
        key = jax.random.key(seed)
        k1, k2, k3 = jax.random.split(key, 3)
        B, H, I, O, Dp1 = (4, 512, 256, 256, 4)
        x = jax.random.normal(k1, (B, H, I, Dp1), dtype=jnp.float32)
        weight = 0.1 * jax.random.normal(k2, (O, Dp1), dtype=jnp.float32)
        weighted_sum = 0.1 * jax.random.normal(k3, (O, I), dtype=jnp.float32)
        return {'x': x, 'weight': weight, 'weighted_sum': weighted_sum}
    _L0_tok_all = _L0_tok_setup()
    _L0_tok_in = {k: v for k, v in _L0_tok_all.items() if k in ('weight', 'weighted_sum')}
    del _L0_tok_all

    def _L0_attn_setup():
        import jax, jax.numpy as jnp
        import numpy as np
        SL, BS, E, H, PF, STRIDE, SHIFT = (512, 2, 256, 16, 16, 1, 0)
        DH = E // H

        def _layernorm(x, g, b, eps=1e-05):
            m = x.mean(-1, keepdims=True)
            v = jnp.var(x, axis=-1, keepdims=True)
            return (x - m) * jax.lax.rsqrt(v + eps) * g + b

        def _sparsify(context, h):
            c = context.shape[0]
            base = (jnp.arange(h) + 1) * STRIDE - PF + SHIFT
            idx = (base[None, :] + jnp.arange(PF)[:, None]) % c
            return context[idx.reshape(-1)].reshape(PF, h, context.shape[1], context.shape[2])
        key = jax.random.key(seed)
        ks = jax.random.split(key, 6)
        s = 0.02
        return {'x': jax.random.normal(ks[0], (SL, BS, E), jnp.float32), 'ln_g': jnp.ones((E,), jnp.float32), 'ln_b': jnp.zeros((E,), jnp.float32), 'Wq': jax.random.normal(ks[1], (E, E), jnp.float32) * s, 'bq': jnp.zeros((E,), jnp.float32), 'Wk': jax.random.normal(ks[2], (E, E), jnp.float32) * s, 'bk': jnp.zeros((E,), jnp.float32), 'Wv': jax.random.normal(ks[3], (E, E), jnp.float32) * s, 'bv': jnp.zeros((E,), jnp.float32), 'Wo': jax.random.normal(ks[4], (E, E), jnp.float32) * s, 'bo': jnp.zeros((E,), jnp.float32)}
    _L0_attn_all = _L0_attn_setup()
    _L0_attn_in = {k: v for k, v in _L0_attn_all.items() if k in ('ln_g', 'ln_b', 'Wq', 'bq', 'Wk', 'bk', 'Wv', 'bv', 'Wo', 'bo')}
    del _L0_attn_all

    def _L0_ffn_setup():
        import math
        import jax, jax.numpy as jnp
        import numpy as np
        NUM_EXPERTS = 8
        CAPACITY_FACTOR = 1.5
        key = jax.random.key(seed)
        ks = jax.random.split(key, 4)
        B, T, D, F, E = (4, 512, 256, 1024, NUM_EXPERTS)
        scale = 0.02
        return {'x': jax.random.normal(ks[0], (B, T, D), dtype=jnp.float32), 'router_w': jax.random.normal(ks[1], (E, D), dtype=jnp.float32) * scale, 'w1': jax.random.normal(ks[2], (E, D, F), dtype=jnp.float32) * scale, 'b1': jnp.zeros((E, F), dtype=jnp.float32), 'w2': jax.random.normal(ks[3], (E, F, D), dtype=jnp.float32) * scale, 'b2': jnp.zeros((E, D), dtype=jnp.float32)}
    _L0_ffn_all = _L0_ffn_setup()
    _L0_ffn_in = {k: v for k, v in _L0_ffn_all.items() if k in ('router_w', 'w1', 'b1', 'w2', 'b2')}
    del _L0_ffn_all
    return {'x': x, 'txt': txt, 'L0_tok_weight': _L0_tok_in['weight'], 'L0_tok_weighted_sum': _L0_tok_in['weighted_sum'], 'L0_attn_ln_g': _L0_attn_in['ln_g'], 'L0_attn_ln_b': _L0_attn_in['ln_b'], 'L0_attn_Wq': _L0_attn_in['Wq'], 'L0_attn_bq': _L0_attn_in['bq'], 'L0_attn_Wk': _L0_attn_in['Wk'], 'L0_attn_bk': _L0_attn_in['bk'], 'L0_attn_Wv': _L0_attn_in['Wv'], 'L0_attn_bv': _L0_attn_in['bv'], 'L0_attn_Wo': _L0_attn_in['Wo'], 'L0_attn_bo': _L0_attn_in['bo'], 'L0_ffn_router_w': _L0_ffn_in['router_w'], 'L0_ffn_w1': _L0_ffn_in['w1'], 'L0_ffn_b1': _L0_ffn_in['b1'], 'L0_ffn_w2': _L0_ffn_in['w2'], 'L0_ffn_b2': _L0_ffn_in['b2']}

def reference(x, txt, L0_tok_weight, L0_tok_weighted_sum, L0_attn_ln_g, L0_attn_ln_b, L0_attn_Wq, L0_attn_bq, L0_attn_Wk, L0_attn_bk, L0_attn_Wv, L0_attn_bv, L0_attn_Wo, L0_attn_bo, L0_ffn_router_w, L0_ffn_w1, L0_ffn_b1, L0_ffn_w2, L0_ffn_b2):
    import jax
    import jax.numpy as jnp

    def _L0_tok_ref(x, weight, weighted_sum):
        import jax, jax.numpy as jnp
        import numpy as np
        return jnp.einsum('bhid,oi,od->bho', x, weighted_sum, weight)

    def _L0_attn_ref(x, ln_g, ln_b, Wq, bq, Wk, bk, Wv, bv, Wo, bo):
        import jax, jax.numpy as jnp
        import numpy as np
        SL, BS, E, H, PF, STRIDE, SHIFT = (512, 2, 256, 16, 16, 1, 0)
        DH = E // H

        def _layernorm(x, g, b, eps=1e-05):
            m = x.mean(-1, keepdims=True)
            v = jnp.var(x, axis=-1, keepdims=True)
            return (x - m) * jax.lax.rsqrt(v + eps) * g + b

        def _sparsify(context, h):
            c = context.shape[0]
            base = (jnp.arange(h) + 1) * STRIDE - PF + SHIFT
            idx = (base[None, :] + jnp.arange(PF)[:, None]) % c
            return context[idx.reshape(-1)].reshape(PF, h, context.shape[1], context.shape[2])
        sl, bs, e = x.shape
        residual = x
        xn = _layernorm(x, ln_g, ln_b)
        fetch = _sparsify(xn, sl)
        q = (xn @ Wq + bq).reshape(sl, bs, H, DH)
        k = (fetch @ Wk + bk).reshape(PF, sl, bs, H, DH)
        v = (fetch @ Wv + bv).reshape(PF, sl, bs, H, DH)
        scale = 1.0 / jnp.sqrt(jnp.float32(DH))
        scores = jnp.einsum('sbhd,psbhd->sbhp', q, k) * scale
        attn = jax.nn.softmax(scores, axis=-1)
        out = jnp.einsum('sbhp,psbhd->sbhd', attn, v).reshape(sl, bs, e)
        out = out @ Wo + bo
        return residual + out

    def _L0_ffn_ref(x, router_w, w1, b1, w2, b2):
        import math
        import jax, jax.numpy as jnp
        import numpy as np
        NUM_EXPERTS = 8
        CAPACITY_FACTOR = 1.5
        B, T, D = x.shape
        E = router_w.shape[0]
        N = B * T
        C = max(math.ceil(CAPACITY_FACTOR * N / E), 1)
        x_flat = x.reshape(N, D)
        logits = x_flat @ router_w.T
        probs = jax.nn.softmax(logits, axis=-1)
        chosen_e = jnp.argmax(probs, axis=-1)
        chosen_p = jnp.max(probs, axis=-1)
        onehot = jax.nn.one_hot(chosen_e, E, dtype=jnp.float32)
        pos = jnp.take_along_axis(jnp.cumsum(onehot, axis=0), chosen_e[:, None], axis=1)[:, 0] - 1.0
        pos = pos.astype(jnp.int32)
        kept = pos < C
        pos_c = jnp.clip(pos, 0, C - 1)
        buf = jnp.zeros((E, C, D), dtype=x.dtype).at[chosen_e, pos_c].add(x_flat * kept[:, None].astype(x.dtype))
        h = jax.nn.gelu(jnp.einsum('ecd,edf->ecf', buf, w1) + b1[:, None, :], approximate=False)
        eo = jnp.einsum('ecf,efd->ecd', h, w2) + b2[:, None, :]
        y = eo[chosen_e, pos_c] * (chosen_p * kept.astype(x.dtype))[:, None]
        return y.reshape(B, T, D)
    h = _L0_tok_ref(x, L0_tok_weight, L0_tok_weighted_sum)
    h = jnp.concatenate([h, txt], axis=1)
    h = h + _L0_attn_ref(_layernorm(h, axis=-1), L0_attn_ln_g, L0_attn_ln_b, L0_attn_Wq, L0_attn_bq, L0_attn_Wk, L0_attn_bk, L0_attn_Wv, L0_attn_bv, L0_attn_Wo, L0_attn_bo)
    h = h + _L0_ffn_ref(_layernorm(h, axis=-1), L0_ffn_router_w, L0_ffn_w1, L0_ffn_b1, L0_ffn_w2, L0_ffn_b2)
    return h

_drawn_inputs = setup_inputs


def setup_inputs(seed=0):
    import zlib

    import numpy as np

    out = dict(_drawn_inputs(seed))
    spreads = {'L0_attn_ln_g': (1.0, 0.6),
     'L0_attn_ln_b': (0.0, 0.8),
     'L0_attn_bq': (0.0, 0.8),
     'L0_attn_bk': (0.0, 0.8),
     'L0_attn_bv': (0.0, 0.342),
     'L0_attn_bo': (0.0, 0.1),
     'L0_ffn_b1': (0.0, 0.8),
     'L0_ffn_b2': (0.0, 0.568)}
    factors = {'L0_attn_Wq': 8.0,
     'L0_attn_Wk': 8.0,
     'L0_attn_Wv': 2.736,
     'L0_ffn_router_w': 2.776,
     'L0_ffn_w1': 3.743,
     'L0_ffn_w2': 3.486}
    for name, (base, spread) in spreads.items():
        noise = np.random.default_rng([zlib.crc32(name.encode()), seed]).standard_normal(out[name].shape)
        drawn = base * np.exp(spread * noise) if base else spread * noise
        out[name] = jnp.asarray(drawn.astype(out[name].dtype))
    for name, factor in factors.items():
        out[name] = (out[name] * factor).astype(out[name].dtype)
    return out
```

```python
import concourse.bass as bass
from concourse import mybir
from contextlib import ExitStack

F32 = mybir.dt.float32
F32R = mybir.dt.float32r
BF16 = mybir.dt.bfloat16
I32 = mybir.dt.int32
ALU = mybir.AluOpType
ACT = mybir.ActivationFunctionType
AX = mybir.AxisListType.X

P = 128
B, TT, TX, D = 16, 512, 128, 256
KT = 1024
CK = KT // P
TL = P // B
NTT, NTX = TT // TL, TX // TL
NT = NTT + NTX
NI = NT // 2
NH, DH = 16, 16
KC = D // P
HC = NH // KC
EPS = 1e-5
SCALE = DH ** -0.5
NE, FF = 8, 1024
FC = FF // P
NTOK = B * (TT + TX)
CAP = -(-3 * NTOK // (2 * NE))
BT = 3
BLK = BT * P
NBE = CAP // BLK
NB = NE * NBE
ROW = D + 4
NOWHERE = float(1 << 20)
RT = 4
NR = NT // RT


def after(eng, sem, i, n=1, k=None):
    v = i * n + (n if k is None else k)
    if isinstance(v, int) and v <= 0:
        return
    eng.wait_ge(sem, v)


def fusion_kernel(nc, x, txt, tok_w, tok_ws, ln_g, ln_b, wq, bq, wk, bk, wv, bv, wo, bo,
                  router_w, w1, b1, w2, b2, out):
    ctx = ExitStack()

    def sbt(c, name, shape, dt=F32):
        return c.enter_context(nc.sbuf_tensor(name, shape, dt))

    def pst(c, name, shape):
        return c.enter_context(nc.psum_tensor(name, shape, F32))

    def sem(name):
        return ctx.enter_context(nc.semaphore(name))

    def one_newton_step(link, e, v, y, t):
        link(e.tensor_tensor(t, y, y, ALU.mult))
        link(e.tensor_tensor(t, t, v, ALU.mult))
        link(e.tensor_scalar(t, t, -0.5, 1.5, ALU.mult, ALU.add))
        link(e.tensor_tensor(y, y, t, ALU.mult))

    def whole_stats(link, e, st, halves, t):
        link(e.tensor_tensor(st[:, 0, :], halves[:, :, 1], halves[:, :, 4], ALU.add))
        link(e.tensor_tensor(t, halves[:, :, 1], halves[:, :, 4], ALU.subtract))
        link(e.tensor_tensor(t, t, t, ALU.mult))
        link(e.tensor_tensor(st[:, 1, :], halves[:, :, 2], halves[:, :, 5], ALU.add))
        link(e.tensor_scalar(st[:, 0, :], st[:, 0, :], 0.5, None, ALU.mult))
        link(e.tensor_scalar(st[:, 1, :], st[:, 1, :], 1.0 / D, None, ALU.mult))
        link(e.scalar_tensor_tensor(out=st[:, 1, :], in0=t, scalar=0.25, in1=st[:, 1, :], op0=ALU.mult, op1=ALU.add))

    with ctx:
        slots = nc.dram_tensor("slots", [NE * CAP, ROW], F32, kind="Internal").ap()
        out_rows = out.rearrange("b t f -> (b t) f")
        ident = sbt(ctx, "ident", [P, P])
        wr_t = sbt(ctx, "wr_t", [P, KC, NE])
        b1_t = sbt(ctx, "b1_t", [P, NE * FC])
        ident_ready = sem("ident_ready")
        slots_filled = sem("slots_filled")
        default_out = sem("default_out")

        gated = sbt(ctx, "gated", [P, 2, BT])

        hctx = ctx.enter_context(ExitStack())
        H = sbt(hctx, "H", [P, NT, D])
        halves = sbt(hctx, "halves", [P, NT, 6])
        st = sbt(hctx, "st", [P, 2, NT])
        lnw = sbt(hctx, "lnw", [P, 5, NT])

        def gate(e, passed, par, t=0):
            e.tensor_tensor(gated[:, par, t:t + 1], ident[:, 0:1], ident[:, 0:1], ALU.add).then_inc(passed, 1)

        fill = sbt(hctx, "fill", [P, ROW])

        def tok_phase(c, attn_w, bq_c, bk_c, bo_b):
            XS = sbt(c, "XS", [P, 2, 2, KT])
            XH = sbt(c, "XH", [P, 2, KT], F32R)
            XL = sbt(c, "XL", [P, 2, KT], F32R)
            WH = sbt(c, "WH", [P, CK, D], F32R)
            WL = sbt(c, "WL", [P, CK, D], F32R)
            w_outer = sbt(c, "w_outer", [P, KC, D, 4])
            ws_in = sbt(c, "ws_in", [P, KC, D])
            w_in = sbt(c, "w_in", [P, KC, 4])
            aw_in = sbt(c, "aw_in", [P, 4, KC, D])
            g_c = sbt(c, "g_c", [P, KC])
            b_c = sbt(c, "b_c", [P, KC])
            bias_in = sbt(c, "bias_in", [P, 3, KC])
            bv_b = sbt(c, "bv_b", [P, KC, P])
            bo_in = sbt(c, "bo_in", [P, D])
            wr_in = sbt(c, "wr_in", [NE, D])
            b1_in = sbt(c, "b1_in", [NE * FC, P])
            XT = pst(c, "XT", [P, 2, 2, 512])
            HP = pst(c, "HP", [P, 2, 512])
            WB = pst(c, "WB", [P, 2, 512])
            tok_weights_in, small_in, txt_in = sem("tok_weights_in"), sem("small_in"), sem("txt_in")
            x_in = [sem("x_in0"), sem("x_in1")]
            outer_made, w_transposed, w_hi, w_lo = sem("outer_made"), sem("w_transposed"), sem("w_hi"), sem("w_lo")
            fill_made, x_transposed, x_hi, x_lo = sem("fill_made"), sem("x_transposed"), sem("x_hi"), sem("x_lo")
            h_made, h_copied, h_stats = sem("h_made"), sem("h_copied"), sem("h_stats")
            tok_chain, bias_made, bv_spread, bo_made = sem("tok_chain"), sem("bias_made"), sem("bv_spread"), sem("bo_made")
            router_transposed, b1_transposed, small_copied = sem("router_transposed"), sem("b1_transposed"), sem("small_copied")
            NSMALL = 4 + 5 + 3
            xr = x.rearrange("b h i d -> (b h) (i d)").rearrange("(p t) k -> p t k", t=NTT)
            txr = txt.rearrange("b t f -> (b t) f").rearrange("(p t) f -> p t f", t=NTX)
            outer2 = w_outer[:, :, :, :].rearrange("p c i d -> p c (i d)")

            with nc.Block() as block:
                @block.sync
                def _(e):
                    e.dma_start(ws_in[:, :, :], tok_ws.rearrange("(c p) i -> p c i", p=P)).then_inc(tok_weights_in, 16)
                    e.dma_start(w_in[:, :, :], tok_w.rearrange("(c p) d -> p c d", p=P)).then_inc(tok_weights_in, 16)
                    for u in range(2):
                        e.dma_start(XS[:, u, :, :], xr[:, 2 * u:2 * u + 2, :]).then_inc(x_in[u], 16)
                    with e.Fori(1, NTT // 4) as n:
                        for u in range(2):
                            e.wait_ge(x_transposed, n * 8 + (4 * u - 4))
                            e.dma_start(XS[:, u, :, :], xr[:, bass.ds(n * 4 + 2 * u, 2), :]).then_inc(x_in[u], 16)

                @block.gpsimd
                def _(e):
                    e.memset(fill[:, :], 0.0).then_inc(fill_made, 1)
                    e.memset(ident[:, :], 0.0).then_inc(fill_made, 1)
                    e.wait_ge(fill_made, 2)
                    e.memset(fill[:, D + 3:ROW], NOWHERE).then_inc(fill_made, 1)
                    e.affine_select(out=ident[:, :], in_=ident[:, :], compare_op=ALU.not_equal, fill=1.0, base=0,
                                    pattern=[[-1, P]], channel_multiplier=1).then_inc(ident_ready, 1)

                @block.scalar
                def _(e):
                    for i, w in enumerate((wq, wk, wv, wo)):
                        e.dma_start(aw_in[:, i, :, :], w.rearrange("(c p) n -> p c n", p=P)).then_inc(small_in, 16)
                    for dst, src in ((g_c[:, :], ln_g), (b_c[:, :], ln_b), (bias_in[:, 0, :], bq),
                                     (bias_in[:, 1, :], bk), (bias_in[:, 2, :], bv)):
                        e.dma_start(dst, src.rearrange("(c p) -> p c", p=P),
                                    allow_slow_non_contiguous=True).then_inc(small_in, 16)
                    e.dma_start(bo_in[:, :], bo.unsqueeze(0).broadcast_to([P, D])).then_inc(small_in, 16)
                    e.dma_start(wr_in[:, :], router_w).then_inc(small_in, 16)
                    e.dma_start(b1_in[:, :], b1.rearrange("e (f p) -> (e f) p", p=P)).then_inc(small_in, 16)
                    e.dma_start(H[:, NTT:, :], txr).then_inc(txt_in, 16)
                    e.wait_ge(fill_made, 3)
                    e.dma_start(slots.rearrange("(p t) r -> p t r", p=P),
                                fill[:, :].unsqueeze(1).broadcast_to([P, NE * CAP // P, ROW])).then_inc(slots_filled, 16)
                    for k in range(CK):
                        e.wait_ge(w_transposed, k + 1)
                        e.activation(WH[:, k, :], WB[:, k % 2, 0:D], ACT.Copy).then_inc(w_hi, 1)

                    def hi(T, par):
                        for h in range(2):
                            after(e, x_transposed, T, 2, h + 1)
                            after(e, h_made, T - 2)
                            e.activation(XH[:, par, h * 512:(h + 1) * 512], XT[:, par, h, :], ACT.Copy).then_inc(x_hi, 1)

                    def copy_h(T, par):
                        after(e, h_made, T)
                        e.activation(H[:, T, :], HP[:, par, 0:D], ACT.Copy).then_inc(h_copied, 1)

                    hi(0, 0)
                    with e.Fori(0, NTT // 2 - 1) as n:
                        for u in range(2):
                            hi(n * 2 + (u + 1), (u + 1) % 2)
                            copy_h(n * 2 + u, u)
                    hi(NTT - 1, 1)
                    copy_h(NTT - 2, 0)
                    copy_h(NTT - 1, 1)

                @block.vector
                def _(e):
                    chained = [0]

                    def link(ins):
                        chained[0] += 1
                        ins.then_inc(tok_chain, 1)
                        e.wait_ge(tok_chain, chained[0])

                    e.wait_ge(tok_weights_in, 32)
                    for c_ in range(KC):
                        e.tensor_tensor(w_outer[:, c_, :, :], ws_in[:, c_, :].unsqueeze(2).broadcast_to([P, D, 4]),
                                        w_in[:, c_, :].unsqueeze(1).broadcast_to([P, D, 4]), ALU.mult).then_inc(outer_made, 1)
                    for k in range(CK):
                        e.wait_ge(w_hi, k + 1)
                        e.tensor_tensor(WL[:, k, :], WB[:, k % 2, 0:D], WH[:, k, :].bitcast(F32),
                                        ALU.subtract).then_inc(w_lo, 1)
                    e.wait_ge(small_in, 16 * NSMALL)
                    e.wait_ge(bias_made, 1)
                    e.tensor_tensor(bq_c[:, :], WB[:, 0, 0:KC], bias_in[:, 0, :], ALU.add).then_inc(small_copied, 1)
                    e.tensor_tensor(bk_c[:, :], WB[:, 0, KC:2 * KC], bias_in[:, 1, :], ALU.add).then_inc(small_copied, 1)
                    link(e.tensor_tensor(bias_in[:, 2, :], WB[:, 0, 2 * KC:3 * KC], bias_in[:, 2, :], ALU.add))
                    e.tensor_copy(bv_b[:, :, :], bias_in[:, 2, :].unsqueeze(2).broadcast_to([P, KC, P])).then_inc(bv_spread, 1)
                    for i in range(4):
                        hi_, lo_ = attn_w[i]
                        if i < 3:
                            for k in range(KC):
                                link(e.tensor_scalar(aw_in[:, i, k, :], aw_in[:, i, k, :], g_c[:, k:k + 1], None, ALU.mult))
                        link(e.tensor_copy(hi_[:, :, :], aw_in[:, i, :, :]))
                        link(e.tensor_tensor(lo_[:, :, :], aw_in[:, i, :, :], hi_[:, :, :].bitcast(F32), ALU.subtract))
                    e.wait_ge(bo_made, 1)
                    e.tensor_tensor(bo_b[:, :], WB[:, 1, 0:D], bo_in[:, :], ALU.add).then_inc(small_copied, 1)
                    e.wait_ge(router_transposed, 1)
                    e.tensor_copy(wr_t[:, :, :], WB[:, 0, 0:KC * NE].rearrange("p (c e) -> p c e", c=KC)).then_inc(small_copied, 1)
                    e.wait_ge(b1_transposed, 1)
                    e.tensor_copy(b1_t[:, :], WB[:, 1, 0:NE * FC]).then_inc(small_copied, 1)

                    def lo(T, par):
                        for h in range(2):
                            after(e, x_hi, T, 2, h + 1)
                            e.tensor_tensor(XL[:, par, h * 512:(h + 1) * 512], XT[:, par, h, :],
                                            XH[:, par, h * 512:(h + 1) * 512].bitcast(F32), ALU.subtract).then_inc(x_lo, 1)

                    def stats(T):
                        e.bn_stats(halves[:, T, :], H[:, T, :]).then_inc(h_stats, 1)

                    lo(0, 0)
                    lo(1, 1)
                    e.wait_ge(txt_in, 16)
                    with e.Fori(NTT, NT) as n:
                        stats(n)
                    with e.Fori(0, NTT // 2 - 1) as n:
                        for u in range(2):
                            after(e, h_copied, n * 2 + u)
                            lo(n * 2 + (u + 2), u)
                            stats(n * 2 + u)
                    for T in (NTT - 2, NTT - 1):
                        after(e, h_copied, T)
                        stats(T)
                    e.wait_ge(h_stats, NT)

                @block.tensor
                def _(e):
                    e.wait_ge(ident_ready, 1)
                    e.wait_ge(outer_made, 2)
                    for k in range(CK):
                        if k >= 2:
                            e.wait_ge(w_lo, k - 1)
                        for c_ in range(KC):
                            m = e.transpose(WB[:, k % 2, c_ * P:(c_ + 1) * P], outer2[:, c_, k * P:(k + 1) * P], ident[:, :])
                        m.then_inc(w_transposed, 1)
                    e.wait_ge(small_in, 16 * NSMALL)
                    e.wait_ge(w_lo, CK)
                    for i in range(3):
                        for c_ in range(KC):
                            for k in range(KC):
                                m = e.matmul(WB[:, 0, i * KC + c_:i * KC + c_ + 1], aw_in[:, i, k, c_ * P:(c_ + 1) * P],
                                             b_c[:, k:k + 1], start=(k == 0), stop=(k == KC - 1))
                    m.then_inc(bias_made, 1)
                    e.wait_ge(bv_spread, 1)
                    for k in range(KC):
                        m = e.matmul(WB[:, 1, 0:D], bv_b[:, k, :], aw_in[:, 3, k, :], start=(k == 0), stop=(k == KC - 1))
                    m.then_inc(bo_made, 1)
                    for c_ in range(KC):
                        m = e.transpose(WB[:, 0, c_ * NE:(c_ + 1) * NE], wr_in[:, c_ * P:(c_ + 1) * P], ident[0:NE, 0:NE])
                    m.then_inc(router_transposed, 1)
                    e.wait_ge(small_copied, 3)
                    e.transpose(WB[:, 1, 0:NE * FC], b1_in[:, :], ident[0:NE * FC, 0:NE * FC]).then_inc(b1_transposed, 1)

                    def transposes(T, u):
                        for h in range(2):
                            after(e, x_lo, T - 2, 2, h + 1)
                            for k in range(4):
                                kk = h * 4 + k
                                m = e.transpose(XT[:, u % 2, h, k * P:(k + 1) * P],
                                                XS[:, u // 2, u % 2, kk * P:(kk + 1) * P], ident[:, :])
                            m.then_inc(x_transposed, 1)

                    def products(T, par):
                        after(e, x_lo, T, 2)
                        after(e, h_copied, T - 2)
                        n_ = 0
                        for k in range(CK):
                            for a, w in ((XH, WH), (XH, WL), (XL, WH)):
                                m = e.matmul(HP[:, par, 0:D], a[:, par, k * P:(k + 1) * P], w[:, k, :],
                                             start=(n_ == 0), stop=(n_ == 3 * CK - 1))
                                n_ += 1
                        m.then_inc(h_made, 1)

                    def four(n):
                        for u in range(4):
                            if u == 1:
                                e.wait_ge(x_in[1], n * 16 + 16)
                            if u == 3:
                                e.wait_ge(x_in[0], n * 16 + 32)
                            transposes(n * 4 + (u + 1), (u + 1) % 4)
                            products(n * 4 + u, u % 2)

                    e.wait_ge(x_in[0], 16)
                    transposes(0, 0)
                    four(0)
                    with e.Fori(1, NTT // 4 - 1) as n:
                        four(n)
                    for u in range(3):
                        if u == 1:
                            e.wait_ge(x_in[1], 16 * (NTT // 4))
                        transposes(NTT - 4 + u + 1, u + 1)
                        products(NTT - 4 + u, u % 2)
                    products(NTT - 1, 1)

        def attention_phase(c, attn_w, bq_c, bk_c, bo_b):
            (WQH, WQL), (WKH, WKL), (WVH, WVL), (WOH, WOL) = attn_w
            r, rs, one_r, neg_mr, neg_mrs = (lnw[:, i, :] for i in range(5))
            tmp = sbt(c, "ln_tmp", [P, 2, NT])
            XN = sbt(c, "XN", [P, 2, D])
            XNH = sbt(c, "XNH", [P, KC, D], F32R)
            XNL = sbt(c, "XNL", [P, KC, D], F32R)
            QS = sbt(c, "QS", [P, 3, KC, B * 2 * TL], BF16)
            KS = sbt(c, "KS", [P, KC * 2 * TL, 3, B], BF16)
            VS = sbt(c, "VS", [P, 2, 2 * NH, 3, DH], BF16)
            PS = sbt(c, "PS", [P, 3, B * 2 * NH], BF16)
            RQ = sbt(c, "RQ", [P, 2 * D])
            RK = sbt(c, "RK", [P, 2 * D])
            RV = sbt(c, "RV", [P, 2 * D])
            RP = sbt(c, "RP", [P, 2 * D])
            QBD = sbt(c, "QBD", [P, 3, KC, HC, B * 2 * TL], BF16)
            PX = sbt(c, "PX", [P, 3, TL, B * 2 * NH], BF16)
            SB = sbt(c, "SB", [P, 2 * KC * TL, B])
            SD = sbt(c, "SD", [P, 2 * KC * TL, B])
            EX = sbt(c, "EX", [P, 2 * KC * TL, B])
            PN = sbt(c, "PN", [P, 2 * KC * TL, B])
            MX = sbt(c, "MX", [P, 2 * KC * TL])
            SM = sbt(c, "SM", [P, 2 * KC * TL])
            RC = sbt(c, "RC", [P, 2 * KC * TL])
            OB = sbt(c, "OB", [P, 2 * NH, DH])
            OTH = sbt(c, "OTH", [P, KC * 2, B, TL], F32R)
            OTL = sbt(c, "OTL", [P, KC * 2, B, TL], F32R)
            T1 = sbt(c, "T1", [P, 2, D])
            T2 = sbt(c, "T2", [P, 2, D])
            bank = [pst(c, f"bank{i}", [P, 512]) for i in range(8)]
            XTV, S0, S1, QOT, KB, O0, O1, WB = bank
            SBK, OBK = (S0, S1), (O0, O1)
            S = {n: sem(n) for n in (
                "ln_sqrt", "ln_chain", "zeroed", "xn_made", "xn_transposed", "xn_hi", "xn_lo",
                "q_made", "k_made", "v_made", "q1", "q2", "q3", "q_rest", "k1", "k2", "k3", "k_rest",
                "v1", "v2", "v3", "v_rest", "s_made", "s_summed", "max_made", "shifted", "exp_made", "sum_made",
                "recip_made", "p_made", "p_transposed", "p1", "p2", "p3", "p_rest", "o_made", "o_summed",
                "o_transposed", "o_hi", "o_lo", "wo_made", "res_scaled", "res_bias", "h_updated", "attn_stats",
                "q_spread", "p_spread")}

            def perm(ap):
                return ap.rearrange("p (g t b) -> p g b t", g=2 * KC, t=TL)

            def swapped(ap, n):
                return ap.rearrange("p (b t) -> p t b", b=n)

            def as_made(ap):
                return ap[:, :].rearrange("p (g b t) -> p g b t", g=2 * KC, t=TL)

            def steps(e, body):
                body(-1, 1, True, False, False)
                body(0, 0, True, True, False)
                body(1, 1, True, True, True)
                with e.Fori(1, NI // 2 - 1) as n:
                    for u in range(2):
                        body(n * 2 + u, u, True, True, True)
                body(NI - 2, (NI - 2) % 2, True, True, True, last=True)
                body(NI - 1, (NI - 1) % 2, False, True, True)
                body(NI, NI % 2, False, False, True)

            with nc.Block() as block:
                @block.sync
                def _(e):
                    e.wait_ge(S["zeroed"], 2)

                    def body(i, u, nxt, cur, prv, last=False):
                        if nxt:
                            after(e, S["q3"], i + 1)
                            after(e, S["s_made"], i, 4)
                            for h in range(HC):
                                rows = slice(h * DH, (h + 1) * DH)
                                e.dma_start(QBD[rows, :, :, h, :], QS[rows, :, :, :]).then_inc(S["q_spread"], 16)
                        if cur:
                            after(e, S["p3"], i)
                            after(e, S["o_made"], i - 1, 4)
                            for t in range(TL):
                                rows = slice(t * B, (t + 1) * B)
                                e.dma_start(PX[rows, :, t, :], PS[rows, :, :]).then_inc(S["p_spread"], 16)
                    steps(e, body)

                @block.gpsimd
                def _(e):
                    e.memset(PX[:, :, :, :].rearrange("p a t c -> p (a t c)").bitcast(F32), 0.0).then_inc(S["zeroed"], 1)

                    def third(name, dst, rest, i, src2):
                        after(e, S[name + "_rest"], i, 2 if name in "qk" else 1)
                        after(e, S[name + "2"], i)
                        e.tensor_tensor(dst, rest, src2, ALU.subtract).then_inc(S[name + "3"], 1)

                    def body(i, u, nxt, cur, prv, last=False):
                        if cur:
                            after(e, S["max_made"], i)
                            after(e, S["exp_made"], i - 1)
                            e.tensor_tensor(SD[:, :, :], SB[:, :, :],
                                            MX[:, :].unsqueeze(2).broadcast_to([P, 2 * KC * TL, B]),
                                            ALU.subtract).then_inc(S["shifted"], 1)
                        if nxt:
                            third("q", QS[:, 2, :, :].rearrange("p c n -> p (c n)"), RQ[:, :], i + 1,
                                  QS[:, 1, :, :].rearrange("p c n -> p (c n)"))
                        if cur:
                            after(e, S["recip_made"], i)
                            after(e, S["p_transposed"], i - 1)
                            e.tensor_tensor(PN[:, :, :], EX[:, :, :],
                                            RC[:, :].unsqueeze(2).broadcast_to([P, 2 * KC * TL, B]),
                                            ALU.mult).then_inc(S["p_made"], 1)
                        if nxt:
                            third("k", KS[:, :, 2, :], RK[:, :].rearrange("p (g b) -> p g b", b=B), i + 1, KS[:, :, 1, :])
                            v = (u + 1) % 2
                            third("v", VS[:, v, :, 2, :], RV[:, :].rearrange("p (g d) -> p g d", d=DH), i + 1,
                                  VS[:, v, :, 1, :])
                        if prv:
                            after(e, S["res_scaled"], i - 1)
                            after(e, S["h_updated"], i - 2)
                            e.tensor_tensor(T2[:, :, :], T1[:, :, :], bo_b[:, :].unsqueeze(1).broadcast_to([P, 2, D]),
                                            ALU.add).then_inc(S["res_bias"], 1)
                        if cur:
                            third("p", PS[:, 2, :], RP[:, :], i, PS[:, 1, :])
                    steps(e, body)

                @block.scalar
                def _(e):
                    e.wait_ge(S["ln_chain"], 8)
                    e.activation(r, tmp[:, 0, :], ACT.Sqrt).then_inc(S["ln_sqrt"], 1)
                    e.wait_ge(S["ln_chain"], 16)
                    e.activation(rs, tmp[:, 0, :], ACT.Sqrt).then_inc(S["ln_sqrt"], 1)

                    def body(i, u, nxt, cur, prv, last=False):
                        if nxt:
                            after(e, S["xn_transposed"], i + 1)
                            after(e, S["v_made"], i)
                            e.activation(perm(XNH[:, :, :].rearrange("p c n -> p (c n)")), as_made(XTV), ACT.Copy).then_inc(S["xn_hi"], 1)
                        if cur:
                            after(e, S["shifted"], i)
                            after(e, S["p_made"], i - 1)
                            after(e, S["sum_made"], i - 1)
                            e.activation(EX[:, :, :], SD[:, :, :], ACT.Exp, scale=SCALE).then_inc(S["exp_made"], 1)
                        if nxt:
                            after(e, S["q_spread"], i, 16 * HC)
                            after(e, S["q_made"], i + 1)
                            for c_ in range(KC):
                                e.activation(swapped(QS[:, 0, c_, :], B),
                                             QOT[:, c_ * D:(c_ + 1) * D].rearrange("p (t b) -> p t b", b=B),
                                             ACT.Identity, bias=bq_c[:, c_:c_ + 1]).then_inc(S["q1"], 1)
                            after(e, S["s_made"], i, 4)
                            after(e, S["k_made"], i + 1)
                            for c_ in range(KC):
                                e.activation(KS[:, c_ * 2 * TL:(c_ + 1) * 2 * TL, 0, :],
                                             KB[:, c_ * D:(c_ + 1) * D].rearrange("p (g b) -> p g b", b=B),
                                             ACT.Identity, bias=bk_c[:, c_:c_ + 1]).then_inc(S["k1"], 1)
                            after(e, S["q_rest"], i + 1, 2)
                            e.activation(QS[:, 1, :, :].rearrange("p c n -> p (c n)"), RQ[:, :], ACT.Copy).then_inc(S["q2"], 1)
                            v = (u + 1) % 2
                            after(e, S["v_made"], i + 1)
                            after(e, S["o_made"], i - 1, 4)
                            e.activation(VS[:, v, :, 0, :], XTV[:, :].rearrange("p (g d) -> p g d", d=DH),
                                         ACT.Copy).then_inc(S["v1"], 1)
                            after(e, S["k_rest"], i + 1, 2)
                            e.activation(KS[:, :, 1, :], RK[:, :].rearrange("p (g b) -> p g b", b=B), ACT.Copy).then_inc(S["k2"], 1)
                            after(e, S["v_rest"], i + 1)
                            e.activation(VS[:, v, :, 1, :], RV[:, :].rearrange("p (g d) -> p g d", d=DH),
                                         ACT.Copy).then_inc(S["v2"], 1)
                        if cur:
                            after(e, S["p_transposed"], i)
                            after(e, S["p_spread"], i - 1, 16 * TL)
                            e.activation(swapped(PS[:, 0, :], B), S0[:, :].rearrange("p (h b) -> p h b", b=B), ACT.Copy).then_inc(S["p1"], 1)
                            after(e, S["p_rest"], i)
                            e.activation(PS[:, 1, :], RP[:, :], ACT.Copy).then_inc(S["p2"], 1)
                        if prv:
                            after(e, S["o_transposed"], i - 1)
                            after(e, S["wo_made"], i - 2)
                            e.activation(OTH[:, :, :, :].rearrange("p g b t -> p g t b"),
                                         QOT[:, :].rearrange("p (g t b) -> p g t b", g=4, t=TL), ACT.Copy).then_inc(S["o_hi"], 1)
                    steps(e, body)

                @block.vector
                def _(e):
                    chained = [0]

                    def link(ins):
                        chained[0] += 1
                        ins.then_inc(S["ln_chain"], 1)
                        e.wait_ge(S["ln_chain"], chained[0])

                    v, t = tmp[:, 0, :], tmp[:, 1, :]
                    mean, var = st[:, 0, :], st[:, 1, :]
                    whole_stats(link, e, st, halves, t)
                    link(e.tensor_scalar(v, var, EPS, None, ALU.add))
                    e.wait_ge(S["ln_sqrt"], 1)
                    link(e.reciprocal(r, r))
                    one_newton_step(link, e, v, r, t)
                    link(e.tensor_tensor(t, r, r, ALU.mult))
                    link(e.tensor_tensor(v, t, var, ALU.mult))
                    link(e.tensor_scalar(v, v, EPS, None, ALU.add))
                    assert chained[0] == 16
                    e.wait_ge(S["ln_sqrt"], 2)
                    link(e.reciprocal(rs, rs))
                    one_newton_step(link, e, v, rs, t)
                    link(e.tensor_tensor(rs, rs, r, ALU.mult))
                    link(e.tensor_scalar(one_r, r, 1.0, None, ALU.add))
                    link(e.tensor_scalar(t, mean, -1.0, None, ALU.mult))
                    link(e.tensor_tensor(neg_mr, t, r, ALU.mult))
                    link(e.tensor_tensor(neg_mrs, t, rs, ALU.mult))
                    e.memset(QBD[:, :, :, :, :].rearrange("p a c h n -> p (a c h n)").bitcast(F32), 0.0).then_inc(S["zeroed"], 1)

                    def xn(i):
                        after(e, S["xn_transposed"], i - 1)
                        for j in range(2):
                            T = i * 2 + j
                            e.tensor_scalar(XN[:, j, :], H[:, T, :], rs_col(T), mrs_col(T), ALU.mult, ALU.add
                                            ).then_inc(S["xn_made"], 1)

                    def col(k, T):
                        return lnw[:, k, bass.ds(T, 1)]

                    def rs_col(T):
                        return col(1, T)

                    def mrs_col(T):
                        return col(4, T)

                    def sums_of_three(name, made, banks, dst, i):
                        for s in range(4):
                            after(e, S[made], i, 4, s + 1)
                            e.tensor_reduce(dst[s], banks[s % 2][:, 0:TL * 3 * B].rearrange("p (g a b) -> p g b a", a=3, b=B),
                                            AX, ALU.add).then_inc(S[name], 1)

                    def body(i, u, nxt, cur, prv, last=False):
                        if nxt:
                            after(e, S["xn_hi"], i + 1)
                            e.tensor_tensor(perm(XNL[:, :, :].rearrange("p c n -> p (c n)")), as_made(XTV),
                                            perm(XNH[:, :, :].rearrange("p c n -> p (c n)").bitcast(F32)),
                                            ALU.subtract).then_inc(S["xn_lo"], 1)
                        if cur:
                            after(e, S["shifted"], i - 1)
                            sums_of_three("s_summed", "s_made", SBK,
                                          [SB[:, (s % 2) * 2 * TL + (s // 2) * TL:(s % 2) * 2 * TL + (s // 2) * TL + TL, :]
                                           for s in range(4)], i)
                            after(e, S["s_summed"], i, 4)
                            e.tensor_reduce(MX[:, :], SB[:, :, :], AX, ALU.max).then_inc(S["max_made"], 1)
                        if prv:
                            after(e, S["o_transposed"], i - 2)
                            sums_of_three("o_summed", "o_made", OBK,
                                          [OB[:, s * HC:(s + 1) * HC, :] for s in range(4)], i - 1)
                        if nxt:
                            after(e, S["q3"], i)
                            after(e, S["q2"], i)
                            for c_ in range(KC):
                                after(e, S["q1"], i + 1, 2)
                                e.scalar_tensor_tensor(out=swapped(RQ[:, c_ * D:(c_ + 1) * D], B),
                                                       in0=QOT[:, c_ * D:(c_ + 1) * D].rearrange("p (t b) -> p t b", b=B),
                                                       scalar=bq_c[:, c_:c_ + 1], in1=swapped(QS[:, 0, c_, :], B),
                                                       op0=ALU.add, op1=ALU.subtract).then_inc(S["q_rest"], 1)
                        if cur:
                            after(e, S["exp_made"], i)
                            e.tensor_reduce(SM[:, :], EX[:, :, :], AX, ALU.add).then_inc(S["sum_made"], 1)
                            after(e, S["sum_made"], i)
                            after(e, S["p_made"], i - 1)
                            e.reciprocal(RC[:, :], SM[:, :]).then_inc(S["recip_made"], 1)
                        if nxt:
                            after(e, S["k3"], i)
                            after(e, S["k2"], i)
                            for c_ in range(KC):
                                after(e, S["k1"], i + 1, 2)
                                e.scalar_tensor_tensor(out=RK[:, c_ * D:(c_ + 1) * D].rearrange("p (g b) -> p g b", b=B),
                                                       in0=KB[:, c_ * D:(c_ + 1) * D].rearrange("p (g b) -> p g b", b=B),
                                                       scalar=bk_c[:, c_:c_ + 1],
                                                       in1=KS[:, c_ * 2 * TL:(c_ + 1) * 2 * TL, 0, :],
                                                       op0=ALU.add, op1=ALU.subtract).then_inc(S["k_rest"], 1)
                            after(e, S["v3"], i)
                            after(e, S["v2"], i)
                            after(e, S["v1"], i + 1)
                            e.tensor_tensor(RV[:, :].rearrange("p (g d) -> p g d", d=DH), XTV[:, :].rearrange("p (g d) -> p g d", d=DH),
                                            VS[:, (u + 1) % 2, :, 0, :], ALU.subtract).then_inc(S["v_rest"], 1)
                        if prv:
                            after(e, S["res_bias"], i - 2)
                            for j in range(2):
                                T = i * 2 + (j - 2)
                                m = e.tensor_scalar(T1[:, j, :], H[:, T, :], col(2, T), col(3, T), ALU.mult, ALU.add)
                            m.then_inc(S["res_scaled"], 1)
                        if cur:
                            after(e, S["p3"], i - 1)
                            after(e, S["p2"], i - 1)
                            after(e, S["p1"], i)
                            e.tensor_tensor(swapped(RP[:, :], B), S0[:, :].rearrange("p (h b) -> p h b", b=B),
                                            swapped(PS[:, 0, :], B), ALU.subtract).then_inc(S["p_rest"], 1)
                        if prv:
                            if not (isinstance(i, int) and i == 1):
                                after(e, S["h_updated"], i - 2)
                            after(e, S["o_hi"], i - 1)
                            e.tensor_tensor(OTL[:, :, :, :].rearrange("p g b t -> p g t b"),
                                            QOT[:, :].rearrange("p (g t b) -> p g t b", g=4, t=TL),
                                            OTH[:, :, :, :].rearrange("p g b t -> p g t b").bitcast(F32),
                                            ALU.subtract).then_inc(S["o_lo"], 1)
                            if not (isinstance(i, int) and i == 1):
                                stats(i - 2)
                        if nxt and not last:
                            xn(i + 2)
                        if prv:
                            after(e, S["res_bias"], i - 1)
                            after(e, S["wo_made"], i - 1)
                            e.tensor_tensor(H[:, bass.ds(i * 2 - 2, 2), :], WB[:, :].rearrange("p (j n) -> p j n", j=2),
                                            T2[:, :, :], ALU.add).then_inc(S["h_updated"], 1)

                    def stats(i):
                        for j in range(2):
                            e.bn_stats(halves[:, i * 2 + j, :], H[:, i * 2 + j, :]).then_inc(S["attn_stats"], 1)

                    xn(0)
                    steps(e, body)
                    e.wait_ge(S["h_updated"], NI)
                    stats(NI - 1)
                    e.wait_ge(S["attn_stats"], NT)

                @block.tensor
                def _(e):
                    def project(dst, wh, wl, wait=None):
                        for c_ in range(KC):
                            n_ = 0
                            for k in range(KC):
                                for w, a in ((wh, XNH), (wl, XNH), (wh, XNL)):
                                    m = e.matmul(dst[:, c_ * D:(c_ + 1) * D], w[:, k, c_ * P:(c_ + 1) * P], a[:, k, :],
                                                 start=(n_ == 0), stop=(n_ == 3 * KC - 1))
                                    n_ += 1
                        return m

                    def tokens_by_features(dst, ah, al, wh, wl):
                        for j in range(2):
                            n_ = 0
                            for k in range(KC):
                                for a, w in ((ah, wh), (ah, wl), (al, wh)):
                                    m = e.matmul(dst[:, j * D:(j + 1) * D], a(k, j), w[:, k, :],
                                                 start=(n_ == 0), stop=(n_ == 3 * KC - 1))
                                    n_ += 1
                        return m

                    def small_products(dst, stationary, moving):
                        for t in range(8):
                            for a in range(3):
                                m = e.matmul(dst[:, t * 48:t * 48 + 16 * (3 - a)], stationary(a, t), moving(t, 3 - a),
                                             start=(t == 0 and a == 0), stop=(t == 7 and a == 2), skip_group_check=True)
                        return m

                    def body(i, u, nxt, cur, prv, last=False):
                        if nxt:
                            after(e, S["xn_made"], i + 1, 2)
                            after(e, S["v_rest"], i)
                            for c_ in range(KC):
                                for j in range(2):
                                    m = e.transpose(XTV[:, c_ * D + j * P:c_ * D + (j + 1) * P], XN[:, j, c_ * P:(c_ + 1) * P],
                                                    ident[:, :])
                            m.then_inc(S["xn_transposed"], 1)
                        if cur:
                            after(e, S["q_spread"], i, 16 * HC)
                            after(e, S["k3"], i)
                            for s in range(4):
                                j, c_ = s // 2, s % 2
                                if s == 0:
                                    after(e, S["p_rest"], i - 1)
                                after(e, S["s_summed"], i, 4, s - 1)
                                small_products(SBK[s % 2],
                                               lambda a, t: QBD[:, a, c_, :, :].rearrange("p h (b t) -> p (h b) t", b=B)[:, :, j * TL + t],
                                               lambda t, n: KS[:, c_ * 2 * TL + j * TL + t, 0:n, :]).then_inc(S["s_made"], 1)
                        if prv:
                            after(e, S["p_spread"], i - 1, 16 * TL)
                            after(e, S["v3"], i - 1)
                            for s in range(4):
                                after(e, S["o_summed"], i - 1, 4, s - 1)
                                j = s // 2
                                small_products(OBK[s % 2],
                                               lambda a, t: PX[:, a, :, :].rearrange("p l (b h) -> p (l b) h", b=B)[:, :, s * HC + t],
                                               lambda t, n: VS[:, (u + 1) % 2, s * HC + t, 0:n, :]).then_inc(S["o_made"], 1)
                        if nxt:
                            after(e, S["xn_lo"], i + 1)
                            after(e, S["o_lo"], i - 2)
                            project(QOT, WQH, WQL).then_inc(S["q_made"], 1)
                            after(e, S["k_rest"], i, 2)
                            project(KB, WKH, WKL).then_inc(S["k_made"], 1)
                            tokens_by_features(XTV, lambda k, j: XNH[:, k, j * P:(j + 1) * P],
                                               lambda k, j: XNL[:, k, j * P:(j + 1) * P], WVH, WVL).then_inc(S["v_made"], 1)
                        if cur:
                            after(e, S["p_made"], i)
                            after(e, S["s_summed"], i, 4, 3)
                            for j in range(2):
                                for c_ in range(KC):
                                    m = e.transpose(S0[:, j * D + c_ * P:j * D + (c_ + 1) * P],
                                                    PN[:, (c_ * 2 + j) * TL:(c_ * 2 + j + 1) * TL, :].rearrange("p t b -> p (t b)"),
                                                    ident[:, :])
                            m.then_inc(S["p_transposed"], 1)
                        if prv:
                            after(e, S["o_summed"], i - 1, 4)
                            if nxt:
                                after(e, S["q_rest"], i + 1, 2)
                            for c_ in range(KC):
                                for j in range(2):
                                    m = e.transpose(QOT[:, c_ * D + j * P:c_ * D + (j + 1) * P],
                                                    OB[:, j * NH + c_ * HC:j * NH + (c_ + 1) * HC, :].rearrange("p h d -> p (h d)"),
                                                    ident[:, :])
                            m.then_inc(S["o_transposed"], 1)
                            after(e, S["o_lo"], i - 1)
                            after(e, S["h_updated"], i - 2)
                            tokens_by_features(WB, lambda k, j: OTH[:, k * 2 + j, :, :].rearrange("p b t -> p (b t)"),
                                               lambda k, j: OTL[:, k * 2 + j, :, :].rearrange("p b t -> p (b t)"),
                                               WOH, WOL).then_inc(S["wo_made"], 1)
                    steps(e, body)

        def router_phase(c):
            r3 = lnw[:, 0, :]
            v3 = sbt(c, "v3", [P, NT])
            t3 = sbt(c, "t3", [P, NT])
            X3 = sbt(c, "X3", [P, 2, RT, D])
            X3T = sbt(c, "X3T", [P, 2, KC, RT * P])
            LG = sbt(c, "LG", [P, NT, NE])
            LS = sbt(c, "LS", [P, NT, NE])
            OHT = sbt(c, "OHT", [P, NE, NT])
            CS = sbt(c, "CS", [P, NE, NT])
            go_on = sbt(c, "go_on", [P, NE, NT])
            iota8 = sbt(c, "iota8", [P, NE])
            n_first = sbt(c, "n_first", [P, 2, 2, NE])
            offs = sbt(c, "offs", [P, 2, NE])
            meta = sbt(c, "meta", [P, NT, 4])
            mx = sbt(c, "mx", [P, NT])
            idx = sbt(c, "idx", [P, NT])
            rank = sbt(c, "rank", [P, NT])
            kept = sbt(c, "kept", [P, NT])
            slot_i = sbt(c, "slot_i", [P, NT], I32)
            part_i = sbt(c, "part_i", [P, 2], I32)
            batch_f = sbt(c, "batch_f", [P, 2])
            before = sbt(c, "before", [P, 3, P])
            R = sbt(c, "R", [P, 2, RT, ROW])
            RI = sbt(c, "RI", [P, 2, RT], I32)
            TP = [pst(c, f"x3_bank{i}", [P, KC, 512]) for i in range(2)]
            LP = [pst(c, f"logit_bank{i}", [P, RT, NE]) for i in range(2)]
            OP = pst(c, "offset_bank", [P, 2, NE])
            S = {n: sem(n) for n in ("r3_sqrt", "r3_chain", "x3_made", "x3_transposed", "x3_copied", "logits_made",
                                     "logits_copied", "route_chain", "consts_made", "exp_route", "offsets_made",
                                     "rows_made", "row_gate")}
            rows_sent = [sem("rows_sent0"), sem("rows_sent1")]

            with nc.Block() as block:
                @block.sync
                def _(e):
                    for b in range(B):
                        rows = slice(b * TL, (b + 1) * TL)
                        e.dma_start(out[b, 0:TT, :].rearrange("(l t) f -> l t f", l=TL), H[rows, 0:NTT, :]).then_inc(default_out, 16)
                        e.dma_start(out[b, TT:, :].rearrange("(l t) f -> l t f", l=TL), H[rows, NTT:, :]).then_inc(default_out, 16)
                    e.wait_ge(default_out, 16 * 2 * B)

                @block.gpsimd
                def _(e):
                    n_ = [0]

                    def link(ins):
                        n_[0] += 1
                        ins.then_inc(S["consts_made"], 1)
                        e.wait_ge(S["consts_made"], n_[0])

                    link(e.memset(before[:, :, :], 1.0))
                    b3 = [before[:, i, :] for i in range(3)]
                    link(e.affine_select(out=b3[0], in_=b3[0], compare_op=ALU.is_gt, fill=0.0, base=0,
                                         pattern=[[1, P]], channel_multiplier=-1))
                    for i, base in ((1, 0), (2, TL)):
                        link(e.affine_select(out=b3[i], in_=b3[i], compare_op=ALU.is_gt, fill=0.0, base=base,
                                             pattern=[[TL, B], [0, TL]], channel_multiplier=-1))
                    link(e.iota(iota8[:, :], [[1, NE]], base=0, channel_multiplier=0, allow_small_or_imprecise_dtypes=True))
                    link(e.memset(go_on[:, :, :], 1.0))
                    link(e.memset(go_on[:, :, 0:1], 0.0))
                    link(e.memset(go_on[:, :, NTT:NTT + 1], 0.0))
                    link(e.iota(part_i[:, 0:1], [[0, 1]], base=0, channel_multiplier=1))
                    link(e.iota(mx[:, 0:NTT], [[1, NTT]], base=0, channel_multiplier=NTT, allow_small_or_imprecise_dtypes=True))
                    link(e.iota(mx[:, NTT:], [[1, NTX]], base=TT, channel_multiplier=NTX, allow_small_or_imprecise_dtypes=True))
                    e.wait_ge(slots_filled, 16)

                    def send(n, par):
                        after(e, S["rows_made"], n, 3)
                        gate(e, S["row_gate"], par)
                        for j in range(RT):
                            e.indirect_dma_start(slots, bass.IndirectOffsetOnAxis(ap=RI[:, par, j:j + 1], axis=0),
                                                 R[:, par, j, :], None, bounds_check=NE * CAP - 1, oob_is_err=False
                                                 ).then_inc(rows_sent[par], 16)
                    with e.Fori(0, NR // 2) as n:
                        for u in range(2):
                            send(n * 2 + u, u)
                    for par in range(2):
                        e.wait_ge(rows_sent[par], 16 * NT // 2)

                @block.scalar
                def _(e):
                    e.wait_ge(S["r3_chain"], 8)
                    e.activation(r3, v3[:, :], ACT.Sqrt).then_inc(S["r3_sqrt"], 1)

                    def copy_t(q, par):
                        after(e, S["x3_transposed"], q)
                        after(e, S["logits_made"], q - 2)
                        e.activation(X3T[:, par, :, :], TP[par][:, :, :], ACT.Copy).then_inc(S["x3_copied"], 1)
                    copy_t(0, 0)
                    copy_t(1, 1)
                    with e.Fori(1, NR // 2) as n:
                        for u in range(2):
                            copy_t(n * 2 + u, u)
                    e.wait_ge(S["exp_route"], 1)
                    e.activation(LS[:, :, :], LS[:, :, :], ACT.Exp).then_inc(S["exp_route"], 1)

                @block.vector
                def _(e):
                    n3 = [0]

                    def link3(ins):
                        n3[0] += 1
                        ins.then_inc(S["r3_chain"], 1)
                        e.wait_ge(S["r3_chain"], n3[0])

                    whole_stats(link3, e, st, halves, t3[:, :])
                    link3(e.tensor_scalar(v3[:, :], st[:, 1, :], EPS, None, ALU.add))
                    e.wait_ge(S["r3_sqrt"], 1)
                    link3(e.reciprocal(r3, r3))
                    one_newton_step(link3, e, v3[:, :], r3, t3[:, :])

                    def x3(q, par):
                        after(e, S["x3_transposed"], q - 2)
                        for j in range(RT):
                            T = q * RT + j
                            m = e.tensor_scalar(X3[:, par, j, :], H[:, T, :], st[:, 0, bass.ds(T, 1)], lnw[:, 0, bass.ds(T, 1)],
                                                ALU.subtract, ALU.mult)
                        m.then_inc(S["x3_made"], 1)

                    def copy_l(q, par):
                        after(e, S["logits_made"], q)
                        e.tensor_copy(LG[:, bass.ds(q * RT, RT), :], LP[par][:, :, :]).then_inc(S["logits_copied"], 1)

                    x3(0, 0)
                    x3(1, 1)
                    with e.Fori(0, NR // 2 - 1) as n:
                        for u in range(2):
                            x3(n * 2 + (2 + u), u)
                            copy_l(n * 2 + u, u)
                    copy_l(NR - 2, 0)
                    copy_l(NR - 1, 1)
                    e.wait_ge(S["logits_copied"], NR)
                    n_ = [0]

                    def link(ins):
                        n_[0] += 1
                        ins.then_inc(S["route_chain"], 1)
                        e.wait_ge(S["route_chain"], n_[0])

                    e.wait_ge(S["consts_made"], 11)
                    link(e.tensor_scalar(part_i[:, 1:2], part_i[:, 0:1], TL.bit_length() - 1, None, ALU.logical_shift_right))
                    link(e.tensor_copy(batch_f[:, 0:1], part_i[:, 1:2]))
                    link(e.tensor_scalar(batch_f[:, 1:2], batch_f[:, 0:1], float(TT + TX - TL * NTX), None, ALU.mult))
                    link(e.tensor_scalar(batch_f[:, 0:1], batch_f[:, 0:1], float(TT + TX - TL * NTT), None, ALU.mult))
                    for s, seg in enumerate((slice(0, NTT), slice(NTT, NT))):
                        link(e.tensor_scalar(meta[:, seg, 3], mx[:, seg], batch_f[:, s:s + 1], None, ALU.add))
                    link(e.tensor_reduce(mx[:, :], LG[:, :, :], AX, ALU.max))
                    mxb = mx[:, :].unsqueeze(2).broadcast_to([P, NT, NE])
                    link(e.tensor_tensor(LS[:, :, :], LG[:, :, :], mxb, ALU.subtract))
                    e.tensor_tensor(LG[:, :, :], LG[:, :, :], mxb, ALU.is_equal).then_inc(S["exp_route"], 1)
                    e.wait_ge(S["exp_route"], 2)
                    link(e.tensor_reduce(rank[:, :], LS[:, :, :], AX, ALU.add))
                    link(e.reciprocal(meta[:, :, 2], rank[:, :]))
                    iob = iota8[:, :].unsqueeze(1).broadcast_to([P, NT, NE])
                    link(e.tensor_scalar(LG[:, :, :], LG[:, :, :], -float(NE), float(NE), ALU.mult, ALU.add))
                    link(e.tensor_tensor(LG[:, :, :], LG[:, :, :], iob, ALU.add))
                    link(e.tensor_reduce(idx[:, :], LG[:, :, :], AX, ALU.min))
                    link(e.tensor_tensor(OHT[:, :, :].rearrange("p e t -> p t e"), iob,
                                         idx[:, :].unsqueeze(2).broadcast_to([P, NT, NE]), ALU.is_equal))
                    link(e.tensor_tensor_scan(CS[:, :, :].rearrange("p e t -> p (e t)"), go_on[:, :, :].rearrange("p e t -> p (e t)"),
                                              OHT[:, :, :].rearrange("p e t -> p (e t)"), 0.0, ALU.mult, ALU.add))
                    e.wait_ge(S["offsets_made"], 1)
                    link(e.tensor_copy(offs[:, :, :], OP[:, :, :]))
                    for s, (a, b_) in enumerate(((0, NTT), (NTT, NT))):
                        link(e.tensor_tensor(CS[:, :, a:b_], CS[:, :, a:b_],
                                             offs[:, s, :].unsqueeze(2).broadcast_to([P, NE, b_ - a]), ALU.add))
                    link(e.tensor_tensor(CS[:, :, :], CS[:, :, :], OHT[:, :, :], ALU.mult))
                    link(e.tensor_reduce(rank[:, :], CS[:, :, :].rearrange("p e t -> p t e"), AX, ALU.add))
                    link(e.tensor_scalar(kept[:, :], rank[:, :], float(CAP), NOWHERE, ALU.is_gt, ALU.mult))
                    link(e.tensor_scalar(idx[:, :], idx[:, :], float(CAP), -1.0, ALU.mult, ALU.add))
                    link(e.tensor_tensor(idx[:, :], idx[:, :], rank[:, :], ALU.add))
                    link(e.tensor_tensor(idx[:, :], idx[:, :], kept[:, :], ALU.add))
                    link(e.tensor_copy(slot_i[:, :], idx[:, :]))
                    link(e.tensor_copy(meta[:, :, 0], st[:, 0, :]))
                    link(e.tensor_copy(meta[:, :, 1], r3))

                    def rows(n, par):
                        e.tensor_copy(R[:, par, :, 0:D], H[:, bass.ds(n * RT, RT), :]).then_inc(S["rows_made"], 1)
                        e.tensor_copy(R[:, par, :, D:], meta[:, bass.ds(n * RT, RT), :]).then_inc(S["rows_made"], 1)
                        e.tensor_copy(RI[:, par, :], slot_i[:, bass.ds(n * RT, RT)]).then_inc(S["rows_made"], 1)
                    rows(0, 0)
                    rows(1, 1)
                    with e.Fori(1, NR // 2) as n:
                        for u in range(2):
                            after(e, S["row_gate"], n * 2 + (u - 2))
                            e.wait_ge(rows_sent[u], n * (16 * RT))
                            rows(n * 2 + u, u)

                @block.tensor
                def _(e):
                    def transposes(q, par):
                        after(e, S["x3_made"], q)
                        after(e, S["x3_copied"], q - 2)
                        for c_ in range(KC):
                            for j in range(RT):
                                m = e.transpose(TP[par][:, c_, j * P:(j + 1) * P], X3[:, par, j, c_ * P:(c_ + 1) * P], ident[:, :])
                        m.then_inc(S["x3_transposed"], 1)

                    def logits(q, par):
                        after(e, S["x3_copied"], q)
                        after(e, S["logits_copied"], q - 2)
                        for j in range(RT):
                            for k in range(KC):
                                m = e.matmul(LP[par][:, j, :], X3T[:, par, k, j * P:(j + 1) * P], wr_t[:, k, :],
                                             start=(k == 0), stop=(k == KC - 1))
                        m.then_inc(S["logits_made"], 1)

                    def two(n):
                        for u in range(2):
                            transposes(n * 2 + (1 + u), (1 + u) % 2)
                            logits(n * 2 + u, u)

                    transposes(0, 0)
                    two(0)
                    with e.Fori(1, NR // 2 - 1) as n:
                        two(n)
                    transposes(NR - 1, 1)
                    logits(NR - 2, 0)
                    logits(NR - 1, 1)
                    e.wait_ge(S["route_chain"], 15)
                    tok, text = CS[:, :, NTT - 1], CS[:, :, NT - 1]
                    for s, (m_tok, m_text) in enumerate(((0, 1), (2, 0))):
                        e.matmul(OP[:, s, :], before[:, m_tok, :], tok, start=True, stop=False)
                        m = e.matmul(OP[:, s, :], before[:, m_text, :], text, start=False, stop=True)
                    m.then_inc(S["offsets_made"], 1)

        def experts_phase(c):
            stage1 = sbt(c, "stage1", [P, KC, FF])
            stage2 = sbt(c, "stage2", [P, FC, D])
            W1 = [(sbt(c, f"w1_hi{s}", [P, KC, FF], F32R), sbt(c, f"w1_lo{s}", [P, KC, FF], F32R)) for s in range(2)]
            W2 = [(sbt(c, f"w2_hi{s}", [P, FC, D], F32R), sbt(c, f"w2_lo{s}", [P, FC, D], F32R)) for s in range(2)]
            b1_e = sbt(c, "b1_e", [P, 2, FC])
            b2_b = sbt(c, "b2_b", [P, NE, D])
            X = sbt(c, "X", [P, 2, BT, ROW])
            XE = sbt(c, "XE", [P, BT, D])
            XEH = sbt(c, "XEH", [P, KC, BLK], F32R)
            XEL = sbt(c, "XEL", [P, KC, BLK], F32R)
            G = sbt(c, "G", [P, 2, BLK])
            GH = sbt(c, "GH", [P, FC, BLK], F32R)
            GL = sbt(c, "GL", [P, FC, BLK], F32R)
            Y1 = sbt(c, "Y1", [P, BT, D])
            Y = sbt(c, "Y", [P, 2, BT, D])
            YI = sbt(c, "YI", [P, 2, BT], I32)
            XP = [pst(c, f"xe_bank{i}", [P, 512]) for i in range(KC)]
            GP = [pst(c, f"hidden_bank{i}", [P, 512]) for i in range(2)]
            YP = [pst(c, f"y_bank{i}", [P, 512]) for i in range(2)]
            S = {n: sem(n) for n in ("b2_in", "xe_made", "xe_transposed", "xe_hi", "xe_lo", "hidden_made", "gelu_made",
                                     "g_split", "y_made", "y_added", "b1_ready", "store_gate", "w_split", "w_rounded", "g_rounded", "y_biased")}
            weights_in = sem("weights_in")
            x_rows_in = [sem("x_rows_in0"), sem("x_rows_in1")]
            stored = [sem("stored0"), sem("stored1")]
            slots_v = slots.rearrange("(g p t) r -> g p t r", p=P, t=BT)
            w1_v = w1.rearrange("e (c p) f -> e p c f", p=P)
            w2_v = w2.rearrange("e (c p) f -> e p c f", p=P)
            PIECES = 4

            def blocks(e, body):
                body(0, 0, 0)
                for u in range(1, 2 * NBE):
                    body(0, u, u)
                with e.Fori(1, NE // 2 - 1) as n:
                    for u in range(2 * NBE):
                        body(n, u, n * (2 * NBE) + u)
                for u in range(2 * NBE):
                    body(NE // 2 - 1, u, NB - 2 * NBE + u)

            with nc.Block() as block:
                @block.sync
                def _(e):
                    e.dma_start(b2_b[:, :, :], b2.unsqueeze(0).broadcast_to([P, NE, D])).then_inc(S["b2_in"], 16)

                    def weights(ex):
                        e.dma_start(stage1[:, :, :], w1_v[ex]).then_inc(weights_in, 16)
                        e.dma_start(stage2[:, :, :], w2_v[ex]).then_inc(weights_in, 16)

                    def rows(g, par):
                        e.dma_start(X[:, par, :, :], slots_v[g]).then_inc(x_rows_in[par], 16)

                    weights(0)
                    rows(0, 0)
                    e.wait_ge(S["w_split"], PIECES)
                    weights(1)

                    def body(n, u, g):
                        after(e, S["y_added"], g - 1, BT)
                        if not (isinstance(g, int) and g == NB - 1):
                            rows(g + 1, (u + 1) % 2)
                        if u % NBE == NBE - 1:
                            s = u // NBE
                            ex = n * 2 + s
                            if not (isinstance(ex, int) and (ex + 2 >= NE or ex < 0)):
                                e.wait_ge(S["w_split"], (ex + 2) * PIECES)
                                weights(ex + 2)
                    blocks(e, body)

                @block.gpsimd
                def _(e):
                    def body(n, u, g):
                        for t in range(BT):
                            after(e, S["y_added"], g, BT, t + 1)
                            gate(e, S["store_gate"], u % 2, t)
                            e.indirect_dma_start(out_rows, bass.IndirectOffsetOnAxis(ap=YI[:, u % 2, t:t + 1], axis=0),
                                                 Y[:, u % 2, t, :], None, bounds_check=NTOK - 1, oob_is_err=False
                                                 ).then_inc(stored[u % 2], 16)
                    blocks(e, body)
                    for par in range(2):
                        e.wait_ge(stored[par], 16 * BT * NB // 2)

                @block.scalar
                def _(e):
                    def xe_hi(g):
                        after(e, S["xe_transposed"], g)
                        after(e, S["hidden_made"], g - 1, FC)
                        for c_ in range(KC):
                            e.activation(XEH[:, c_, :], XP[c_][:, 0:BLK], ACT.Copy).then_inc(S["xe_hi"], 1)

                    xe_hi(0)

                    def body(n, u, g):
                        s = u // NBE
                        if u % NBE == 0:
                            e.wait_ge(S["b1_ready"], n * 2 + s + 1)
                        for f in range(FC):
                            after(e, S["hidden_made"], g, FC, f + 1)
                            after(e, S["g_split"], g, FC, f - 1)
                            e.activation(G[:, f % 2, :], GP[f % 2][:, 0:BLK], ACT.Gelu,
                                         bias=b1_e[:, s, f:f + 1]).then_inc(S["gelu_made"], 1)
                        if not (isinstance(g, int) and g == NB - 1):
                            xe_hi(g + 1)
                    blocks(e, body)

                @block.vector
                def _(e):
                    def split_piece(k, s, total):
                        stage, (hi_, lo_), kk = (stage1, W1[s], k) if k < KC else (stage2, W2[s], k - KC)
                        if k < KC:
                            a, h_, l_ = stage[:, kk, :], hi_[:, kk, :], lo_[:, kk, :]
                        else:
                            half = slice(kk * FC // 2, (kk + 1) * FC // 2)
                            a, h_, l_ = stage[:, half, :], hi_[:, half, :], lo_[:, half, :]
                        e.tensor_copy(h_, a).then_inc(S["w_rounded"], 1)
                        e.wait_ge(S["w_rounded"], total)
                        e.tensor_tensor(l_, a, h_.bitcast(F32), ALU.subtract).then_inc(S["w_split"], 1)

                    def expert_b1(ex, s):
                        e.tensor_copy(b1_e[:, s, :], b1_t[:, bass.ds(ex * FC, FC)]).then_inc(S["b1_ready"], 1)

                    def xe(g, par, count):
                        e.wait_ge(x_rows_in[par], count)
                        after(e, S["xe_transposed"], g - 1)
                        for t in range(BT):
                            m = e.tensor_scalar(XE[:, t, :], X[:, par, t, 0:D], X[:, par, t, D:D + 1], X[:, par, t, D + 1:D + 2],
                                                ALU.subtract, ALU.mult)
                        m.then_inc(S["xe_made"], 1)

                    def xe_lo(g):
                        for c_ in range(KC):
                            after(e, S["xe_hi"], g, KC, c_ + 1)
                            e.tensor_tensor(XEL[:, c_, :], XP[c_][:, 0:BLK], XEH[:, c_, :].bitcast(F32),
                                            ALU.subtract).then_inc(S["xe_lo"], 1)

                    e.wait_ge(weights_in, 32)
                    for k in range(PIECES):
                        split_piece(k, 0, k + 1)
                    expert_b1(0, 0)
                    xe(0, 0, 16)
                    xe_lo(0)
                    e.wait_ge(S["b2_in"], 16)

                    def body(n, u, g):
                        par = u % 2
                        s = u // NBE
                        ex = n * 2 + s
                        end = isinstance(g, int) and g == NB - 1
                        after(e, S["y_made"], g - 1, BT)
                        for f in range(FC):
                            after(e, S["gelu_made"], g, FC, f + 1)
                            e.tensor_copy(GH[:, f, :], G[:, f % 2, :]).then_inc(S["g_rounded"], 1)
                            after(e, S["g_rounded"], g, FC, f + 1)
                            e.tensor_tensor(GL[:, f, :], G[:, f % 2, :], GH[:, f, :].bitcast(F32), ALU.subtract
                                            ).then_inc(S["g_split"], 1)
                            if f == FC // 2 and not end:
                                xe(g + 1, 1 - par, (n * NBE + ((u + 1) // 2 + 1)) * 16)
                        if u % NBE < PIECES and not (isinstance(ex, int) and ex == NE - 1):
                            e.wait_ge(weights_in, (ex + 2) * 32)
                            split_piece(u % NBE, 1 - s, ex * PIECES + (PIECES + u % NBE + 1))
                            if u % NBE == 0:
                                expert_b1(ex + 1, 1 - s)
                        if not end:
                            xe_lo(g + 1)
                        later_round = (n * NBE + u // 2) * (16 * BT)
                        for t in range(BT):
                            after(e, S["y_made"], g, BT, t + 1)
                            if t == 0 and not (isinstance(later_round, int) and later_round <= 0):
                                after(e, S["store_gate"], g - 2, BT)
                                e.wait_ge(stored[par], later_round)
                            e.tensor_tensor(Y1[:, t, :], YP[(BT * u + t) % 2][:, 0:D],
                                            b2_b[:, ex, :], ALU.add).then_inc(S["y_biased"], 1)
                            if t == 0:
                                e.tensor_copy(YI[:, par, :], X[:, par, :, D + 3]).then_inc(S["y_biased"], 1)
                            after(e, S["y_biased"], g, BT + 1, t + 2)
                            ins = e.scalar_tensor_tensor(out=Y[:, par, t, :], in0=Y1[:, t, :], scalar=X[:, par, t, D + 2:D + 3],
                                                         in1=X[:, par, t, 0:D], op0=ALU.mult, op1=ALU.add)
                            ins.then_inc(S["y_added"], 1)
                    blocks(e, body)

                @block.tensor
                def _(e):
                    def transposes(g):
                        after(e, S["xe_made"], g)
                        after(e, S["xe_lo"], g - 1, KC)
                        for c_ in range(KC):
                            for t in range(BT):
                                m = e.transpose(XP[c_][:, t * P:(t + 1) * P], XE[:, t, c_ * P:(c_ + 1) * P], ident[:, :])
                        m.then_inc(S["xe_transposed"], 1)

                    transposes(0)

                    def body(n, u, g):
                        s = u // NBE
                        ex = n * 2 + s
                        if u % NBE == 0:
                            e.wait_ge(S["w_split"], (ex + 1) * PIECES)
                        after(e, S["xe_lo"], g, KC)
                        for f in range(FC):
                            after(e, S["gelu_made"], g, FC, f - 1)
                            n_ = 0
                            for k in range(KC):
                                for w, a in ((W1[s][0], XEH), (W1[s][1], XEH), (W1[s][0], XEL)):
                                    m = e.matmul(GP[f % 2][:, 0:BLK], w[:, k, f * P:(f + 1) * P], a[:, k, :],
                                                 start=(n_ == 0), stop=(n_ == 3 * KC - 1))
                                    n_ += 1
                            m.then_inc(S["hidden_made"], 1)
                        if not (isinstance(g, int) and g == NB - 1):
                            transposes(g + 1)
                        for t in range(BT):
                            after(e, S["y_added"], g, BT, t - 1)
                            n_ = 0
                            for f in range(FC):
                                if t == 0:
                                    after(e, S["g_split"], g, FC, f + 1)
                                for a, w in ((GH, W2[s][0]), (GH, W2[s][1]), (GL, W2[s][0])):
                                    m = e.matmul(YP[(BT * u + t) % 2][:, 0:D], a[:, f, t * P:(t + 1) * P], w[:, f, :],
                                                 start=(n_ == 0), stop=(n_ == 3 * FC - 1))
                                    n_ += 1
                            m.then_inc(S["y_made"], 1)
                    blocks(e, body)

        with ExitStack() as ac:
            attn_w = [(sbt(ac, n + "_hi", [P, KC, D], F32R), sbt(ac, n + "_lo", [P, KC, D], F32R))
                      for n in ("wq", "wk", "wv", "wo")]
            bq_c = sbt(ac, "bq_c", [P, KC])
            bk_c = sbt(ac, "bk_c", [P, KC])
            bo_b = sbt(ac, "bo_b", [P, D])
            with ExitStack() as c:
                tok_phase(c, attn_w, bq_c, bk_c, bo_b)
            with ExitStack() as c:
                attention_phase(c, attn_w, bq_c, bk_c, bo_b)
        with ExitStack() as c:
            router_phase(c)
        hctx.close()
        with ExitStack() as c:
            experts_phase(c)


_INS = ["x", "txt", "L0_tok_weight", "L0_tok_weighted_sum", "L0_attn_ln_g", "L0_attn_ln_b", "L0_attn_Wq", "L0_attn_bq",
        "L0_attn_Wk", "L0_attn_bk", "L0_attn_Wv", "L0_attn_bv", "L0_attn_Wo", "L0_attn_bo", "L0_ffn_router_w",
        "L0_ffn_w1", "L0_ffn_b1", "L0_ffn_w2", "L0_ffn_b2"]
_OUTS = [((B, TT + TX, D), "float32")]


def kernel(**inputs):
    import numpy as _np
    import concourse.bacc as _bacc
    from concourse import mybir as _mybir
    from concourse.bass_utils import run_bass_kernel_spmd as _run

    nc = _bacc.Bacc("TRN2", target_bir_lowering=False, num_devices=1)
    arrays, args = {}, []
    for name in _INS:
        a = _np.ascontiguousarray(inputs[name])
        arrays[f"in_{name}_dram"] = a
        args.append(nc.dram_tensor(f"in_{name}_dram", a.shape, _mybir.dt.from_np(a.dtype), kind="ExternalInput").ap())
    for i, (shape, dtype) in enumerate(_OUTS):
        dt = _mybir.dt.from_np(_np.dtype(dtype))
        args.append(nc.dram_tensor(f"out_{i}_dram", shape, dt, kind="ExternalOutput").ap())
    fusion_kernel(nc, *args)
    r = _run(nc, [arrays], core_ids=[0])
    return r.results[0]["out_0_dram"]
```

```python
import concourse.bass as bass
from concourse import mybir
from contextlib import ExitStack

F32 = mybir.dt.float32
F32R = mybir.dt.float32r
BF16 = mybir.dt.bfloat16
I32 = mybir.dt.int32
ALU = mybir.AluOpType
ACT = mybir.ActivationFunctionType
AX = mybir.AxisListType.X

P = 128
B, TT, TX, D = 16, 512, 128, 256
KT = 1024
CK = KT // P
TL = P // B
NTT, NTX = TT // TL, TX // TL
NT = NTT + NTX
NI = NT // 2
NH, DH = 16, 16
KC = D // P
HC = NH // KC
EPS = 1e-5
SCALE = DH ** -0.5
NE, FF = 8, 1024
FC = FF // P
NTOK = B * (TT + TX)
CAP = -(-3 * NTOK // (2 * NE))
BT = 3
BLK = BT * P
NBE = CAP // BLK
NB = NE * NBE
ROW = D + 4
NOWHERE = float(1 << 20)
RT = 4
NR = NT // RT


def after(eng, sem, i, n=1, k=None):
    v = i * n + (n if k is None else k)
    if isinstance(v, int) and v <= 0:
        return
    eng.wait_ge(sem, v)


def fusion_kernel(nc, x, txt, tok_w, tok_ws, ln_g, ln_b, wq, bq, wk, bk, wv, bv, wo, bo,
                  router_w, w1, b1, w2, b2, out):
    ctx = ExitStack()

    def sbt(c, name, shape, dt=F32):
        return c.enter_context(nc.sbuf_tensor(name, shape, dt))

    def pst(c, name, shape):
        return c.enter_context(nc.psum_tensor(name, shape, F32))

    def sem(name):
        return ctx.enter_context(nc.semaphore(name))

    def one_newton_step(link, e, v, y, t):
        link(e.tensor_tensor(t, y, y, ALU.mult))
        link(e.tensor_tensor(t, t, v, ALU.mult))
        link(e.tensor_scalar(t, t, -0.5, 1.5, ALU.mult, ALU.add))
        link(e.tensor_tensor(y, y, t, ALU.mult))

    def whole_stats(link, e, st, halves, t):
        link(e.tensor_tensor(st[:, 0, :], halves[:, :, 1], halves[:, :, 4], ALU.add))
        link(e.tensor_tensor(t, halves[:, :, 1], halves[:, :, 4], ALU.subtract))
        link(e.tensor_tensor(t, t, t, ALU.mult))
        link(e.tensor_tensor(st[:, 1, :], halves[:, :, 2], halves[:, :, 5], ALU.add))
        link(e.tensor_scalar(st[:, 0, :], st[:, 0, :], 0.5, None, ALU.mult))
        link(e.tensor_scalar(st[:, 1, :], st[:, 1, :], 1.0 / D, None, ALU.mult))
        link(e.scalar_tensor_tensor(out=st[:, 1, :], in0=t, scalar=0.25, in1=st[:, 1, :], op0=ALU.mult, op1=ALU.add))

    with ctx:
        slots = nc.dram_tensor("slots", [NE * CAP, ROW], F32, kind="Internal").ap()
        slots_v = slots.rearrange("(g p t) r -> g p t r", p=P, t=BT)
        assert NB == NI
        out_rows = out.rearrange("b t f -> (b t) f")
        ident = sbt(ctx, "ident", [P, P])
        wr_t = sbt(ctx, "wr_t", [P, KC, NE])
        b1_t = sbt(ctx, "b1_t", [P, NE * FC])
        ident_ready = sem("ident_ready")
        slots_filled = sem("slots_filled")
        default_out = sem("default_out")

        gated = sbt(ctx, "gated", [P, 2, BT])

        hctx = ctx.enter_context(ExitStack())
        H = sbt(hctx, "H", [P, NT, D])
        halves = sbt(hctx, "halves", [P, NT, 6])
        st = sbt(hctx, "st", [P, 2, NT])
        lnw = sbt(hctx, "lnw", [P, 5, NT])

        def gate(e, passed, par, t=0):
            e.tensor_tensor(gated[:, par, t:t + 1], ident[:, 0:1], ident[:, 0:1], ALU.add).then_inc(passed, 1)


        fill = sbt(hctx, "fill", [P, ROW])

        def tok_phase(c, attn_w, bq_c, bk_c, bo_b):
            XS = sbt(c, "XS", [P, 2, 2, KT])
            XH = sbt(c, "XH", [P, 2, KT], F32R)
            XL = sbt(c, "XL", [P, 2, KT], F32R)
            WH = sbt(c, "WH", [P, CK, D], F32R)
            WL = sbt(c, "WL", [P, CK, D], F32R)
            w_outer = sbt(c, "w_outer", [P, KC, D, 4])
            ws_in = sbt(c, "ws_in", [P, KC, D])
            w_in = sbt(c, "w_in", [P, KC, 4])
            aw_in = sbt(c, "aw_in", [P, 4, KC, D])
            g_c = sbt(c, "g_c", [P, KC])
            b_c = sbt(c, "b_c", [P, KC])
            bias_in = sbt(c, "bias_in", [P, 3, KC])
            bv_b = sbt(c, "bv_b", [P, KC, P])
            bo_in = sbt(c, "bo_in", [P, D])
            wr_in = sbt(c, "wr_in", [NE, D])
            b1_in = sbt(c, "b1_in", [NE * FC, P])
            XT = pst(c, "XT", [P, 2, 2, 512])
            HP = pst(c, "HP", [P, 2, 512])
            WB = pst(c, "WB", [P, 2, 512])
            tok_weights_in, small_in, txt_in = sem("tok_weights_in"), sem("small_in"), sem("txt_in")
            x_in = [sem("x_in0"), sem("x_in1")]
            outer_made, w_transposed, w_hi, w_lo = sem("outer_made"), sem("w_transposed"), sem("w_hi"), sem("w_lo")
            fill_made, x_transposed, x_hi, x_lo = sem("fill_made"), sem("x_transposed"), sem("x_hi"), sem("x_lo")
            h_made, h_copied, h_stats = sem("h_made"), sem("h_copied"), sem("h_stats")
            tok_chain, bias_made, bv_spread, bo_made = sem("tok_chain"), sem("bias_made"), sem("bv_spread"), sem("bo_made")
            router_transposed, b1_transposed, small_copied = sem("router_transposed"), sem("b1_transposed"), sem("small_copied")
            NSMALL = 4 + 5 + 3
            xr = x.rearrange("b h i d -> (b h) (i d)").rearrange("(p t) k -> p t k", t=NTT)
            txr = txt.rearrange("b t f -> (b t) f").rearrange("(p t) f -> p t f", t=NTX)
            outer2 = w_outer[:, :, :, :].rearrange("p c i d -> p c (i d)")

            with nc.Block() as block:
                @block.sync
                def _(e):
                    e.dma_start(ws_in[:, :, :], tok_ws.rearrange("(c p) i -> p c i", p=P)).then_inc(tok_weights_in, 16)
                    e.dma_start(w_in[:, :, :], tok_w.rearrange("(c p) d -> p c d", p=P)).then_inc(tok_weights_in, 16)
                    for u in range(2):
                        e.dma_start(XS[:, u, :, :], xr[:, 2 * u:2 * u + 2, :]).then_inc(x_in[u], 16)
                    with e.Fori(1, NTT // 4) as n:
                        for u in range(2):
                            e.wait_ge(x_transposed, n * 8 + (4 * u - 4))
                            e.dma_start(XS[:, u, :, :], xr[:, bass.ds(n * 4 + 2 * u, 2), :]).then_inc(x_in[u], 16)

                @block.gpsimd
                def _(e):
                    e.memset(fill[:, :], 0.0).then_inc(fill_made, 1)
                    e.memset(ident[:, :], 0.0).then_inc(fill_made, 1)
                    e.wait_ge(fill_made, 2)
                    e.memset(fill[:, D + 3:ROW], NOWHERE).then_inc(fill_made, 1)
                    e.affine_select(out=ident[:, :], in_=ident[:, :], compare_op=ALU.not_equal, fill=1.0, base=0,
                                    pattern=[[-1, P]], channel_multiplier=1).then_inc(ident_ready, 1)

                @block.scalar
                def _(e):
                    for i, w in enumerate((wq, wk, wv, wo)):
                        e.dma_start(aw_in[:, i, :, :], w.rearrange("(c p) n -> p c n", p=P)).then_inc(small_in, 16)
                    for dst, src in ((g_c[:, :], ln_g), (b_c[:, :], ln_b), (bias_in[:, 0, :], bq),
                                     (bias_in[:, 1, :], bk), (bias_in[:, 2, :], bv)):
                        e.dma_start(dst, src.rearrange("(c p) -> p c", p=P),
                                    allow_slow_non_contiguous=True).then_inc(small_in, 16)
                    e.dma_start(bo_in[:, :], bo.unsqueeze(0).broadcast_to([P, D])).then_inc(small_in, 16)
                    e.dma_start(wr_in[:, :], router_w).then_inc(small_in, 16)
                    e.dma_start(b1_in[:, :], b1.rearrange("e (f p) -> (e f) p", p=P)).then_inc(small_in, 16)
                    e.dma_start(H[:, NTT:, :], txr).then_inc(txt_in, 16)
                    e.wait_ge(fill_made, 3)
                    for k in range(CK):
                        e.wait_ge(w_transposed, k + 1)
                        e.activation(WH[:, k, :], WB[:, k % 2, 0:D], ACT.Copy).then_inc(w_hi, 1)

                    def hi(T, par):
                        for h in range(2):
                            after(e, x_transposed, T, 2, h + 1)
                            after(e, h_made, T - 2)
                            e.activation(XH[:, par, h * 512:(h + 1) * 512], XT[:, par, h, :], ACT.Copy).then_inc(x_hi, 1)

                    def copy_h(T, par):
                        after(e, h_made, T)
                        e.activation(H[:, T, :], HP[:, par, 0:D], ACT.Copy).then_inc(h_copied, 1)

                    hi(0, 0)
                    with e.Fori(0, NTT // 2 - 1) as n:
                        for u in range(2):
                            hi(n * 2 + (u + 1), (u + 1) % 2)
                            copy_h(n * 2 + u, u)
                    hi(NTT - 1, 1)
                    copy_h(NTT - 2, 0)
                    copy_h(NTT - 1, 1)

                @block.vector
                def _(e):
                    chained = [0]

                    def link(ins):
                        chained[0] += 1
                        ins.then_inc(tok_chain, 1)
                        e.wait_ge(tok_chain, chained[0])

                    e.wait_ge(tok_weights_in, 32)
                    for c_ in range(KC):
                        e.tensor_tensor(w_outer[:, c_, :, :], ws_in[:, c_, :].unsqueeze(2).broadcast_to([P, D, 4]),
                                        w_in[:, c_, :].unsqueeze(1).broadcast_to([P, D, 4]), ALU.mult).then_inc(outer_made, 1)
                    for k in range(CK):
                        e.wait_ge(w_hi, k + 1)
                        e.tensor_tensor(WL[:, k, :], WB[:, k % 2, 0:D], WH[:, k, :].bitcast(F32),
                                        ALU.subtract).then_inc(w_lo, 1)
                    e.wait_ge(small_in, 16 * NSMALL)
                    e.wait_ge(bias_made, 1)
                    e.tensor_tensor(bq_c[:, :], WB[:, 0, 0:KC], bias_in[:, 0, :], ALU.add).then_inc(small_copied, 1)
                    e.tensor_tensor(bk_c[:, :], WB[:, 0, KC:2 * KC], bias_in[:, 1, :], ALU.add).then_inc(small_copied, 1)
                    link(e.tensor_tensor(bias_in[:, 2, :], WB[:, 0, 2 * KC:3 * KC], bias_in[:, 2, :], ALU.add))
                    e.tensor_copy(bv_b[:, :, :], bias_in[:, 2, :].unsqueeze(2).broadcast_to([P, KC, P])).then_inc(bv_spread, 1)
                    for i in range(4):
                        hi_, lo_ = attn_w[i]
                        if i < 3:
                            for k in range(KC):
                                link(e.tensor_scalar(aw_in[:, i, k, :], aw_in[:, i, k, :], g_c[:, k:k + 1], None, ALU.mult))
                        link(e.tensor_copy(hi_[:, :, :], aw_in[:, i, :, :]))
                        link(e.tensor_tensor(lo_[:, :, :], aw_in[:, i, :, :], hi_[:, :, :].bitcast(F32), ALU.subtract))
                    e.wait_ge(bo_made, 1)
                    e.tensor_tensor(bo_b[:, :], WB[:, 1, 0:D], bo_in[:, :], ALU.add).then_inc(small_copied, 1)
                    e.wait_ge(router_transposed, 1)
                    e.tensor_copy(wr_t[:, :, :], WB[:, 0, 0:KC * NE].rearrange("p (c e) -> p c e", c=KC)).then_inc(small_copied, 1)
                    e.wait_ge(b1_transposed, 1)
                    e.tensor_copy(b1_t[:, :], WB[:, 1, 0:NE * FC]).then_inc(small_copied, 1)

                    def lo(T, par):
                        for h in range(2):
                            after(e, x_hi, T, 2, h + 1)
                            e.tensor_tensor(XL[:, par, h * 512:(h + 1) * 512], XT[:, par, h, :],
                                            XH[:, par, h * 512:(h + 1) * 512].bitcast(F32), ALU.subtract).then_inc(x_lo, 1)

                    def stats(T):
                        e.bn_stats(halves[:, T, :], H[:, T, :]).then_inc(h_stats, 1)

                    lo(0, 0)
                    lo(1, 1)
                    e.wait_ge(txt_in, 16)

                    def two(n):
                        for u in range(2):
                            after(e, h_copied, n * 2 + u)
                            lo(n * 2 + (u + 2), u)
                            stats(n * 2 + u)
                    with e.Fori(0, NTX) as n:
                        two(n)
                        stats(n + NTT)
                    with e.Fori(NTX, NTT // 2 - 1) as n:
                        two(n)
                    for T in (NTT - 2, NTT - 1):
                        after(e, h_copied, T)
                        stats(T)
                    e.wait_ge(h_stats, NT)

                @block.tensor
                def _(e):
                    e.wait_ge(ident_ready, 1)
                    e.wait_ge(outer_made, 2)
                    for k in range(CK):
                        if k >= 2:
                            e.wait_ge(w_lo, k - 1)
                        for c_ in range(KC):
                            m = e.transpose(WB[:, k % 2, c_ * P:(c_ + 1) * P], outer2[:, c_, k * P:(k + 1) * P], ident[:, :])
                        m.then_inc(w_transposed, 1)
                    e.wait_ge(small_in, 16 * NSMALL)
                    e.wait_ge(w_lo, CK)
                    for i in range(3):
                        for c_ in range(KC):
                            for k in range(KC):
                                m = e.matmul(WB[:, 0, i * KC + c_:i * KC + c_ + 1], aw_in[:, i, k, c_ * P:(c_ + 1) * P],
                                             b_c[:, k:k + 1], start=(k == 0), stop=(k == KC - 1))
                    m.then_inc(bias_made, 1)
                    e.wait_ge(bv_spread, 1)
                    for k in range(KC):
                        m = e.matmul(WB[:, 1, 0:D], bv_b[:, k, :], aw_in[:, 3, k, :], start=(k == 0), stop=(k == KC - 1))
                    m.then_inc(bo_made, 1)
                    for c_ in range(KC):
                        m = e.transpose(WB[:, 0, c_ * NE:(c_ + 1) * NE], wr_in[:, c_ * P:(c_ + 1) * P], ident[0:NE, 0:NE])
                    m.then_inc(router_transposed, 1)
                    e.wait_ge(small_copied, 3)
                    e.transpose(WB[:, 1, 0:NE * FC], b1_in[:, :], ident[0:NE * FC, 0:NE * FC]).then_inc(b1_transposed, 1)

                    def transposes(T, u):
                        for h in range(2):
                            after(e, x_lo, T - 2, 2, h + 1)
                            for k in range(4):
                                kk = h * 4 + k
                                m = e.transpose(XT[:, u % 2, h, k * P:(k + 1) * P],
                                                XS[:, u // 2, u % 2, kk * P:(kk + 1) * P], ident[:, :])
                            m.then_inc(x_transposed, 1)

                    def products(T, par):
                        after(e, x_lo, T, 2)
                        after(e, h_copied, T - 2)
                        n_ = 0
                        for k in range(CK):
                            for a, w in ((XH, WH), (XH, WL), (XL, WH)):
                                m = e.matmul(HP[:, par, 0:D], a[:, par, k * P:(k + 1) * P], w[:, k, :],
                                             start=(n_ == 0), stop=(n_ == 3 * CK - 1))
                                n_ += 1
                        m.then_inc(h_made, 1)

                    def four(n):
                        for u in range(4):
                            if u == 1:
                                e.wait_ge(x_in[1], n * 16 + 16)
                            if u == 3:
                                e.wait_ge(x_in[0], n * 16 + 32)
                            transposes(n * 4 + (u + 1), (u + 1) % 4)
                            products(n * 4 + u, u % 2)

                    e.wait_ge(x_in[0], 16)
                    transposes(0, 0)
                    four(0)
                    with e.Fori(1, NTT // 4 - 1) as n:
                        four(n)
                    for u in range(3):
                        if u == 1:
                            e.wait_ge(x_in[1], 16 * (NTT // 4))
                        transposes(NTT - 4 + u + 1, u + 1)
                        products(NTT - 4 + u, u % 2)
                    products(NTT - 1, 1)

        def attention_phase(c, attn_w, bq_c, bk_c, bo_b):
            (WQH, WQL), (WKH, WKL), (WVH, WVL), (WOH, WOL) = attn_w
            r, rs, one_r, neg_mr, neg_mrs = (lnw[:, i, :] for i in range(5))
            XN = sbt(c, "XN", [P, 2, D])
            XNH = sbt(c, "XNH", [P, KC, D], F32R)
            XNL = sbt(c, "XNL", [P, KC, D], F32R)
            QS = sbt(c, "QS", [P, 2, 3, KC, B * 2 * TL], BF16)
            KS = sbt(c, "KS", [P, KC * 2 * TL, 3, B], BF16)
            VS = sbt(c, "VS", [P, 4, 2 * NH, 3, DH], BF16)
            PS = sbt(c, "PS", [P, 3, B * 2 * NH], BF16)
            RQ = sbt(c, "RQ", [P, 2 * D])
            RK = sbt(c, "RK", [P, 2 * D])
            RV = sbt(c, "RV", [P, 2 * D])
            RP = sbt(c, "RP", [P, 2 * D])
            QBD = sbt(c, "QBD", [P, 3, KC, HC, B * 2 * TL], BF16)
            PX = sbt(c, "PX", [P, 3, TL, B * 2 * NH], BF16)
            SB = sbt(c, "SB", [P, 2 * KC * TL, B])
            SD = sbt(c, "SD", [P, 2 * KC * TL, B])
            EX = sbt(c, "EX", [P, 2 * KC * TL, B])
            PN = sbt(c, "PN", [P, 2 * KC * TL, B])
            MX = sbt(c, "MX", [P, 2 * KC * TL])
            SM = sbt(c, "SM", [P, 2 * KC * TL])
            RC = sbt(c, "RC", [P, 2 * KC * TL])
            OB = sbt(c, "OB", [P, 2 * NH, DH])
            OTH = sbt(c, "OTH", [P, KC * 2, B, TL], F32R)
            OTL = sbt(c, "OTL", [P, KC * 2, B, TL], F32R)
            T1 = sbt(c, "T1", [P, 2, D])
            T2 = sbt(c, "T2", [P, 2, D])
            tmp = T1[:, :, 0:NT]
            bank = [pst(c, f"bank{i}", [P, 512]) for i in range(8)]
            XTV, S0, S1, QOT, KB, O0, O1, WB = bank
            SBK, OBK = (S0, S1), (O0, O1, S1, O0)
            S = {n: sem(n) for n in (
                "ln_sqrt", "ln_chain", "ln_done", "zeroed", "xn_made", "xn_transposed", "xn_hi", "xn_lo",
                "q_made", "k_made", "v_made", "q1", "q2", "q3", "q_rest", "k1", "k2", "k3", "k_rest",
                "v1", "v2", "v3", "v_rest", "s_made", "s_summed", "max_made", "shifted", "exp_made", "sum_made",
                "recip_made", "p_made", "p_transposed", "p1", "p2", "p3", "p_rest", "o_made", "o_summed",
                "o_transposed", "o_hi", "o_lo", "wo_made", "res_scaled", "res_bias", "h_updated", "attn_stats",
                "q_spread", "p_spread")}

            def perm(ap):
                return ap.rearrange("p (g t b) -> p g b t", g=2 * KC, t=TL)

            def swapped(ap, n):
                return ap.rearrange("p (b t) -> p t b", b=n)

            def as_made(ap):
                return ap[:, :].rearrange("p (g b t) -> p g b t", g=2 * KC, t=TL)

            class Step:
                def __init__(self, i, at):
                    self.i = i
                    self.q = (at + 1) % 2, at % 2
                    self.v = (at + 1) % 4, (at - 1) % 4
                    self.xn, self.xt, self.nxt, self.cur, self.prv, self.old = (0 <= at + d < NI for d in (3, 2, 1, 0, -1, -2))

            def steps(e, body):
                for i in range(-1, 4):
                    body(Step(i, i))
                with e.Fori(1, NI // 4 - 1) as n:
                    for u in range(4):
                        body(Step(n * 4 + u, 4 + u))
                for i in range(NI - 4, NI + 2):
                    body(Step(i, i))

            with nc.Block() as block:
                @block.sync
                def _(e):
                    e.wait_ge(S["zeroed"], 2)

                    def body(st_):
                        i = st_.i
                        if st_.prv:
                            after(e, S["p3"], i - 1)
                            after(e, S["o_made"], i - 2, 4)
                            for t in range(TL):
                                rows = slice(t * B, (t + 1) * B)
                                e.dma_start(PX[rows, :, t, :], PS[rows, :, :]).then_inc(S["p_spread"], 16)
                        if st_.nxt:
                            after(e, S["q3"], i + 1)
                            after(e, S["s_made"], i, 4)
                            for h in range(HC):
                                rows = slice(h * DH, (h + 1) * DH)
                                e.dma_start(QBD[rows, :, :, h, :], QS[rows, st_.q[0], :, :, :]).then_inc(S["q_spread"], 16)
                            e.dma_start(slots_v[bass.ds(i + 1, 1)].rearrange("g p t r -> p (g t) r"),
                                        fill[:, :].unsqueeze(1).broadcast_to([P, BT, ROW])).then_inc(slots_filled, 16)
                    steps(e, body)

                @block.gpsimd
                def _(e):
                    e.memset(PX[:, :, :, :].rearrange("p a t c -> p (a t c)").bitcast(F32), 0.0).then_inc(S["zeroed"], 1)

                    def third(name, dst, rest, i, src2):
                        after(e, S[name + "_rest"], i, 2 if name in "qk" else 1)
                        after(e, S[name + "2"], i)
                        e.tensor_tensor(dst, rest, src2, ALU.subtract).then_inc(S[name + "3"], 1)

                    def body(st_):
                        i = st_.i
                        if st_.prv:
                            third("p", PS[:, 2, :], RP[:, :], i - 1, PS[:, 1, :])
                        if st_.nxt:
                            third("q", QS[:, st_.q[0], 2, :, :].rearrange("p c n -> p (c n)"), RQ[:, :], i + 1,
                                  QS[:, st_.q[0], 1, :, :].rearrange("p c n -> p (c n)"))
                        if st_.old:
                            after(e, S["h_updated"], i - 3)
                            after(e, S["res_scaled"], i - 2)
                            e.tensor_tensor(T2[:, :, :], T1[:, :, :], bo_b[:, :].unsqueeze(1).broadcast_to([P, 2, D]),
                                            ALU.add).then_inc(S["res_bias"], 1)
                        if st_.cur:
                            after(e, S["exp_made"], i - 1)
                            after(e, S["max_made"], i)
                            e.tensor_tensor(SD[:, :, :], SB[:, :, :],
                                            MX[:, :].unsqueeze(2).broadcast_to([P, 2 * KC * TL, B]),
                                            ALU.subtract).then_inc(S["shifted"], 1)
                            after(e, S["p_transposed"], i - 1)
                            after(e, S["recip_made"], i)
                            e.tensor_tensor(PN[:, :, :], EX[:, :, :],
                                            RC[:, :].unsqueeze(2).broadcast_to([P, 2 * KC * TL, B]),
                                            ALU.mult).then_inc(S["p_made"], 1)
                        if st_.nxt:
                            third("k", KS[:, :, 2, :], RK[:, :].rearrange("p (g b) -> p g b", b=B), i + 1, KS[:, :, 1, :])
                            v = st_.v[0]
                            third("v", VS[:, v, :, 2, :], RV[:, :].rearrange("p (g d) -> p g d", d=DH), i + 1,
                                  VS[:, v, :, 1, :])
                    steps(e, body)

                @block.scalar
                def _(e):
                    e.wait_ge(S["ln_chain"], 8)
                    e.activation(r, tmp[:, 0, :], ACT.Sqrt).then_inc(S["ln_sqrt"], 1)
                    e.wait_ge(S["ln_chain"], 16)
                    e.activation(rs, tmp[:, 0, :], ACT.Sqrt).then_inc(S["ln_sqrt"], 1)

                    def xn(i):
                        for j in range(2):
                            T = i * 2 + j
                            e.activation(XN[:, j, :], H[:, T, :], ACT.Identity, scale=lnw[:, 1, bass.ds(T, 1)],
                                         bias=lnw[:, 4, bass.ds(T, 1)]).then_inc(S["xn_made"], 1)

                    def xn_hi(i):
                        after(e, S["v_made"], i - 1)
                        after(e, S["xn_transposed"], i)
                        e.activation(perm(XNH[:, :, :].rearrange("p c n -> p (c n)")), as_made(XTV), ACT.Copy).then_inc(S["xn_hi"], 1)

                    e.wait_ge(S["ln_done"], 1)
                    xn(0)
                    xn_hi(0)
                    xn(1)

                    def body(st_):
                        i = st_.i
                        v = st_.v[0]
                        if st_.prv:
                            after(e, S["p_spread"], i - 2, 16 * TL)
                            after(e, S["p_transposed"], i - 1)
                            e.activation(swapped(PS[:, 0, :], B), S0[:, :].rearrange("p (h b) -> p h b", b=B), ACT.Copy).then_inc(S["p1"], 1)
                        if st_.old:
                            after(e, S["wo_made"], i - 3)
                            after(e, S["o_transposed"], i - 2)
                            e.activation(OTH[:, :, :, :].rearrange("p g b t -> p g t b"),
                                         O1[:, :].rearrange("p (g t b) -> p g t b", g=4, t=TL), ACT.Copy).then_inc(S["o_hi"], 1)
                        if st_.prv:
                            after(e, S["p_rest"], i - 1)
                            e.activation(PS[:, 1, :], RP[:, :], ACT.Copy).then_inc(S["p2"], 1)
                        if st_.nxt:
                            after(e, S["q_spread"], i - 1, 16 * HC)
                            after(e, S["q_made"], i + 1)
                            for c_ in range(KC):
                                e.activation(swapped(QS[:, st_.q[0], 0, c_, :], B),
                                             QOT[:, c_ * D:(c_ + 1) * D].rearrange("p (t b) -> p t b", b=B),
                                             ACT.Identity, bias=bq_c[:, c_:c_ + 1]).then_inc(S["q1"], 1)
                            if st_.old:
                                after(e, S["res_bias"], i - 3)
                            after(e, S["q_rest"], i + 1, 2)
                            e.activation(QS[:, st_.q[0], 1, :, :].rearrange("p c n -> p (c n)"), RQ[:, :], ACT.Copy).then_inc(S["q2"], 1)
                        if st_.old:
                            if not st_.nxt:
                                after(e, S["res_bias"], i - 3)
                            for j in range(2):
                                T = i * 2 + (j - 4)
                                m = e.activation(T1[:, j, :], H[:, T, :], ACT.Identity, scale=lnw[:, 2, bass.ds(T, 1)],
                                                 bias=lnw[:, 3, bass.ds(T, 1)])
                            m.then_inc(S["res_scaled"], 1)
                        if st_.nxt:
                            after(e, S["s_made"], i, 4)
                            after(e, S["k_made"], i + 1)
                            for c_ in range(KC):
                                e.activation(KS[:, c_ * 2 * TL:(c_ + 1) * 2 * TL, 0, :],
                                             KB[:, c_ * D:(c_ + 1) * D].rearrange("p (g b) -> p g b", b=B),
                                             ACT.Identity, bias=bk_c[:, c_:c_ + 1]).then_inc(S["k1"], 1)
                            after(e, S["o_made"], i - 3, 4)
                            after(e, S["v_made"], i + 1)
                            e.activation(VS[:, v, :, 0, :], XTV[:, :].rearrange("p (g d) -> p g d", d=DH),
                                         ACT.Copy).then_inc(S["v1"], 1)
                        if st_.cur:
                            after(e, S["p_made"], i - 1)
                            after(e, S["sum_made"], i - 1)
                            after(e, S["shifted"], i)
                            e.activation(EX[:, :, :], SD[:, :, :], ACT.Exp, scale=SCALE).then_inc(S["exp_made"], 1)
                        if st_.xt:
                            xn_hi(i + 2)
                        if st_.nxt:
                            after(e, S["k_rest"], i + 1, 2)
                            e.activation(KS[:, :, 1, :], RK[:, :].rearrange("p (g b) -> p g b", b=B), ACT.Copy).then_inc(S["k2"], 1)
                            after(e, S["v_rest"], i + 1)
                            e.activation(VS[:, v, :, 1, :], RV[:, :].rearrange("p (g d) -> p g d", d=DH),
                                         ACT.Copy).then_inc(S["v2"], 1)
                        if st_.xn:
                            xn(i + 3)
                    steps(e, body)

                @block.vector
                def _(e):
                    chained = [0]

                    def link(ins):
                        chained[0] += 1
                        ins.then_inc(S["ln_chain"], 1)
                        e.wait_ge(S["ln_chain"], chained[0])

                    v, t = tmp[:, 0, :], tmp[:, 1, :]
                    mean, var = st[:, 0, :], st[:, 1, :]
                    whole_stats(link, e, st, halves, t)
                    link(e.tensor_scalar(v, var, EPS, None, ALU.add))
                    e.wait_ge(S["ln_sqrt"], 1)
                    link(e.reciprocal(r, r))
                    one_newton_step(link, e, v, r, t)
                    link(e.tensor_tensor(t, r, r, ALU.mult))
                    link(e.tensor_tensor(v, t, var, ALU.mult))
                    link(e.tensor_scalar(v, v, EPS, None, ALU.add))
                    assert chained[0] == 16
                    e.wait_ge(S["ln_sqrt"], 2)
                    link(e.reciprocal(rs, rs))
                    one_newton_step(link, e, v, rs, t)
                    link(e.tensor_tensor(rs, rs, r, ALU.mult))
                    link(e.tensor_scalar(t, mean, -1.0, None, ALU.mult))
                    link(e.tensor_scalar(one_r, r, 1.0, None, ALU.add))
                    link(e.tensor_tensor(neg_mr, t, r, ALU.mult))
                    e.tensor_tensor(neg_mrs, t, rs, ALU.mult).then_inc(S["ln_done"], 1)
                    e.memset(QBD[:, :, :, :, :].rearrange("p a c h n -> p (a c h n)").bitcast(F32), 0.0).then_inc(S["zeroed"], 1)

                    def xn_lo(i):
                        after(e, S["xn_hi"], i)
                        e.tensor_tensor(perm(XNL[:, :, :].rearrange("p c n -> p (c n)")), as_made(XTV),
                                        perm(XNH[:, :, :].rearrange("p c n -> p (c n)").bitcast(F32)),
                                        ALU.subtract).then_inc(S["xn_lo"], 1)

                    def sum_of_three(name, made, bank_, dst, i, s_):
                        after(e, S[made], i, 4, s_ + 1)
                        e.tensor_reduce(dst, bank_[:, 0:TL * 3 * B].rearrange("p (g a b) -> p g b a", a=3, b=B),
                                        AX, ALU.add).then_inc(S[name], 1)

                    def o_sum(i, s_):
                        sum_of_three("o_summed", "o_made", OBK[s_], OB[:, s_ * HC:(s_ + 1) * HC, :], i, s_)

                    def stats(i):
                        for j in range(2):
                            e.bn_stats(halves[:, i * 2 + j, :], H[:, i * 2 + j, :]).then_inc(S["attn_stats"], 1)

                    xn_lo(0)

                    def body(st_):
                        i = st_.i
                        if st_.prv:
                            after(e, S["p3"], i - 2)
                            after(e, S["p1"], i - 1)
                            e.tensor_tensor(swapped(RP[:, :], B), S0[:, :].rearrange("p (h b) -> p h b", b=B),
                                            swapped(PS[:, 0, :], B), ALU.subtract).then_inc(S["p_rest"], 1)
                        if st_.old:
                            after(e, S["o_hi"], i - 2)
                            e.tensor_tensor(OTL[:, :, :, :].rearrange("p g b t -> p g t b"),
                                            O1[:, :].rearrange("p (g t b) -> p g t b", g=4, t=TL),
                                            OTH[:, :, :, :].rearrange("p g b t -> p g t b").bitcast(F32),
                                            ALU.subtract).then_inc(S["o_lo"], 1)
                        if st_.nxt:
                            after(e, S["q3"], i)
                            for c_ in range(KC):
                                after(e, S["q1"], i + 1, 2)
                                e.scalar_tensor_tensor(out=swapped(RQ[:, c_ * D:(c_ + 1) * D], B),
                                                       in0=QOT[:, c_ * D:(c_ + 1) * D].rearrange("p (t b) -> p t b", b=B),
                                                       scalar=bq_c[:, c_:c_ + 1], in1=swapped(QS[:, st_.q[0], 0, c_, :], B),
                                                       op0=ALU.add, op1=ALU.subtract).then_inc(S["q_rest"], 1)
                        if st_.cur:
                            after(e, S["shifted"], i - 1)
                            for s_ in range(4):
                                g = (s_ % 2) * 2 * TL + (s_ // 2) * TL
                                sum_of_three("s_summed", "s_made", SBK[s_ % 2], SB[:, g:g + TL, :], i, s_)
                            after(e, S["s_summed"], i, 4)
                            e.tensor_reduce(MX[:, :], SB[:, :, :], AX, ALU.max).then_inc(S["max_made"], 1)
                        if st_.nxt:
                            after(e, S["k3"], i)
                            for c_ in range(KC):
                                after(e, S["k1"], i + 1, 2)
                                e.scalar_tensor_tensor(out=RK[:, c_ * D:(c_ + 1) * D].rearrange("p (g b) -> p g b", b=B),
                                                       in0=KB[:, c_ * D:(c_ + 1) * D].rearrange("p (g b) -> p g b", b=B),
                                                       scalar=bk_c[:, c_:c_ + 1],
                                                       in1=KS[:, c_ * 2 * TL:(c_ + 1) * 2 * TL, 0, :],
                                                       op0=ALU.add, op1=ALU.subtract).then_inc(S["k_rest"], 1)
                            after(e, S["v3"], i)
                            after(e, S["v1"], i + 1)
                            e.tensor_tensor(RV[:, :].rearrange("p (g d) -> p g d", d=DH), XTV[:, :].rearrange("p (g d) -> p g d", d=DH),
                                            VS[:, st_.v[0], :, 0, :], ALU.subtract).then_inc(S["v_rest"], 1)
                        if st_.old:
                            after(e, S["res_bias"], i - 2)
                            after(e, S["wo_made"], i - 2)
                            e.tensor_tensor(H[:, bass.ds(i * 2 - 4, 2), :], WB[:, :].rearrange("p (j n) -> p j n", j=2),
                                            T2[:, :, :], ALU.add).then_inc(S["h_updated"], 1)
                        if st_.cur:
                            after(e, S["exp_made"], i)
                            e.tensor_reduce(SM[:, :], EX[:, :, :], AX, ALU.add).then_inc(S["sum_made"], 1)
                            after(e, S["p_made"], i - 1)
                            after(e, S["sum_made"], i)
                            e.reciprocal(RC[:, :], SM[:, :]).then_inc(S["recip_made"], 1)
                        if st_.xt:
                            xn_lo(i + 2)
                        if st_.prv:
                            after(e, S["o_transposed"], i - 2)
                            for s_ in range(4):
                                if s_ == 3 and st_.old:
                                    after(e, S["h_updated"], i - 2)
                                o_sum(i - 1, s_)
                        if st_.old:
                            if not st_.prv:
                                after(e, S["h_updated"], i - 2)
                            stats(i - 2)
                    steps(e, body)
                    e.wait_ge(S["attn_stats"], NT)

                @block.tensor
                def _(e):
                    def project(dst, wh, wl, wait=None):
                        for c_ in range(KC):
                            n_ = 0
                            for k in range(KC):
                                for w, a in ((wh, XNH), (wl, XNH), (wh, XNL)):
                                    m = e.matmul(dst[:, c_ * D:(c_ + 1) * D], w[:, k, c_ * P:(c_ + 1) * P], a[:, k, :],
                                                 start=(n_ == 0), stop=(n_ == 3 * KC - 1))
                                    n_ += 1
                        return m

                    def tokens_by_features(dst, ah, al, wh, wl):
                        for j in range(2):
                            n_ = 0
                            for k in range(KC):
                                for a, w in ((ah, wh), (ah, wl), (al, wh)):
                                    m = e.matmul(dst[:, j * D:(j + 1) * D], a(k, j), w[:, k, :],
                                                 start=(n_ == 0), stop=(n_ == 3 * KC - 1))
                                    n_ += 1
                        return m

                    def small_products(dst, stationary, moving):
                        for t in range(8):
                            for a in range(3):
                                m = e.matmul(dst[:, t * 48:t * 48 + 16 * (3 - a)], stationary(a, t), moving(t, 3 - a),
                                             start=(t == 0 and a == 0), stop=(t == 7 and a == 2), skip_group_check=True)
                        return m

                    def xn_transposes(i):
                        after(e, S["v_rest"], i - 1)
                        after(e, S["xn_made"], i, 2)
                        for c_ in range(KC):
                            for j in range(2):
                                m = e.transpose(XTV[:, c_ * D + j * P:c_ * D + (j + 1) * P], XN[:, j, c_ * P:(c_ + 1) * P],
                                                ident[:, :])
                        m.then_inc(S["xn_transposed"], 1)

                    xn_transposes(0)

                    def body(st_):
                        i = st_.i
                        if st_.nxt:
                            after(e, S["q_rest"], i, 2)
                            after(e, S["xn_lo"], i + 1)
                            project(QOT, WQH, WQL).then_inc(S["q_made"], 1)
                            after(e, S["k_rest"], i, 2)
                            project(KB, WKH, WKL).then_inc(S["k_made"], 1)
                        if st_.cur:
                            after(e, S["k3"], i)
                            after(e, S["p_rest"], i - 1)
                            after(e, S["q_spread"], i, 16 * HC)
                            for s_ in range(4):
                                j, c_ = s_ // 2, s_ % 2
                                after(e, S["s_summed"], i, 4, s_ - 1)
                                small_products(SBK[s_ % 2],
                                               lambda a, t: QBD[:, a, c_, :, :].rearrange("p h (b t) -> p (h b) t", b=B)[:, :, j * TL + t],
                                               lambda t, n: KS[:, c_ * 2 * TL + j * TL + t, 0:n, :]).then_inc(S["s_made"], 1)
                        if st_.nxt:
                            tokens_by_features(XTV, lambda k, j: XNH[:, k, j * P:(j + 1) * P],
                                               lambda k, j: XNL[:, k, j * P:(j + 1) * P], WVH, WVL).then_inc(S["v_made"], 1)
                        if st_.old:
                            after(e, S["h_updated"], i - 3)
                            after(e, S["o_lo"], i - 2)
                            tokens_by_features(WB, lambda k, j: OTH[:, k * 2 + j, :, :].rearrange("p b t -> p (b t)"),
                                               lambda k, j: OTL[:, k * 2 + j, :, :].rearrange("p b t -> p (b t)"),
                                               WOH, WOL).then_inc(S["wo_made"], 1)
                        if st_.xt:
                            xn_transposes(i + 2)
                        if st_.prv:
                            if st_.old:
                                after(e, S["o_lo"], i - 2)
                            after(e, S["v3"], i - 1)
                            after(e, S["p_spread"], i - 1, 16 * TL)
                            for s_ in range(4):
                                if s_ == 2 and st_.cur:
                                    after(e, S["s_summed"], i, 4)
                                if s_ == 3:
                                    after(e, S["o_summed"], i - 1, 4, 1)
                                small_products(OBK[s_],
                                               lambda a, t: PX[:, a, :, :].rearrange("p l (b h) -> p (l b) h", b=B)[:, :, s_ * HC + t],
                                               lambda t, n: VS[:, st_.v[1], s_ * HC + t, 0:n, :]).then_inc(S["o_made"], 1)
                        if st_.cur:
                            after(e, S["s_summed"], i, 4)
                            after(e, S["p_made"], i)
                            for j in range(2):
                                for c_ in range(KC):
                                    m = e.transpose(S0[:, j * D + c_ * P:j * D + (c_ + 1) * P],
                                                    PN[:, (c_ * 2 + j) * TL:(c_ * 2 + j + 1) * TL, :].rearrange("p t b -> p (t b)"),
                                                    ident[:, :])
                            m.then_inc(S["p_transposed"], 1)
                        if st_.prv:
                            after(e, S["o_summed"], i - 1, 4)
                            for c_ in range(KC):
                                for j in range(2):
                                    m = e.transpose(O1[:, c_ * D + j * P:c_ * D + (j + 1) * P],
                                                    OB[:, j * NH + c_ * HC:j * NH + (c_ + 1) * HC, :].rearrange("p h d -> p (h d)"),
                                                    ident[:, :])
                            m.then_inc(S["o_transposed"], 1)
                    steps(e, body)

        weights_in, w_split, w_rounded, b1_ready = sem("weights_in"), sem("w_split"), sem("w_rounded"), sem("b1_ready")
        w1_v = w1.rearrange("e (c p) f -> e p c f", p=P)
        w2_v = w2.rearrange("e (c p) f -> e p c f", p=P)
        PIECES = 4

        def weight_slot(c, W1, W2):
            s = len(W1)
            W1.append((sbt(c, f"w1_hi{s}", [P, KC, FF], F32R), sbt(c, f"w1_lo{s}", [P, KC, FF], F32R)))
            W2.append((sbt(c, f"w2_hi{s}", [P, FC, D], F32R), sbt(c, f"w2_lo{s}", [P, FC, D], F32R)))

        def weight_buffers(c):
            stages = sbt(c, "stage1", [P, KC, FF]), sbt(c, "stage2", [P, FC, D])
            W1, W2 = [], []
            weight_slot(c, W1, W2)
            b1_e = sbt(c, "b1_e", [P, 2, FC])

            def load_weights(e, ex):
                e.dma_start(stages[0][:, :, :], w1_v[ex]).then_inc(weights_in, 16)
                e.dma_start(stages[1][:, :, :], w2_v[ex]).then_inc(weights_in, 16)

            def split_piece(e, k, s, total):
                w, kk = k // KC, k % KC
                rows = slice(kk, kk + 1) if w == 0 else slice(kk * FC // KC, (kk + 1) * FC // KC)
                a, h_, l_ = (t[:, rows, :] for t in (stages[w], *(W1, W2)[w][s]))
                e.tensor_copy(h_, a).then_inc(w_rounded, 1)
                e.wait_ge(w_rounded, total)
                e.tensor_tensor(l_, a, h_.bitcast(F32), ALU.subtract).then_inc(w_split, 1)

            def expert_b1(e, ex, s):
                e.tensor_copy(b1_e[:, s, :], b1_t[:, bass.ds(ex * FC, FC)]).then_inc(b1_ready, 1)

            return W1, W2, b1_e, load_weights, split_piece, expert_b1

        def router_phase(c, load_weights, split_piece, expert_b1):
            r3 = lnw[:, 0, :]
            v3 = sbt(c, "v3", [P, NT])
            t3 = sbt(c, "t3", [P, NT])
            X3 = sbt(c, "X3", [P, 2, RT, D])
            X3H = sbt(c, "X3H", [P, 2, KC, RT * P], F32R)
            X3L = sbt(c, "X3L", [P, 2, KC, RT * P], F32R)
            wr_hi = sbt(c, "wr_hi", [P, KC, NE], F32R)
            wr_lo = sbt(c, "wr_lo", [P, KC, NE], F32R)
            LGT = sbt(c, "LGT", [NE, 2, RT * P])
            LG = sbt(c, "LG", [P, NT, NE])
            LS = sbt(c, "LS", [P, NT, NE])
            OHT = sbt(c, "OHT", [P, NE, NT])
            CS = sbt(c, "CS", [P, NE, NT])
            go_on = sbt(c, "go_on", [P, NE, NT])
            iota8 = sbt(c, "iota8", [P, NE])
            n_first = sbt(c, "n_first", [P, 2, 2, NE])
            offs = sbt(c, "offs", [P, 2, NE])
            meta = sbt(c, "meta", [P, NT, 4])
            mx = sbt(c, "mx", [P, NT])
            idx = sbt(c, "idx", [P, NT])
            rank = sbt(c, "rank", [P, NT])
            kept = sbt(c, "kept", [P, NT])
            slot_i = sbt(c, "slot_i", [P, NT], I32)
            part_i = sbt(c, "part_i", [P, 2], I32)
            batch_f = sbt(c, "batch_f", [P, 2])
            before = sbt(c, "before", [P, 3, P])
            R = sbt(c, "R", [P, 2, RT, ROW])
            RI = sbt(c, "RI", [P, 2, RT], I32)
            TP = [pst(c, f"x3_bank{i}", [P, KC, 512]) for i in range(2)]
            LP = [pst(c, f"logit_bank{i}", [P, RT, NE]) for i in range(2)]
            LTP = [pst(c, f"logit_t_bank{i}", [P, 512]) for i in range(2)]
            OP = LP[0]
            S = {n: sem(n) for n in ("r3_sqrt", "r3_chain", "x3_made", "x3_transposed", "x3_hi", "x3_lo", "logits_made",
                                     "logits_t_copied", "logits_turned", "logits_copied", "wr_split", "route_chain", "consts_made", "exp_route", "offsets_made",
                                     "rows_made", "row_gate")}
            rows_sent = [sem("rows_sent0"), sem("rows_sent1")]

            def rounds(body):
                def run(q, at):
                    body(q, at % 2, lambda d: 0 <= at + d < NR)
                return run

            def all_rounds(e, body):
                run = rounds(body)
                for q in range(-1, 4):
                    run(q, q)
                with e.Fori(2, NR // 2 - 1) as n:
                    for u in range(2):
                        run(n * 2 + u, 4 + u)
                for q in range(NR - 2, NR + 1):
                    run(q, q)

            with nc.Block() as block:
                @block.sync
                def _(e):
                    load_weights(e, 0)
                    for b in range(B):
                        rows = slice(b * TL, (b + 1) * TL)
                        e.dma_start(out[b, 0:TT, :].rearrange("(l t) f -> l t f", l=TL), H[rows, 0:NTT, :]).then_inc(default_out, 16)
                        e.dma_start(out[b, TT:, :].rearrange("(l t) f -> l t f", l=TL), H[rows, NTT:, :]).then_inc(default_out, 16)
                    e.wait_ge(default_out, 16 * 2 * B)

                @block.gpsimd
                def _(e):
                    n_ = [0]

                    def link(ins):
                        n_[0] += 1
                        ins.then_inc(S["consts_made"], 1)
                        e.wait_ge(S["consts_made"], n_[0])

                    link(e.memset(before[:, :, :], 1.0))
                    b3 = [before[:, i, :] for i in range(3)]
                    link(e.affine_select(out=b3[0], in_=b3[0], compare_op=ALU.is_gt, fill=0.0, base=0,
                                         pattern=[[1, P]], channel_multiplier=-1))
                    for i, base in ((1, 0), (2, TL)):
                        link(e.affine_select(out=b3[i], in_=b3[i], compare_op=ALU.is_gt, fill=0.0, base=base,
                                             pattern=[[TL, B], [0, TL]], channel_multiplier=-1))
                    link(e.iota(iota8[:, :], [[1, NE]], base=0, channel_multiplier=0, allow_small_or_imprecise_dtypes=True))
                    link(e.memset(go_on[:, :, :], 1.0))
                    link(e.memset(go_on[:, :, 0:1], 0.0))
                    link(e.memset(go_on[:, :, NTT:NTT + 1], 0.0))
                    link(e.iota(part_i[:, 0:1], [[0, 1]], base=0, channel_multiplier=1))
                    link(e.iota(mx[:, 0:NTT], [[1, NTT]], base=0, channel_multiplier=NTT, allow_small_or_imprecise_dtypes=True))
                    link(e.iota(mx[:, NTT:], [[1, NTX]], base=TT, channel_multiplier=NTX, allow_small_or_imprecise_dtypes=True))
                    e.wait_ge(slots_filled, 16 * NI)

                    def send(n, par):
                        after(e, S["rows_made"], n, 3)
                        gate(e, S["row_gate"], par)
                        for j in range(RT):
                            e.indirect_dma_start(slots, bass.IndirectOffsetOnAxis(ap=RI[:, par, j:j + 1], axis=0),
                                                 R[:, par, j, :], None, bounds_check=NE * CAP - 1, oob_is_err=False
                                                 ).then_inc(rows_sent[par], 16)
                    with e.Fori(0, NR // 2) as n:
                        for u in range(2):
                            send(n * 2 + u, u)
                    for par in range(2):
                        e.wait_ge(rows_sent[par], 16 * NT // 2)

                @block.scalar
                def _(e):
                    e.wait_ge(S["r3_chain"], 8)
                    e.activation(r3, v3[:, :], ACT.Sqrt).then_inc(S["r3_sqrt"], 1)

                    def body(q, par, of):
                        if of(1):
                            after(e, S["logits_made"], q - 1)
                            after(e, S["x3_transposed"], q + 1)
                            e.activation(X3H[:, 1 - par, :, :], TP[1 - par][:, :, :], ACT.Copy).then_inc(S["x3_hi"], 1)
                        if of(0):
                            after(e, S["logits_turned"], q - 2)
                            after(e, S["logits_made"], q)
                            e.activation(LGT[:, par, :], LTP[par][0:NE, :], ACT.Copy).then_inc(S["logits_t_copied"], 1)
                    all_rounds(e, body)
                    e.wait_ge(S["exp_route"], 1)
                    e.activation(LS[:, :, :], LS[:, :, :], ACT.Exp).then_inc(S["exp_route"], 1)

                @block.vector
                def _(e):
                    n3 = [0]

                    def link3(ins):
                        n3[0] += 1
                        ins.then_inc(S["r3_chain"], 1)
                        e.wait_ge(S["r3_chain"], n3[0])

                    whole_stats(link3, e, st, halves, t3[:, :])
                    link3(e.tensor_scalar(v3[:, :], st[:, 1, :], EPS, None, ALU.add))
                    e.wait_ge(S["r3_sqrt"], 1)
                    link3(e.reciprocal(r3, r3))
                    one_newton_step(link3, e, v3[:, :], r3, t3[:, :])

                    def x3(q, par):
                        after(e, S["x3_transposed"], q - 2)
                        for j in range(RT):
                            T = q * RT + j
                            m = e.tensor_scalar(X3[:, par, j, :], H[:, T, :], st[:, 0, bass.ds(T, 1)], lnw[:, 0, bass.ds(T, 1)],
                                                ALU.subtract, ALU.mult)
                        m.then_inc(S["x3_made"], 1)

                    e.tensor_copy(wr_hi[:, :, :], wr_t[:, :, :]).then_inc(S["wr_split"], 1)
                    e.wait_ge(S["wr_split"], 1)
                    e.tensor_tensor(wr_lo[:, :, :], wr_t[:, :, :], wr_hi[:, :, :].bitcast(F32), ALU.subtract).then_inc(S["wr_split"], 1)
                    x3(0, 0)

                    def body(q, par, of):
                        if of(2):
                            x3(q + 2, par)
                        if of(1):
                            after(e, S["logits_made"], q - 1)
                            after(e, S["x3_hi"], q + 1)
                            e.tensor_tensor(X3L[:, 1 - par, :, :], TP[1 - par][:, :, :], X3H[:, 1 - par, :, :].bitcast(F32),
                                            ALU.subtract).then_inc(S["x3_lo"], 1)
                        if of(-1):
                            after(e, S["logits_turned"], q - 1)
                            e.tensor_copy(LG[:, bass.ds(q * RT - RT, RT), :], LP[1 - par][:, :, :]).then_inc(S["logits_copied"], 1)
                    all_rounds(e, body)
                    e.wait_ge(S["logits_copied"], NR)
                    n_ = [0]

                    def link(ins):
                        n_[0] += 1
                        ins.then_inc(S["route_chain"], 1)
                        e.wait_ge(S["route_chain"], n_[0])

                    e.wait_ge(S["consts_made"], 11)
                    link(e.tensor_scalar(part_i[:, 1:2], part_i[:, 0:1], TL.bit_length() - 1, None, ALU.logical_shift_right))
                    link(e.tensor_copy(batch_f[:, 0:1], part_i[:, 1:2]))
                    link(e.tensor_scalar(batch_f[:, 1:2], batch_f[:, 0:1], float(TT + TX - TL * NTX), None, ALU.mult))
                    link(e.tensor_scalar(batch_f[:, 0:1], batch_f[:, 0:1], float(TT + TX - TL * NTT), None, ALU.mult))
                    for s, seg in enumerate((slice(0, NTT), slice(NTT, NT))):
                        link(e.tensor_scalar(meta[:, seg, 3], mx[:, seg], batch_f[:, s:s + 1], None, ALU.add))
                    link(e.tensor_reduce(mx[:, :], LG[:, :, :], AX, ALU.max))
                    mxb = mx[:, :].unsqueeze(2).broadcast_to([P, NT, NE])
                    link(e.tensor_tensor(LS[:, :, :], LG[:, :, :], mxb, ALU.subtract))
                    e.tensor_tensor(LG[:, :, :], LG[:, :, :], mxb, ALU.is_equal).then_inc(S["exp_route"], 1)
                    e.wait_ge(S["exp_route"], 2)
                    link(e.tensor_reduce(rank[:, :], LS[:, :, :], AX, ALU.add))
                    link(e.reciprocal(meta[:, :, 2], rank[:, :]))
                    iob = iota8[:, :].unsqueeze(1).broadcast_to([P, NT, NE])
                    link(e.tensor_scalar(LG[:, :, :], LG[:, :, :], -float(NE), float(NE), ALU.mult, ALU.add))
                    link(e.tensor_tensor(LG[:, :, :], LG[:, :, :], iob, ALU.add))
                    link(e.tensor_reduce(idx[:, :], LG[:, :, :], AX, ALU.min))
                    link(e.tensor_tensor(OHT[:, :, :].rearrange("p e t -> p t e"), iob,
                                         idx[:, :].unsqueeze(2).broadcast_to([P, NT, NE]), ALU.is_equal))
                    link(e.tensor_tensor_scan(CS[:, :, :].rearrange("p e t -> p (e t)"), go_on[:, :, :].rearrange("p e t -> p (e t)"),
                                              OHT[:, :, :].rearrange("p e t -> p (e t)"), 0.0, ALU.mult, ALU.add))
                    e.wait_ge(S["offsets_made"], 1)
                    link(e.tensor_copy(offs[:, :, :], OP[:, 0:2, :]))
                    for s, (a, b_) in enumerate(((0, NTT), (NTT, NT))):
                        link(e.tensor_tensor(CS[:, :, a:b_], CS[:, :, a:b_],
                                             offs[:, s, :].unsqueeze(2).broadcast_to([P, NE, b_ - a]), ALU.add))
                    link(e.tensor_tensor(CS[:, :, :], CS[:, :, :], OHT[:, :, :], ALU.mult))
                    link(e.tensor_reduce(rank[:, :], CS[:, :, :].rearrange("p e t -> p t e"), AX, ALU.add))
                    link(e.tensor_scalar(kept[:, :], rank[:, :], float(CAP), NOWHERE, ALU.is_gt, ALU.mult))
                    link(e.tensor_scalar(idx[:, :], idx[:, :], float(CAP), -1.0, ALU.mult, ALU.add))
                    link(e.tensor_tensor(idx[:, :], idx[:, :], rank[:, :], ALU.add))
                    link(e.tensor_tensor(idx[:, :], idx[:, :], kept[:, :], ALU.add))
                    link(e.tensor_copy(slot_i[:, :], idx[:, :]))
                    link(e.tensor_copy(meta[:, :, 0], st[:, 0, :]))
                    link(e.tensor_copy(meta[:, :, 1], r3))

                    def rows(n, par):
                        e.tensor_copy(R[:, par, :, 0:D], H[:, bass.ds(n * RT, RT), :]).then_inc(S["rows_made"], 1)
                        e.tensor_copy(R[:, par, :, D:], meta[:, bass.ds(n * RT, RT), :]).then_inc(S["rows_made"], 1)
                        e.tensor_copy(RI[:, par, :], slot_i[:, bass.ds(n * RT, RT)]).then_inc(S["rows_made"], 1)
                    rows(0, 0)
                    rows(1, 1)
                    with e.Fori(1, NR // 2) as n:
                        for u in range(2):
                            after(e, S["row_gate"], n * 2 + (u - 2))
                            e.wait_ge(rows_sent[u], n * (16 * RT))
                            rows(n * 2 + u, u)
                    e.wait_ge(weights_in, 32)
                    for k in range(PIECES):
                        split_piece(e, k, 0, k + 1)
                    expert_b1(e, 0, 0)

                @block.tensor
                def _(e):
                    e.wait_ge(S["wr_split"], 2)

                    def body(q, par, of):
                        if of(1):
                            after(e, S["x3_lo"], q - 1)
                            after(e, S["x3_made"], q + 1)
                            for c_ in range(KC):
                                for j in range(RT):
                                    m = e.transpose(TP[1 - par][:, c_, j * P:(j + 1) * P], X3[:, 1 - par, j, c_ * P:(c_ + 1) * P],
                                                    ident[:, :])
                            m.then_inc(S["x3_transposed"], 1)
                        if of(0):
                            after(e, S["logits_t_copied"], q - 2)
                            after(e, S["x3_lo"], q)
                            n_ = 0
                            for k in range(KC):
                                for w, a in ((wr_hi, X3H), (wr_lo, X3H), (wr_hi, X3L)):
                                    m = e.matmul(LTP[par][0:NE, :], w[:, k, :], a[:, par, k, :],
                                                 start=(n_ == 0), stop=(n_ == 3 * KC - 1))
                                    n_ += 1
                            m.then_inc(S["logits_made"], 1)
                        if of(-1):
                            after(e, S["logits_copied"], q - 3)
                            after(e, S["logits_t_copied"], q - 1)
                            for j in range(RT):
                                m = e.matmul(LP[1 - par][:, j, :], LGT[:, 1 - par, j * P:(j + 1) * P], ident[0:NE, 0:NE],
                                             start=True, stop=True)
                            m.then_inc(S["logits_turned"], 1)
                    all_rounds(e, body)
                    e.wait_ge(S["route_chain"], 15)
                    tok, text = CS[:, :, NTT - 1], CS[:, :, NT - 1]
                    for s, (m_tok, m_text) in enumerate(((0, 1), (2, 0))):
                        e.matmul(OP[:, s, :], before[:, m_tok, :], tok, start=True, stop=False)
                        m = e.matmul(OP[:, s, :], before[:, m_text, :], text, start=False, stop=True)
                    m.then_inc(S["offsets_made"], 1)

        def experts_phase(c, W1, W2, b1_e, load_weights, split_piece, expert_b1):
            weight_slot(c, W1, W2)
            XE = H[:, 0:BT, :]
            Y1 = H[:, BT:2 * BT, :]
            Y = H[:, 2 * BT:4 * BT, :].rearrange("p (s t) d -> p s t d", s=2)
            b2_b = H[:, 4 * BT:4 * BT + NE, :]
            X = sbt(c, "X", [P, 2, BT, ROW])
            XEH = sbt(c, "XEH", [P, KC, BLK], F32R)
            XEL = sbt(c, "XEL", [P, KC, BLK], F32R)
            G = sbt(c, "G", [P, 2, BLK])
            GH = sbt(c, "GH", [P, FC, BLK], F32R)
            GL = sbt(c, "GL", [P, FC, BLK], F32R)
            YI = sbt(c, "YI", [P, 2, BT], I32)
            XP = [pst(c, f"xe_bank{i}", [P, 512]) for i in range(KC)]
            GP = [pst(c, f"hidden_bank{i}", [P, 512]) for i in range(2)]
            YP = [pst(c, f"y_bank{i}", [P, 512]) for i in range(2)]
            S = {n: sem(n) for n in ("b2_in", "xe_made", "xe_transposed", "xe_hi", "xe_lo", "hidden_made", "gelu_made",
                                     "g_split", "y_made", "y_added", "store_gate", "g_rounded", "y_biased")}
            x_rows_in = [sem("x_rows_in0"), sem("x_rows_in1")]
            stored = [sem("stored0"), sem("stored1")]

            def blocks(e, body):
                body(0, 0, 0)
                for u in range(1, 2 * NBE):
                    body(0, u, u)
                with e.Fori(1, NE // 2 - 1) as n:
                    for u in range(2 * NBE):
                        body(n, u, n * (2 * NBE) + u)
                for u in range(2 * NBE):
                    body(NE // 2 - 1, u, NB - 2 * NBE + u)

            with nc.Block() as block:
                @block.sync
                def _(e):
                    e.dma_start(b2_b[:, :, :], b2.unsqueeze(0).broadcast_to([P, NE, D])).then_inc(S["b2_in"], 16)

                    def rows(g, par):
                        e.dma_start(X[:, par, :, :], slots_v[g]).then_inc(x_rows_in[par], 16)

                    rows(0, 0)
                    e.wait_ge(w_split, PIECES)
                    load_weights(e, 1)

                    def body(n, u, g):
                        after(e, S["y_added"], g - 1, BT)
                        if not (isinstance(g, int) and g == NB - 1):
                            rows(g + 1, (u + 1) % 2)
                        if u % NBE == NBE - 1:
                            s = u // NBE
                            ex = n * 2 + s
                            if not (isinstance(ex, int) and (ex + 2 >= NE or ex < 0)):
                                e.wait_ge(w_split, (ex + 2) * PIECES)
                                load_weights(e, ex + 2)
                    blocks(e, body)

                @block.gpsimd
                def _(e):
                    def body(n, u, g):
                        for t in range(BT):
                            after(e, S["y_added"], g, BT, t + 1)
                            gate(e, S["store_gate"], u % 2, t)
                            e.indirect_dma_start(out_rows, bass.IndirectOffsetOnAxis(ap=YI[:, u % 2, t:t + 1], axis=0),
                                                 Y[:, u % 2, t, :], None, bounds_check=NTOK - 1, oob_is_err=False
                                                 ).then_inc(stored[u % 2], 16)
                    blocks(e, body)
                    for par in range(2):
                        e.wait_ge(stored[par], 16 * BT * NB // 2)

                @block.scalar
                def _(e):
                    def xe_hi(g):
                        after(e, S["xe_transposed"], g)
                        after(e, S["hidden_made"], g - 1, FC)
                        for c_ in range(KC):
                            e.activation(XEH[:, c_, :], XP[c_][:, 0:BLK], ACT.Copy).then_inc(S["xe_hi"], 1)

                    xe_hi(0)

                    def body(n, u, g):
                        s = u // NBE
                        if u % NBE == 0:
                            e.wait_ge(b1_ready, n * 2 + s + 1)
                        for f in range(FC):
                            after(e, S["hidden_made"], g, FC, f + 1)
                            after(e, S["g_split"], g, FC, f - 1)
                            e.activation(G[:, f % 2, :], GP[f % 2][:, 0:BLK], ACT.Gelu,
                                         bias=b1_e[:, s, f:f + 1]).then_inc(S["gelu_made"], 1)
                        if not (isinstance(g, int) and g == NB - 1):
                            xe_hi(g + 1)
                    blocks(e, body)

                @block.vector
                def _(e):
                    def xe(g, par, count):
                        e.wait_ge(x_rows_in[par], count)
                        after(e, S["xe_transposed"], g - 1)
                        for t in range(BT):
                            m = e.tensor_scalar(XE[:, t, :], X[:, par, t, 0:D], X[:, par, t, D:D + 1], X[:, par, t, D + 1:D + 2],
                                                ALU.subtract, ALU.mult)
                        m.then_inc(S["xe_made"], 1)

                    def xe_lo(g):
                        for c_ in range(KC):
                            after(e, S["xe_hi"], g, KC, c_ + 1)
                            e.tensor_tensor(XEL[:, c_, :], XP[c_][:, 0:BLK], XEH[:, c_, :].bitcast(F32),
                                            ALU.subtract).then_inc(S["xe_lo"], 1)

                    xe(0, 0, 16)
                    xe_lo(0)
                    e.wait_ge(S["b2_in"], 16)

                    def body(n, u, g):
                        par = u % 2
                        s = u // NBE
                        ex = n * 2 + s
                        end = isinstance(g, int) and g == NB - 1
                        after(e, S["y_made"], g - 1, BT)
                        for f in range(FC):
                            after(e, S["gelu_made"], g, FC, f + 1)
                            e.tensor_copy(GH[:, f, :], G[:, f % 2, :]).then_inc(S["g_rounded"], 1)
                            after(e, S["g_rounded"], g, FC, f + 1)
                            e.tensor_tensor(GL[:, f, :], G[:, f % 2, :], GH[:, f, :].bitcast(F32), ALU.subtract
                                            ).then_inc(S["g_split"], 1)
                            if f == FC // 2 and not end:
                                xe(g + 1, 1 - par, (n * NBE + ((u + 1) // 2 + 1)) * 16)
                        if u % NBE < PIECES and not (isinstance(ex, int) and ex == NE - 1):
                            e.wait_ge(weights_in, (ex + 2) * 32)
                            split_piece(e, u % NBE, 1 - s, ex * PIECES + (PIECES + u % NBE + 1))
                            if u % NBE == 0:
                                expert_b1(e, ex + 1, 1 - s)
                        if not end:
                            xe_lo(g + 1)
                        later_round = (n * NBE + u // 2) * (16 * BT)
                        for t in range(BT):
                            after(e, S["y_made"], g, BT, t + 1)
                            if t == 0 and not (isinstance(later_round, int) and later_round <= 0):
                                after(e, S["store_gate"], g - 2, BT)
                                e.wait_ge(stored[par], later_round)
                            e.tensor_tensor(Y1[:, t, :], YP[(BT * u + t) % 2][:, 0:D],
                                            b2_b[:, ex, :], ALU.add).then_inc(S["y_biased"], 1)
                            if t == 0:
                                e.tensor_copy(YI[:, par, :], X[:, par, :, D + 3]).then_inc(S["y_biased"], 1)
                            after(e, S["y_biased"], g, BT + 1, t + 2)
                            ins = e.scalar_tensor_tensor(out=Y[:, par, t, :], in0=Y1[:, t, :], scalar=X[:, par, t, D + 2:D + 3],
                                                         in1=X[:, par, t, 0:D], op0=ALU.mult, op1=ALU.add)
                            ins.then_inc(S["y_added"], 1)
                    blocks(e, body)

                @block.tensor
                def _(e):
                    def transposes(g):
                        after(e, S["xe_made"], g)
                        after(e, S["xe_lo"], g - 1, KC)
                        for c_ in range(KC):
                            for t in range(BT):
                                m = e.transpose(XP[c_][:, t * P:(t + 1) * P], XE[:, t, c_ * P:(c_ + 1) * P], ident[:, :])
                        m.then_inc(S["xe_transposed"], 1)

                    transposes(0)

                    def body(n, u, g):
                        s = u // NBE
                        ex = n * 2 + s
                        if u % NBE == 0:
                            e.wait_ge(w_split, (ex + 1) * PIECES)
                        after(e, S["xe_lo"], g, KC)
                        for f in range(FC):
                            after(e, S["gelu_made"], g, FC, f - 1)
                            n_ = 0
                            for k in range(KC):
                                for w, a in ((W1[s][0], XEH), (W1[s][1], XEH), (W1[s][0], XEL)):
                                    m = e.matmul(GP[f % 2][:, 0:BLK], w[:, k, f * P:(f + 1) * P], a[:, k, :],
                                                 start=(n_ == 0), stop=(n_ == 3 * KC - 1))
                                    n_ += 1
                            m.then_inc(S["hidden_made"], 1)
                        if not (isinstance(g, int) and g == NB - 1):
                            transposes(g + 1)
                        for t in range(BT):
                            after(e, S["y_added"], g, BT, t - 1)
                            n_ = 0
                            for f in range(FC):
                                if t == 0:
                                    after(e, S["g_split"], g, FC, f + 1)
                                for a, w in ((GH, W2[s][0]), (GH, W2[s][1]), (GL, W2[s][0])):
                                    m = e.matmul(YP[(BT * u + t) % 2][:, 0:D], a[:, f, t * P:(t + 1) * P], w[:, f, :],
                                                 start=(n_ == 0), stop=(n_ == 3 * FC - 1))
                                    n_ += 1
                            m.then_inc(S["y_made"], 1)
                    blocks(e, body)

        with ExitStack() as ac:
            attn_w = [(sbt(ac, n + "_hi", [P, KC, D], F32R), sbt(ac, n + "_lo", [P, KC, D], F32R))
                      for n in ("wq", "wk", "wv", "wo")]
            bq_c = sbt(ac, "bq_c", [P, KC])
            bk_c = sbt(ac, "bk_c", [P, KC])
            bo_b = sbt(ac, "bo_b", [P, D])
            with ExitStack() as c:
                tok_phase(c, attn_w, bq_c, bk_c, bo_b)
            with ExitStack() as c:
                attention_phase(c, attn_w, bq_c, bk_c, bo_b)
        with ExitStack() as wc:
            W1, W2, b1_e, *weights = weight_buffers(wc)
            with ExitStack() as c:
                router_phase(c, *weights)
            with ExitStack() as c:
                experts_phase(c, W1, W2, b1_e, *weights)


_INS = ["x", "txt", "L0_tok_weight", "L0_tok_weighted_sum", "L0_attn_ln_g", "L0_attn_ln_b", "L0_attn_Wq", "L0_attn_bq",
        "L0_attn_Wk", "L0_attn_bk", "L0_attn_Wv", "L0_attn_bv", "L0_attn_Wo", "L0_attn_bo", "L0_ffn_router_w",
        "L0_ffn_w1", "L0_ffn_b1", "L0_ffn_w2", "L0_ffn_b2"]
_OUTS = [((B, TT + TX, D), "float32")]


def kernel(**inputs):
    import numpy as _np
    import concourse.bacc as _bacc
    from concourse import mybir as _mybir
    from concourse.bass_utils import run_bass_kernel_spmd as _run

    nc = _bacc.Bacc("TRN2", target_bir_lowering=False, num_devices=1)
    arrays, args = {}, []
    for name in _INS:
        a = _np.ascontiguousarray(inputs[name])
        arrays[f"in_{name}_dram"] = a
        args.append(nc.dram_tensor(f"in_{name}_dram", a.shape, _mybir.dt.from_np(a.dtype), kind="ExternalInput").ap())
    for i, (shape, dtype) in enumerate(_OUTS):
        dt = _mybir.dt.from_np(_np.dtype(dtype))
        args.append(nc.dram_tensor(f"out_{i}_dram", shape, dt, kind="ExternalOutput").ap())
    fusion_kernel(nc, *args)
    r = _run(nc, [arrays], core_ids=[0])
    return r.results[0]["out_0_dram"]
```

```python
import concourse.bass as bass
from concourse import mybir
from contextlib import ExitStack

F32 = mybir.dt.float32
F32R = mybir.dt.float32r
BF16 = mybir.dt.bfloat16
I32 = mybir.dt.int32
ALU = mybir.AluOpType
ACT = mybir.ActivationFunctionType
AX = mybir.AxisListType.X

P = 128
B, TT, TX, D = 16, 512, 128, 256
KT = 1024
CK = KT // P
TL = P // B
NTT, NTX = TT // TL, TX // TL
NT = NTT + NTX
NI = NT // 2
NH, DH = 16, 16
KC = D // P
HC = NH // KC
EPS = 1e-5
SCALE = DH ** -0.5
NE, FF = 8, 1024
FC = FF // P
NTOK = B * (TT + TX)
CAP = -(-3 * NTOK // (2 * NE))
BT = 3
BLK = BT * P
NBE = -(-CAP // BLK)
NB = (NTOK + NE * (BLK - 1)) // BLK
NB_MAIN = 2 * round((NTOK / BLK + NE / 2) / 2)
ROW = D + 4
NOWHERE = float(1 << 20)
RT = 4
NR = NT // RT


def after(eng, sem, i, n=1, k=None):
    v = i * n + (n if k is None else k)
    if isinstance(v, int) and v <= 0:
        return
    eng.wait_ge(sem, v)


def fusion_kernel(nc, x, txt, tok_w, tok_ws, ln_g, ln_b, wq, bq, wk, bk, wv, bv, wo, bo,
                  router_w, w1, b1, w2, b2, out):
    ctx = ExitStack()

    def sbt(c, name, shape, dt=F32):
        return c.enter_context(nc.sbuf_tensor(name, shape, dt))

    def pst(c, name, shape):
        return c.enter_context(nc.psum_tensor(name, shape, F32))

    def sem(name):
        return ctx.enter_context(nc.semaphore(name))

    def one_newton_step(link, e, v, y, t):
        link(e.tensor_tensor(t, y, y, ALU.mult))
        link(e.tensor_tensor(t, t, v, ALU.mult))
        link(e.tensor_scalar(t, t, -0.5, 1.5, ALU.mult, ALU.add))
        link(e.tensor_tensor(y, y, t, ALU.mult))

    def whole_stats(link, e, st, halves, t):
        link(e.tensor_tensor(st[:, 0, :], halves[:, :, 1], halves[:, :, 4], ALU.add))
        link(e.tensor_tensor(t, halves[:, :, 1], halves[:, :, 4], ALU.subtract))
        link(e.tensor_tensor(t, t, t, ALU.mult))
        link(e.tensor_tensor(st[:, 1, :], halves[:, :, 2], halves[:, :, 5], ALU.add))
        link(e.tensor_scalar(st[:, 0, :], st[:, 0, :], 0.5, None, ALU.mult))
        link(e.tensor_scalar(st[:, 1, :], st[:, 1, :], 1.0 / D, None, ALU.mult))
        link(e.scalar_tensor_tensor(out=st[:, 1, :], in0=t, scalar=0.25, in1=st[:, 1, :], op0=ALU.mult, op1=ALU.add))

    with ctx:
        slots = nc.dram_tensor("slots", [NI * BLK, ROW], F32, kind="Internal").ap()
        slots_v = slots.rearrange("(g p t) r -> g p t r", p=P, t=BT)
        assert NB <= NI and NB % 2 == 0
        out_rows = out.rearrange("b t f -> (b t) f")
        ident = sbt(ctx, "ident", [P, P])
        wr_t = sbt(ctx, "wr_t", [P, KC, NE])
        b1_t = sbt(ctx, "b1_t", [P, NE * FC])
        ident_ready = sem("ident_ready")
        slots_filled = sem("slots_filled")
        default_out = sem("default_out")

        gated = sbt(ctx, "gated", [P, 2, BT])

        hctx = ctx.enter_context(ExitStack())
        H = sbt(hctx, "H", [P, NT, D])
        halves = sbt(hctx, "halves", [P, NT, 6])
        st = sbt(hctx, "st", [P, 2, NT])
        lnw = sbt(hctx, "lnw", [P, 5, NT])

        def gate(e, passed, par, t=0):
            e.tensor_tensor(gated[:, par, t:t + 1], ident[:, 0:1], ident[:, 0:1], ALU.add).then_inc(passed, 1)


        fill = sbt(hctx, "fill", [P, ROW])
        block_expert = sbt(hctx, "block_expert", [P, NB], I32)
        blocks_used = sbt(hctx, "blocks_used", [P, 1], I32)

        def tok_phase(c, attn_w, bq_c, bk_c, bo_b):
            XS = sbt(c, "XS", [P, 2, 2, KT])
            XH = sbt(c, "XH", [P, 2, KT], F32R)
            XL = sbt(c, "XL", [P, 2, KT], F32R)
            WH = sbt(c, "WH", [P, CK, D], F32R)
            WL = sbt(c, "WL", [P, CK, D], F32R)
            w_outer = sbt(c, "w_outer", [P, KC, D, 4])
            ws_in = sbt(c, "ws_in", [P, KC, D])
            w_in = sbt(c, "w_in", [P, KC, 4])
            aw_in = sbt(c, "aw_in", [P, 4, KC, D])
            g_c = sbt(c, "g_c", [P, KC])
            b_c = sbt(c, "b_c", [P, KC])
            bias_in = sbt(c, "bias_in", [P, 3, KC])
            bv_b = sbt(c, "bv_b", [P, KC, P])
            bo_in = sbt(c, "bo_in", [P, D])
            wr_in = sbt(c, "wr_in", [NE, D])
            b1_in = sbt(c, "b1_in", [NE * FC, P])
            XT = pst(c, "XT", [P, 2, 2, 512])
            HP = pst(c, "HP", [P, 2, 512])
            WB = pst(c, "WB", [P, 2, 512])
            tok_weights_in, small_in, txt_in = sem("tok_weights_in"), sem("small_in"), sem("txt_in")
            x_in = [sem("x_in0"), sem("x_in1")]
            outer_made, w_transposed, w_hi, w_lo = sem("outer_made"), sem("w_transposed"), sem("w_hi"), sem("w_lo")
            fill_made, x_transposed, x_hi, x_lo = sem("fill_made"), sem("x_transposed"), sem("x_hi"), sem("x_lo")
            h_made, h_copied, h_stats = sem("h_made"), sem("h_copied"), sem("h_stats")
            tok_chain, bias_made, bv_spread, bo_made = sem("tok_chain"), sem("bias_made"), sem("bv_spread"), sem("bo_made")
            router_transposed, b1_transposed, small_copied = sem("router_transposed"), sem("b1_transposed"), sem("small_copied")
            weights_chain = sem("weights_chain")
            NSMALL = 4 + 5 + 3
            xr = x.rearrange("b h i d -> (b h) (i d)").rearrange("(p t) k -> p t k", t=NTT)
            txr = txt.rearrange("b t f -> (b t) f").rearrange("(p t) f -> p t f", t=NTX)
            outer2 = w_outer[:, :, :, :].rearrange("p c i d -> p c (i d)")

            with nc.Block() as block:
                @block.sync
                def _(e):
                    e.dma_start(ws_in[:, :, :], tok_ws.rearrange("(c p) i -> p c i", p=P)).then_inc(tok_weights_in, 16)
                    e.dma_start(w_in[:, :, :], tok_w.rearrange("(c p) d -> p c d", p=P)).then_inc(tok_weights_in, 16)
                    for u in range(2):
                        e.dma_start(XS[:, u, :, :], xr[:, 2 * u:2 * u + 2, :]).then_inc(x_in[u], 16)
                    with e.Fori(1, NTT // 4) as n:
                        for u in range(2):
                            e.wait_ge(x_transposed, n * 8 + (4 * u - 4))
                            e.dma_start(XS[:, u, :, :], xr[:, bass.ds(n * 4 + 2 * u, 2), :]).then_inc(x_in[u], 16)

                @block.gpsimd
                def _(e):
                    e.memset(fill[:, :], 0.0).then_inc(fill_made, 1)
                    e.memset(ident[:, :], 0.0).then_inc(fill_made, 1)
                    e.wait_ge(fill_made, 2)
                    e.memset(fill[:, D + 3:ROW], NOWHERE).then_inc(fill_made, 1)
                    e.affine_select(out=ident[:, :], in_=ident[:, :], compare_op=ALU.not_equal, fill=1.0, base=0,
                                    pattern=[[-1, P]], channel_multiplier=1).then_inc(ident_ready, 1)
                    chained = [0]

                    def link(ins):
                        chained[0] += 1
                        ins.then_inc(weights_chain, 1)
                        e.wait_ge(weights_chain, chained[0])

                    e.wait_ge(small_in, 16 * NSMALL)
                    e.wait_ge(bias_made, 1)
                    for i in range(4):
                        hi_, lo_ = attn_w[i]
                        if i < 3:
                            for k in range(KC):
                                link(e.tensor_scalar(aw_in[:, i, k, :], aw_in[:, i, k, :], g_c[:, k:k + 1], None, ALU.mult))
                        link(e.tensor_copy(hi_[:, :, :], aw_in[:, i, :, :]))
                        link(e.tensor_tensor(lo_[:, :, :], aw_in[:, i, :, :], hi_[:, :, :].bitcast(F32), ALU.subtract))

                @block.scalar
                def _(e):
                    for i, w in enumerate((wq, wk, wv, wo)):
                        e.dma_start(aw_in[:, i, :, :], w.rearrange("(c p) n -> p c n", p=P)).then_inc(small_in, 16)
                    for dst, src in ((g_c[:, :], ln_g), (b_c[:, :], ln_b), (bias_in[:, 0, :], bq),
                                     (bias_in[:, 1, :], bk), (bias_in[:, 2, :], bv)):
                        e.dma_start(dst, src.rearrange("(c p) -> p c", p=P),
                                    allow_slow_non_contiguous=True).then_inc(small_in, 16)
                    e.dma_start(bo_in[:, :], bo.unsqueeze(0).broadcast_to([P, D])).then_inc(small_in, 16)
                    e.dma_start(wr_in[:, :], router_w).then_inc(small_in, 16)
                    e.dma_start(b1_in[:, :], b1.rearrange("e (f p) -> (e f) p", p=P)).then_inc(small_in, 16)
                    e.dma_start(H[:, NTT:, :], txr).then_inc(txt_in, 16)
                    e.wait_ge(fill_made, 3)
                    for k in range(CK):
                        e.wait_ge(w_transposed, k + 1)
                        e.activation(WH[:, k, :], WB[:, k % 2, 0:D], ACT.Copy).then_inc(w_hi, 1)

                    def hi(T, par):
                        for h in range(2):
                            after(e, x_transposed, T, 2, h + 1)
                            after(e, h_made, T - 2)
                            e.activation(XH[:, par, h * 512:(h + 1) * 512], XT[:, par, h, :], ACT.Copy).then_inc(x_hi, 1)

                    def copy_h(T, par):
                        after(e, h_made, T)
                        e.activation(H[:, T, :], HP[:, par, 0:D], ACT.Copy).then_inc(h_copied, 1)

                    hi(0, 0)
                    with e.Fori(0, NTT // 2 - 1) as n:
                        for u in range(2):
                            hi(n * 2 + (u + 1), (u + 1) % 2)
                            copy_h(n * 2 + u, u)
                    hi(NTT - 1, 1)
                    copy_h(NTT - 2, 0)
                    copy_h(NTT - 1, 1)

                @block.vector
                def _(e):
                    chained = [0]

                    def link(ins):
                        chained[0] += 1
                        ins.then_inc(tok_chain, 1)
                        e.wait_ge(tok_chain, chained[0])

                    e.wait_ge(tok_weights_in, 32)
                    for c_ in range(KC):
                        e.tensor_tensor(w_outer[:, c_, :, :], ws_in[:, c_, :].unsqueeze(2).broadcast_to([P, D, 4]),
                                        w_in[:, c_, :].unsqueeze(1).broadcast_to([P, D, 4]), ALU.mult).then_inc(outer_made, 1)
                    for k in range(CK):
                        e.wait_ge(w_hi, k + 1)
                        e.tensor_tensor(WL[:, k, :], WB[:, k % 2, 0:D], WH[:, k, :].bitcast(F32),
                                        ALU.subtract).then_inc(w_lo, 1)
                    e.wait_ge(small_in, 16 * NSMALL)
                    e.wait_ge(bias_made, 1)
                    e.tensor_tensor(bq_c[:, :], WB[:, 0, 0:KC], bias_in[:, 0, :], ALU.add).then_inc(small_copied, 1)
                    e.tensor_tensor(bk_c[:, :], WB[:, 0, KC:2 * KC], bias_in[:, 1, :], ALU.add).then_inc(small_copied, 1)
                    link(e.tensor_tensor(bias_in[:, 2, :], WB[:, 0, 2 * KC:3 * KC], bias_in[:, 2, :], ALU.add))
                    e.tensor_copy(bv_b[:, :, :], bias_in[:, 2, :].unsqueeze(2).broadcast_to([P, KC, P])).then_inc(bv_spread, 1)
                    e.wait_ge(bo_made, 1)
                    e.tensor_tensor(bo_b[:, :], WB[:, 1, 0:D], bo_in[:, :], ALU.add).then_inc(small_copied, 1)
                    e.wait_ge(router_transposed, 1)
                    e.tensor_copy(wr_t[:, :, :], WB[:, 0, 0:KC * NE].rearrange("p (c e) -> p c e", c=KC)).then_inc(small_copied, 1)
                    e.wait_ge(b1_transposed, 1)
                    e.tensor_copy(b1_t[:, :], WB[:, 1, 0:NE * FC]).then_inc(small_copied, 1)

                    def lo(T, par):
                        for h in range(2):
                            after(e, x_hi, T, 2, h + 1)
                            e.tensor_tensor(XL[:, par, h * 512:(h + 1) * 512], XT[:, par, h, :],
                                            XH[:, par, h * 512:(h + 1) * 512].bitcast(F32), ALU.subtract).then_inc(x_lo, 1)

                    def stats(T):
                        e.bn_stats(halves[:, T, :], H[:, T, :]).then_inc(h_stats, 1)

                    lo(0, 0)
                    lo(1, 1)
                    e.wait_ge(txt_in, 16)

                    def two(n):
                        for u in range(2):
                            after(e, h_copied, n * 2 + u)
                            lo(n * 2 + (u + 2), u)
                            stats(n * 2 + u)
                    with e.Fori(0, NTX) as n:
                        two(n)
                        stats(n + NTT)
                    with e.Fori(NTX, NTT // 2 - 1) as n:
                        two(n)
                    for T in (NTT - 2, NTT - 1):
                        after(e, h_copied, T)
                        stats(T)
                    e.wait_ge(h_stats, NT)

                @block.tensor
                def _(e):
                    e.wait_ge(ident_ready, 1)
                    e.wait_ge(outer_made, 2)
                    for k in range(CK):
                        if k >= 2:
                            e.wait_ge(w_lo, k - 1)
                        for c_ in range(KC):
                            m = e.transpose(WB[:, k % 2, c_ * P:(c_ + 1) * P], outer2[:, c_, k * P:(k + 1) * P], ident[:, :])
                        m.then_inc(w_transposed, 1)
                    e.wait_ge(small_in, 16 * NSMALL)
                    e.wait_ge(w_lo, CK)
                    for i in range(3):
                        for c_ in range(KC):
                            for k in range(KC):
                                m = e.matmul(WB[:, 0, i * KC + c_:i * KC + c_ + 1], aw_in[:, i, k, c_ * P:(c_ + 1) * P],
                                             b_c[:, k:k + 1], start=(k == 0), stop=(k == KC - 1))
                    m.then_inc(bias_made, 1)
                    e.wait_ge(bv_spread, 1)
                    for k in range(KC):
                        m = e.matmul(WB[:, 1, 0:D], bv_b[:, k, :], aw_in[:, 3, k, :], start=(k == 0), stop=(k == KC - 1))
                    m.then_inc(bo_made, 1)
                    for c_ in range(KC):
                        m = e.transpose(WB[:, 0, c_ * NE:(c_ + 1) * NE], wr_in[:, c_ * P:(c_ + 1) * P], ident[0:NE, 0:NE])
                    m.then_inc(router_transposed, 1)
                    e.wait_ge(small_copied, 3)
                    e.transpose(WB[:, 1, 0:NE * FC], b1_in[:, :], ident[0:NE * FC, 0:NE * FC]).then_inc(b1_transposed, 1)

                    def transposes(T, u):
                        for h in range(2):
                            after(e, x_lo, T - 2, 2, h + 1)
                            for k in range(4):
                                kk = h * 4 + k
                                m = e.transpose(XT[:, u % 2, h, k * P:(k + 1) * P],
                                                XS[:, u // 2, u % 2, kk * P:(kk + 1) * P], ident[:, :])
                            m.then_inc(x_transposed, 1)

                    def products(T, par):
                        after(e, x_lo, T, 2)
                        after(e, h_copied, T - 2)
                        n_ = 0
                        for k in range(CK):
                            for a, w in ((XH, WH), (XH, WL), (XL, WH)):
                                m = e.matmul(HP[:, par, 0:D], a[:, par, k * P:(k + 1) * P], w[:, k, :],
                                             start=(n_ == 0), stop=(n_ == 3 * CK - 1))
                                n_ += 1
                        m.then_inc(h_made, 1)

                    def four(n):
                        for u in range(4):
                            if u == 1:
                                e.wait_ge(x_in[1], n * 16 + 16)
                            if u == 3:
                                e.wait_ge(x_in[0], n * 16 + 32)
                            transposes(n * 4 + (u + 1), (u + 1) % 4)
                            products(n * 4 + u, u % 2)

                    e.wait_ge(x_in[0], 16)
                    transposes(0, 0)
                    four(0)
                    with e.Fori(1, NTT // 4 - 1) as n:
                        four(n)
                    for u in range(3):
                        if u == 1:
                            e.wait_ge(x_in[1], 16 * (NTT // 4))
                        transposes(NTT - 4 + u + 1, u + 1)
                        products(NTT - 4 + u, u % 2)
                    products(NTT - 1, 1)

        def attention_phase(c, attn_w, bq_c, bk_c, bo_b):
            (WQH, WQL), (WKH, WKL), (WVH, WVL), (WOH, WOL) = attn_w
            r, rs, one_r, neg_mr, neg_mrs = (lnw[:, i, :] for i in range(5))
            XN = sbt(c, "XN", [P, 2, D])
            XNH = sbt(c, "XNH", [P, KC, D], F32R)
            XNL = sbt(c, "XNL", [P, KC, D], F32R)
            QS = sbt(c, "QS", [P, 3, KC, B * 2 * TL], BF16)
            KS = sbt(c, "KS", [P, KC * 2 * TL, 3, B], BF16)
            VS = sbt(c, "VS", [P, 4, 2 * NH, 3, DH], BF16)
            PS = sbt(c, "PS", [P, 2, 3, B * 2 * NH], BF16)
            RQ = sbt(c, "RQ", [P, 2 * D])
            RK = sbt(c, "RK", [P, 2 * D])
            RV = sbt(c, "RV", [P, 2 * D])
            RP = sbt(c, "RP", [P, 2 * D])
            QBD = sbt(c, "QBD", [P, 3, KC, HC, B * 2 * TL], BF16)
            PX = sbt(c, "PX", [P, 3, TL, B * 2 * NH], BF16)
            SB = sbt(c, "SB", [P, 2 * KC * TL, B])
            SD = sbt(c, "SD", [P, 2 * KC * TL, B])
            EX = sbt(c, "EX", [P, 2 * KC * TL, B])
            PN = sbt(c, "PN", [P, 2 * KC * TL, B])
            MX = sbt(c, "MX", [P, 2 * KC * TL])
            SM = sbt(c, "SM", [P, 2 * KC * TL])
            RC = sbt(c, "RC", [P, 2 * KC * TL])
            OB = sbt(c, "OB", [P, 2 * NH, DH])
            OTH = sbt(c, "OTH", [P, KC * 2, B, TL], F32R)
            OTL = sbt(c, "OTL", [P, KC * 2, B, TL], F32R)
            T1 = sbt(c, "T1", [P, 2, D])
            T2 = sbt(c, "T2", [P, 2, D])
            tmp = T1[:, :, 0:NT]
            bank = [pst(c, f"bank{i}", [P, 512]) for i in range(8)]
            XTV, S0, S1, QOT, KB, O0, O1, WB = bank
            SBK, OBK = (S0, S1), (O0, O1, S1, WB)
            S = {n: sem(n) for n in (
                "ln_sqrt", "ln_chain", "ln_done", "zeroed", "xn_made", "xn_transposed", "xn_hi", "xn_lo",
                "q_made", "k_made", "v_made", "q1", "q2", "q3", "q_rest", "k1", "k2", "k3", "k_rest",
                "v1", "v2", "v3", "v_rest", "s_made", "s_summed", "max_made", "shifted", "exp_made", "sum_made",
                "recip_made", "p_made", "p_transposed", "p1", "p2", "p3", "p_rest", "o_made", "o_summed",
                "o_transposed", "o_hi", "o_lo", "wo_made", "res_scaled", "res_bias", "h_updated", "attn_stats",
                "q_spread", "p_spread")}

            def perm(ap):
                return ap.rearrange("p (g t b) -> p g b t", g=2 * KC, t=TL)

            def swapped(ap, n):
                return ap.rearrange("p (b t) -> p t b", b=n)

            def as_made(ap):
                return ap[:, :].rearrange("p (g b t) -> p g b t", g=2 * KC, t=TL)

            class Step:
                def __init__(self, i, at):
                    self.i = i
                    self.p = (at - 1) % 2
                    self.v = (at + 1) % 4, (at - 2) % 4
                    self.xn, self.xt, self.nxt, self.cur, self.prv, self.old, self.older = (
                        0 <= at + d < NI for d in (3, 2, 1, 0, -1, -2, -3))

            def steps(e, body):
                for i in range(-1, 4):
                    body(Step(i, i))
                with e.Fori(1, NI // 4 - 1) as n:
                    for u in range(4):
                        body(Step(n * 4 + u, 4 + u))
                for i in range(NI - 4, NI + 3):
                    body(Step(i, i))

            with nc.Block() as block:
                @block.sync
                def _(e):
                    e.wait_ge(S["zeroed"], 2)

                    def body(st_):
                        i = st_.i
                        if st_.nxt:
                            after(e, S["q3"], i + 1)
                            after(e, S["s_made"], i, 4)
                            for h in range(HC):
                                rows = slice(h * DH, (h + 1) * DH)
                                e.dma_start(QBD[rows, :, :, h, :], QS[rows, :, :, :]).then_inc(S["q_spread"], 16)
                            e.dma_start(slots_v[bass.ds(i + 1, 1)].rearrange("g p t r -> p (g t) r"),
                                        fill[:, :].unsqueeze(1).broadcast_to([P, BT, ROW])).then_inc(slots_filled, 16)
                        if st_.prv:
                            after(e, S["p3"], i - 1)
                            after(e, S["o_made"], i - 2, 4)
                            for t in range(TL):
                                rows = slice(t * B, (t + 1) * B)
                                e.dma_start(PX[rows, :, t, :], PS[rows, st_.p, :, :]).then_inc(S["p_spread"], 16)
                    steps(e, body)

                @block.gpsimd
                def _(e):
                    e.memset(PX[:, :, :, :].rearrange("p a t c -> p (a t c)").bitcast(F32), 0.0).then_inc(S["zeroed"], 1)

                    def third(name, dst, rest, i, src2):
                        after(e, S[name + "_rest"], i, 2 if name in "qk" else 1)
                        after(e, S[name + "2"], i)
                        e.tensor_tensor(dst, rest, src2, ALU.subtract).then_inc(S[name + "3"], 1)

                    def body(st_):
                        i = st_.i
                        if st_.nxt:
                            third("q", QS[:, 2, :, :].rearrange("p c n -> p (c n)"), RQ[:, :], i + 1,
                                  QS[:, 1, :, :].rearrange("p c n -> p (c n)"))
                        if st_.prv:
                            third("p", PS[:, st_.p, 2, :], RP[:, :], i - 1, PS[:, st_.p, 1, :])
                        if st_.older:
                            after(e, S["h_updated"], i - 4)
                            after(e, S["res_scaled"], i - 3)
                            e.tensor_tensor(T2[:, :, :], T1[:, :, :], bo_b[:, :].unsqueeze(1).broadcast_to([P, 2, D]),
                                            ALU.add).then_inc(S["res_bias"], 1)
                        if st_.cur:
                            after(e, S["exp_made"], i - 1)
                            after(e, S["max_made"], i)
                            e.tensor_tensor(SD[:, :, :], SB[:, :, :],
                                            MX[:, :].unsqueeze(2).broadcast_to([P, 2 * KC * TL, B]),
                                            ALU.subtract).then_inc(S["shifted"], 1)
                            after(e, S["p_transposed"], i - 1)
                            after(e, S["recip_made"], i)
                            e.tensor_tensor(PN[:, :, :], EX[:, :, :],
                                            RC[:, :].unsqueeze(2).broadcast_to([P, 2 * KC * TL, B]),
                                            ALU.mult).then_inc(S["p_made"], 1)
                        if st_.nxt:
                            third("k", KS[:, :, 2, :], RK[:, :].rearrange("p (g b) -> p g b", b=B), i + 1, KS[:, :, 1, :])
                            v = st_.v[0]
                            third("v", VS[:, v, :, 2, :], RV[:, :].rearrange("p (g d) -> p g d", d=DH), i + 1,
                                  VS[:, v, :, 1, :])
                    steps(e, body)

                @block.scalar
                def _(e):
                    e.wait_ge(S["ln_chain"], 8)
                    e.activation(r, tmp[:, 0, :], ACT.Sqrt).then_inc(S["ln_sqrt"], 1)
                    e.wait_ge(S["ln_chain"], 16)
                    e.activation(rs, tmp[:, 0, :], ACT.Sqrt).then_inc(S["ln_sqrt"], 1)

                    def xn(i):
                        for j in range(2):
                            T = i * 2 + j
                            e.activation(XN[:, j, :], H[:, T, :], ACT.Identity, scale=lnw[:, 1, bass.ds(T, 1)],
                                         bias=lnw[:, 4, bass.ds(T, 1)]).then_inc(S["xn_made"], 1)

                    def xn_hi(i):
                        after(e, S["v_made"], i - 1)
                        after(e, S["xn_transposed"], i)
                        e.activation(perm(XNH[:, :, :].rearrange("p c n -> p (c n)")), as_made(XTV), ACT.Copy).then_inc(S["xn_hi"], 1)

                    e.wait_ge(S["ln_done"], 1)
                    xn(0)
                    xn_hi(0)
                    xn(1)

                    def body(st_):
                        i = st_.i
                        v = st_.v[0]
                        if st_.nxt:
                            after(e, S["q_spread"], i, 16 * HC)
                            after(e, S["q_made"], i + 1)
                            for c_ in range(KC):
                                e.activation(swapped(QS[:, 0, c_, :], B),
                                             QOT[:, c_ * D:(c_ + 1) * D].rearrange("p (t b) -> p t b", b=B),
                                             ACT.Identity, bias=bq_c[:, c_:c_ + 1]).then_inc(S["q1"], 1)
                        if st_.prv:
                            after(e, S["p_spread"], i - 3, 16 * TL)
                            after(e, S["p_transposed"], i - 1)
                            e.activation(swapped(PS[:, st_.p, 0, :], B), O0[:, :].rearrange("p (h b) -> p h b", b=B), ACT.Copy).then_inc(S["p1"], 1)
                        if st_.nxt:
                            if st_.older:
                                after(e, S["res_bias"], i - 4)
                            after(e, S["q_rest"], i + 1, 2)
                            e.activation(QS[:, 1, :, :].rearrange("p c n -> p (c n)"), RQ[:, :], ACT.Copy).then_inc(S["q2"], 1)
                        if st_.older:
                            after(e, S["wo_made"], i - 4)
                            after(e, S["o_transposed"], i - 3)
                            e.activation(OTH[:, :, :, :].rearrange("p g b t -> p g t b"),
                                         O1[:, :].rearrange("p (g t b) -> p g t b", g=4, t=TL), ACT.Copy).then_inc(S["o_hi"], 1)
                        if st_.prv:
                            after(e, S["p_rest"], i - 1)
                            e.activation(PS[:, st_.p, 1, :], RP[:, :], ACT.Copy).then_inc(S["p2"], 1)
                        if st_.older:
                            if not st_.nxt:
                                after(e, S["res_bias"], i - 4)
                            for j in range(2):
                                T = i * 2 + (j - 6)
                                m = e.activation(T1[:, j, :], H[:, T, :], ACT.Identity, scale=lnw[:, 2, bass.ds(T, 1)],
                                                 bias=lnw[:, 3, bass.ds(T, 1)])
                            m.then_inc(S["res_scaled"], 1)
                        if st_.nxt:
                            after(e, S["s_made"], i, 4)
                            after(e, S["k_made"], i + 1)
                            for c_ in range(KC):
                                e.activation(KS[:, c_ * 2 * TL:(c_ + 1) * 2 * TL, 0, :],
                                             KB[:, c_ * D:(c_ + 1) * D].rearrange("p (g b) -> p g b", b=B),
                                             ACT.Identity, bias=bk_c[:, c_:c_ + 1]).then_inc(S["k1"], 1)
                            after(e, S["o_made"], i - 3, 4)
                            after(e, S["v_made"], i + 1)
                            e.activation(VS[:, v, :, 0, :], XTV[:, :].rearrange("p (g d) -> p g d", d=DH),
                                         ACT.Copy).then_inc(S["v1"], 1)
                        if st_.cur:
                            after(e, S["p_made"], i - 1)
                            after(e, S["sum_made"], i - 1)
                            after(e, S["shifted"], i)
                            e.activation(EX[:, :, :], SD[:, :, :], ACT.Exp, scale=SCALE).then_inc(S["exp_made"], 1)
                        if st_.xt:
                            xn_hi(i + 2)
                        if st_.nxt:
                            after(e, S["k_rest"], i + 1, 2)
                            e.activation(KS[:, :, 1, :], RK[:, :].rearrange("p (g b) -> p g b", b=B), ACT.Copy).then_inc(S["k2"], 1)
                            after(e, S["v_rest"], i + 1)
                            e.activation(VS[:, v, :, 1, :], RV[:, :].rearrange("p (g d) -> p g d", d=DH),
                                         ACT.Copy).then_inc(S["v2"], 1)
                        if st_.xn:
                            xn(i + 3)
                    steps(e, body)

                @block.vector
                def _(e):
                    chained = [0]

                    def link(ins):
                        chained[0] += 1
                        ins.then_inc(S["ln_chain"], 1)
                        e.wait_ge(S["ln_chain"], chained[0])

                    v, t = tmp[:, 0, :], tmp[:, 1, :]
                    mean, var = st[:, 0, :], st[:, 1, :]
                    whole_stats(link, e, st, halves, t)
                    link(e.tensor_scalar(v, var, EPS, None, ALU.add))
                    e.wait_ge(S["ln_sqrt"], 1)
                    link(e.reciprocal(r, r))
                    one_newton_step(link, e, v, r, t)
                    link(e.tensor_tensor(t, r, r, ALU.mult))
                    link(e.tensor_tensor(v, t, var, ALU.mult))
                    link(e.tensor_scalar(v, v, EPS, None, ALU.add))
                    assert chained[0] == 16
                    e.wait_ge(S["ln_sqrt"], 2)
                    link(e.reciprocal(rs, rs))
                    one_newton_step(link, e, v, rs, t)
                    link(e.tensor_tensor(rs, rs, r, ALU.mult))
                    link(e.tensor_scalar(t, mean, -1.0, None, ALU.mult))
                    link(e.tensor_scalar(one_r, r, 1.0, None, ALU.add))
                    link(e.tensor_tensor(neg_mr, t, r, ALU.mult))
                    e.tensor_tensor(neg_mrs, t, rs, ALU.mult).then_inc(S["ln_done"], 1)
                    e.memset(QBD[:, :, :, :, :].rearrange("p a c h n -> p (a c h n)").bitcast(F32), 0.0).then_inc(S["zeroed"], 1)

                    def xn_lo(i):
                        after(e, S["xn_hi"], i)
                        e.tensor_tensor(perm(XNL[:, :, :].rearrange("p c n -> p (c n)")), as_made(XTV),
                                        perm(XNH[:, :, :].rearrange("p c n -> p (c n)").bitcast(F32)),
                                        ALU.subtract).then_inc(S["xn_lo"], 1)

                    def sum_of_three(name, made, bank_, dst, i, s_):
                        after(e, S[made], i, 4, s_ + 1)
                        e.tensor_reduce(dst, bank_[:, 0:TL * 3 * B].rearrange("p (g a b) -> p g b a", a=3, b=B),
                                        AX, ALU.add).then_inc(S[name], 1)

                    def s_sum(i, s_):
                        g = (s_ % 2) * 2 * TL + (s_ // 2) * TL
                        sum_of_three("s_summed", "s_made", SBK[s_ % 2], SB[:, g:g + TL, :], i, s_)

                    def o_sum(i, s_):
                        sum_of_three("o_summed", "o_made", OBK[s_], OB[:, s_ * HC:(s_ + 1) * HC, :], i, s_)

                    def stats(i):
                        for j in range(2):
                            e.bn_stats(halves[:, i * 2 + j, :], H[:, i * 2 + j, :]).then_inc(S["attn_stats"], 1)

                    xn_lo(0)

                    def body(st_):
                        i = st_.i
                        if st_.nxt:
                            after(e, S["q3"], i)
                            for c_ in range(KC):
                                after(e, S["q1"], i + 1, 2)
                                e.scalar_tensor_tensor(out=swapped(RQ[:, c_ * D:(c_ + 1) * D], B),
                                                       in0=QOT[:, c_ * D:(c_ + 1) * D].rearrange("p (t b) -> p t b", b=B),
                                                       scalar=bq_c[:, c_:c_ + 1], in1=swapped(QS[:, 0, c_, :], B),
                                                       op0=ALU.add, op1=ALU.subtract).then_inc(S["q_rest"], 1)
                        if st_.prv:
                            after(e, S["p3"], i - 2)
                            after(e, S["p1"], i - 1)
                            e.tensor_tensor(swapped(RP[:, :], B), O0[:, :].rearrange("p (h b) -> p h b", b=B),
                                            swapped(PS[:, st_.p, 0, :], B), ALU.subtract).then_inc(S["p_rest"], 1)
                        if st_.cur:
                            after(e, S["shifted"], i - 1)
                            s_sum(i, 0)
                            s_sum(i, 1)
                        if st_.older:
                            after(e, S["o_hi"], i - 3)
                            e.tensor_tensor(OTL[:, :, :, :].rearrange("p g b t -> p g t b"),
                                            O1[:, :].rearrange("p (g t b) -> p g t b", g=4, t=TL),
                                            OTH[:, :, :, :].rearrange("p g b t -> p g t b").bitcast(F32),
                                            ALU.subtract).then_inc(S["o_lo"], 1)
                        if st_.cur:
                            s_sum(i, 2)
                            s_sum(i, 3)
                            after(e, S["s_summed"], i, 4)
                            e.tensor_reduce(MX[:, :], SB[:, :, :], AX, ALU.max).then_inc(S["max_made"], 1)
                        if st_.nxt:
                            after(e, S["k3"], i)
                            for c_ in range(KC):
                                after(e, S["k1"], i + 1, 2)
                                e.scalar_tensor_tensor(out=RK[:, c_ * D:(c_ + 1) * D].rearrange("p (g b) -> p g b", b=B),
                                                       in0=KB[:, c_ * D:(c_ + 1) * D].rearrange("p (g b) -> p g b", b=B),
                                                       scalar=bk_c[:, c_:c_ + 1],
                                                       in1=KS[:, c_ * 2 * TL:(c_ + 1) * 2 * TL, 0, :],
                                                       op0=ALU.add, op1=ALU.subtract).then_inc(S["k_rest"], 1)
                            after(e, S["v3"], i)
                            after(e, S["v1"], i + 1)
                            e.tensor_tensor(RV[:, :].rearrange("p (g d) -> p g d", d=DH), XTV[:, :].rearrange("p (g d) -> p g d", d=DH),
                                            VS[:, st_.v[0], :, 0, :], ALU.subtract).then_inc(S["v_rest"], 1)
                        if st_.older:
                            after(e, S["res_bias"], i - 3)
                            after(e, S["wo_made"], i - 3)
                            e.tensor_tensor(H[:, bass.ds(i * 2 - 6, 2), :], WB[:, :].rearrange("p (j n) -> p j n", j=2),
                                            T2[:, :, :], ALU.add).then_inc(S["h_updated"], 1)
                        if st_.cur:
                            after(e, S["exp_made"], i)
                            e.tensor_reduce(SM[:, :], EX[:, :, :], AX, ALU.add).then_inc(S["sum_made"], 1)
                            after(e, S["p_made"], i - 1)
                            after(e, S["sum_made"], i)
                            e.reciprocal(RC[:, :], SM[:, :]).then_inc(S["recip_made"], 1)
                        if st_.xt:
                            xn_lo(i + 2)
                        if st_.older:
                            after(e, S["h_updated"], i - 3)
                        if st_.old:
                            after(e, S["o_transposed"], i - 3)
                            for s_ in range(4):
                                o_sum(i - 2, s_)
                        if st_.older:
                            stats(i - 3)
                    steps(e, body)
                    e.wait_ge(S["attn_stats"], NT)

                @block.tensor
                def _(e):
                    def project(dst, wh, wl, wait=None):
                        for c_ in range(KC):
                            n_ = 0
                            for k in range(KC):
                                for w, a in ((wh, XNH), (wl, XNH), (wh, XNL)):
                                    m = e.matmul(dst[:, c_ * D:(c_ + 1) * D], w[:, k, c_ * P:(c_ + 1) * P], a[:, k, :],
                                                 start=(n_ == 0), stop=(n_ == 3 * KC - 1))
                                    n_ += 1
                        return m

                    def tokens_by_features(dst, ah, al, wh, wl):
                        for j in range(2):
                            n_ = 0
                            for k in range(KC):
                                for a, w in ((ah, wh), (ah, wl), (al, wh)):
                                    m = e.matmul(dst[:, j * D:(j + 1) * D], a(k, j), w[:, k, :],
                                                 start=(n_ == 0), stop=(n_ == 3 * KC - 1))
                                    n_ += 1
                        return m

                    def small_products(dst, stationary, moving):
                        for t in range(8):
                            for a in range(3):
                                m = e.matmul(dst[:, t * 48:t * 48 + 16 * (3 - a)], stationary(a, t), moving(t, 3 - a),
                                             start=(t == 0 and a == 0), stop=(t == 7 and a == 2), skip_group_check=True)
                        return m

                    def xn_transposes(i):
                        after(e, S["v_rest"], i - 1)
                        after(e, S["xn_made"], i, 2)
                        for c_ in range(KC):
                            for j in range(2):
                                m = e.transpose(XTV[:, c_ * D + j * P:c_ * D + (j + 1) * P], XN[:, j, c_ * P:(c_ + 1) * P],
                                                ident[:, :])
                        m.then_inc(S["xn_transposed"], 1)

                    xn_transposes(0)

                    def body(st_):
                        i = st_.i
                        if st_.nxt:
                            after(e, S["q_rest"], i, 2)
                            after(e, S["xn_lo"], i + 1)
                            project(QOT, WQH, WQL).then_inc(S["q_made"], 1)
                        if st_.prv:
                            if st_.older:
                                after(e, S["o_summed"], i - 3, 4, 1)
                            after(e, S["p_made"], i - 1)
                            for j in range(2):
                                for c_ in range(KC):
                                    m = e.transpose(O0[:, j * D + c_ * P:j * D + (c_ + 1) * P],
                                                    PN[:, (c_ * 2 + j) * TL:(c_ * 2 + j + 1) * TL, :].rearrange("p t b -> p (t b)"),
                                                    ident[:, :])
                            m.then_inc(S["p_transposed"], 1)
                        if st_.nxt:
                            after(e, S["k_rest"], i, 2)
                            project(KB, WKH, WKL).then_inc(S["k_made"], 1)
                        if st_.older:
                            after(e, S["o_summed"], i - 3, 4)
                            for c_ in range(KC):
                                for j in range(2):
                                    m = e.transpose(O1[:, c_ * D + j * P:c_ * D + (j + 1) * P],
                                                    OB[:, j * NH + c_ * HC:j * NH + (c_ + 1) * HC, :].rearrange("p h d -> p (h d)"),
                                                    ident[:, :])
                            m.then_inc(S["o_transposed"], 1)
                        if st_.cur:
                            after(e, S["k3"], i)
                            after(e, S["s_summed"], i - 1, 4)
                            after(e, S["q_spread"], i, 16 * HC)
                            for s_ in range(4):
                                j, c_ = s_ // 2, s_ % 2
                                after(e, S["s_summed"], i, 4, s_ - 1)
                                small_products(SBK[s_ % 2],
                                               lambda a, t: QBD[:, a, c_, :, :].rearrange("p h (b t) -> p (h b) t", b=B)[:, :, j * TL + t],
                                               lambda t, n: KS[:, c_ * 2 * TL + j * TL + t, 0:n, :]).then_inc(S["s_made"], 1)
                        if st_.nxt:
                            tokens_by_features(XTV, lambda k, j: XNH[:, k, j * P:(j + 1) * P],
                                               lambda k, j: XNL[:, k, j * P:(j + 1) * P], WVH, WVL).then_inc(S["v_made"], 1)
                        if st_.older:
                            after(e, S["h_updated"], i - 4)
                            after(e, S["o_lo"], i - 3)
                            tokens_by_features(WB, lambda k, j: OTH[:, k * 2 + j, :, :].rearrange("p b t -> p (b t)"),
                                               lambda k, j: OTL[:, k * 2 + j, :, :].rearrange("p b t -> p (b t)"),
                                               WOH, WOL).then_inc(S["wo_made"], 1)
                        if st_.xt and not st_.old:
                            xn_transposes(i + 2)
                        if st_.old:
                            if st_.older:
                                after(e, S["o_lo"], i - 3)
                            if st_.prv:
                                after(e, S["p_rest"], i - 1)
                            after(e, S["v3"], i - 2)
                            after(e, S["p_spread"], i - 2, 16 * TL)
                            for s_ in range(4):
                                if s_ == 1 and st_.xt:
                                    xn_transposes(i + 2)
                                if s_ == 2 and st_.cur:
                                    after(e, S["s_summed"], i, 4)
                                if s_ == 3 and st_.older:
                                    after(e, S["h_updated"], i - 3)
                                small_products(OBK[s_],
                                               lambda a, t: PX[:, a, :, :].rearrange("p l (b h) -> p (l b) h", b=B)[:, :, s_ * HC + t],
                                               lambda t, n: VS[:, st_.v[1], s_ * HC + t, 0:n, :]).then_inc(S["o_made"], 1)
                    steps(e, body)

        PIECES = 4
        experts_known = sem("experts_known")

        class WeightSignals:
            def __init__(self, first, tag):
                self.first = first
                self.loaded = [sem(f"weights_in{k}{tag}") for k in range(PIECES)]
                self.rounded, self.split = sem("w_rounded" + tag), sem("w_split" + tag)

        main_signals, tail_signals = WeightSignals(0, ""), WeightSignals(NB_MAIN, "_tail")
        w1_v = w1.rearrange("e (c p) f -> e p c f", p=P)
        w2_v = w2.rearrange("e (c p) f -> e p c f", p=P)

        def weight_slot(c, W1, W2):
            s = len(W1)
            W1.append((sbt(c, f"w1_hi{s}", [P, KC, FF], F32R), sbt(c, f"w1_lo{s}", [P, KC, FF], F32R)))
            W2.append((sbt(c, f"w2_hi{s}", [P, FC, D], F32R), sbt(c, f"w2_lo{s}", [P, FC, D], F32R)))

        def weight_buffers(c):
            stages = sbt(c, "stage1", [P, KC, FF]), sbt(c, "stage2", [P, FC, D])
            W1, W2 = [], []
            weight_slot(c, W1, W2)

            def piece(k, s):
                w, kk = k // 2, k % 2
                n_ = (KC, FC)[w] // 2
                return (t[:, kk * n_:(kk + 1) * n_, :] for t in (stages[w], *(W1, W2)[w][s]))

            def expert_of(e, g):
                return e.value_load(block_expert[0:1, bass.ds(g, 1)], min_val=0, max_val=NE - 1)

            def load_piece(e, ws, k, ex):
                w, kk = k // 2, k % 2
                n_ = (KC, FC)[w] // 2
                e.dma_start(stages[w][:, kk * n_:(kk + 1) * n_, :], (w1_v, w2_v)[w][ex][:, kk * n_:(kk + 1) * n_, :]
                            ).then_inc(ws.loaded[k], 16)

            def round_piece(e, ws, k, g, s):
                e.wait_ge(ws.loaded[k], (g + 1) * 16)
                a, h_, _ = piece(k, s)
                e.activation(h_, a, ACT.Copy).then_inc(ws.rounded, 1)

            def split_piece(e, ws, k, g, s):
                after(e, ws.rounded, g, PIECES, k + 1)
                a, h_, l_ = piece(k, s)
                e.tensor_tensor(l_, a, h_.bitcast(F32), ALU.subtract).then_inc(ws.split, 1)

            return W1, W2, expert_of, load_piece, round_piece, split_piece

        def router_phase(c, expert_of, load_piece, round_piece, split_piece):
            r3 = lnw[:, 0, :]
            v3 = sbt(c, "v3", [P, NT])
            t3 = sbt(c, "t3", [P, NT])
            X3 = sbt(c, "X3", [P, 2, RT, D])
            X3H = sbt(c, "X3H", [P, 2, KC, RT * P], F32R)
            X3L = sbt(c, "X3L", [P, 2, KC, RT * P], F32R)
            wr_hi = sbt(c, "wr_hi", [P, KC, NE], F32R)
            wr_lo = sbt(c, "wr_lo", [P, KC, NE], F32R)
            LGT = sbt(c, "LGT", [NE, 2, RT * P])
            LG = sbt(c, "LG", [P, NT, NE])
            LS = sbt(c, "LS", [P, NT, NE])
            OHT = sbt(c, "OHT", [P, NE, NT])
            CS = sbt(c, "CS", [P, NE, NT])
            go_on = sbt(c, "go_on", [P, NE, NT])
            iota8 = sbt(c, "iota8", [P, NE])
            n_first = sbt(c, "n_first", [P, 2, 2, NE])
            offs = sbt(c, "offs", [P, 3, NE])
            meta = sbt(c, "meta", [P, NT, 4])
            mx = sbt(c, "mx", [P, NT])
            idx = sbt(c, "idx", [P, NT])
            rank = sbt(c, "rank", [P, NT])
            kept = sbt(c, "kept", [P, NT])
            slot_i = sbt(c, "slot_i", [P, NT], I32)
            part_i = sbt(c, "part_i", [P, 2], I32)
            batch_f = sbt(c, "batch_f", [P, 2])
            before = sbt(c, "before", [P, 4, P])
            block_iota = sbt(c, "block_iota", [P, NB])
            limits = sbt(c, "limits", [P, NBE])
            n_all = sbt(c, "n_all", [P, NE])
            over = sbt(c, "over", [P, NE, NBE])
            n_blocks = sbt(c, "n_blocks", [P, NE])
            last_block = sbt(c, "last_block", [P, NE])
            base = sbt(c, "base", [P, NE])
            passed = sbt(c, "passed", [P, NB, NE])
            block_e = sbt(c, "block_e", [P, NB])
            R = sbt(c, "R", [P, 2, RT, ROW])
            RI = sbt(c, "RI", [P, 2, RT], I32)
            TP = [pst(c, f"x3_bank{i}", [P, KC, 512]) for i in range(2)]
            LP = [pst(c, f"logit_bank{i}", [P, RT, NE]) for i in range(2)]
            LTP = [pst(c, f"logit_t_bank{i}", [P, 512]) for i in range(2)]
            OP = LP[0]
            S = {n: sem(n) for n in ("r3_sqrt", "r3_chain", "x3_made", "x3_transposed", "x3_hi", "x3_lo", "logits_made",
                                     "logits_t_copied", "logits_turned", "logits_copied", "wr_split", "route_chain", "consts_made", "exp_route", "offsets_made",
                                     "rows_made", "row_gate")}
            rows_sent = [sem("rows_sent0"), sem("rows_sent1")]

            def all_rounds(e, body):
                def run(q, at):
                    body(q, at % 2, lambda d: 0 <= at + d < NR)

                for q in range(-1, 4):
                    run(q, q)
                with e.Fori(2, NR // 2 - 1) as n:
                    for u in range(2):
                        run(n * 2 + u, 4 + u)
                for q in range(NR - 2, NR + 1):
                    run(q, q)

            with nc.Block() as block:
                @block.sync
                def _(e):
                    for b in range(B):
                        rows = slice(b * TL, (b + 1) * TL)
                        e.dma_start(out[b, 0:TT, :].rearrange("(l t) f -> l t f", l=TL), H[rows, 0:NTT, :]).then_inc(default_out, 16)
                        e.dma_start(out[b, TT:, :].rearrange("(l t) f -> l t f", l=TL), H[rows, NTT:, :]).then_inc(default_out, 16)
                    e.wait_ge(experts_known, 1)
                    ex = expert_of(e, 0)
                    for k in range(PIECES):
                        load_piece(e, main_signals, k, ex)
                    e.wait_ge(default_out, 16 * 2 * B)

                @block.gpsimd
                def _(e):
                    n_ = [0]

                    def link(ins):
                        n_[0] += 1
                        ins.then_inc(S["consts_made"], 1)
                        e.wait_ge(S["consts_made"], n_[0])

                    link(e.memset(before[:, :, :], 1.0))
                    b3 = [before[:, i, :] for i in range(3)]
                    link(e.affine_select(out=b3[0], in_=b3[0], compare_op=ALU.is_gt, fill=0.0, base=0,
                                         pattern=[[1, P]], channel_multiplier=-1))
                    for i, base in ((1, 0), (2, TL)):
                        link(e.affine_select(out=b3[i], in_=b3[i], compare_op=ALU.is_gt, fill=0.0, base=base,
                                             pattern=[[TL, B], [0, TL]], channel_multiplier=-1))
                    link(e.iota(iota8[:, :], [[1, NE]], base=0, channel_multiplier=0, allow_small_or_imprecise_dtypes=True))
                    link(e.memset(go_on[:, :, :], 1.0))
                    link(e.memset(go_on[:, :, 0:1], 0.0))
                    link(e.memset(go_on[:, :, NTT:NTT + 1], 0.0))
                    link(e.iota(block_iota[:, :], [[1, NB]], base=0, channel_multiplier=0, allow_small_or_imprecise_dtypes=True))
                    link(e.iota(limits[:, :], [[BLK, NBE]], base=0, channel_multiplier=0, allow_small_or_imprecise_dtypes=True))
                    link(e.iota(part_i[:, 0:1], [[0, 1]], base=0, channel_multiplier=1))
                    link(e.iota(mx[:, 0:NTT], [[1, NTT]], base=0, channel_multiplier=NTT, allow_small_or_imprecise_dtypes=True))
                    link(e.iota(mx[:, NTT:], [[1, NTX]], base=TT, channel_multiplier=NTX, allow_small_or_imprecise_dtypes=True))
                    e.wait_ge(slots_filled, 16 * NI)

                    def send(n, par):
                        after(e, S["rows_made"], n, 3)
                        gate(e, S["row_gate"], par)
                        for j in range(RT):
                            e.indirect_dma_start(slots, bass.IndirectOffsetOnAxis(ap=RI[:, par, j:j + 1], axis=0),
                                                 R[:, par, j, :], None, bounds_check=NB * BLK - 1, oob_is_err=False
                                                 ).then_inc(rows_sent[par], 16)
                    with e.Fori(0, NR // 2) as n:
                        for u in range(2):
                            send(n * 2 + u, u)
                    for par in range(2):
                        e.wait_ge(rows_sent[par], 16 * NT // 2)

                @block.scalar
                def _(e):
                    e.wait_ge(S["r3_chain"], 8)
                    e.activation(r3, v3[:, :], ACT.Sqrt).then_inc(S["r3_sqrt"], 1)

                    def body(q, par, of):
                        if of(1):
                            after(e, S["logits_made"], q - 1)
                            after(e, S["x3_transposed"], q + 1)
                            e.activation(X3H[:, 1 - par, :, :], TP[1 - par][:, :, :], ACT.Copy).then_inc(S["x3_hi"], 1)
                        if of(0):
                            after(e, S["logits_turned"], q - 2)
                            after(e, S["logits_made"], q)
                            e.activation(LGT[:, par, :], LTP[par][0:NE, :], ACT.Copy).then_inc(S["logits_t_copied"], 1)
                    all_rounds(e, body)
                    e.wait_ge(S["exp_route"], 1)
                    e.activation(LS[:, :, :], LS[:, :, :], ACT.Exp).then_inc(S["exp_route"], 1)
                    for k in range(PIECES):
                        round_piece(e, main_signals, k, 0, 0)

                @block.vector
                def _(e):
                    n3 = [0]

                    def link3(ins):
                        n3[0] += 1
                        ins.then_inc(S["r3_chain"], 1)
                        e.wait_ge(S["r3_chain"], n3[0])

                    whole_stats(link3, e, st, halves, t3[:, :])
                    link3(e.tensor_scalar(v3[:, :], st[:, 1, :], EPS, None, ALU.add))
                    e.wait_ge(S["r3_sqrt"], 1)
                    link3(e.reciprocal(r3, r3))
                    one_newton_step(link3, e, v3[:, :], r3, t3[:, :])

                    def x3(q, par):
                        after(e, S["x3_transposed"], q - 2)
                        for j in range(RT):
                            T = q * RT + j
                            m = e.tensor_scalar(X3[:, par, j, :], H[:, T, :], st[:, 0, bass.ds(T, 1)], lnw[:, 0, bass.ds(T, 1)],
                                                ALU.subtract, ALU.mult)
                        m.then_inc(S["x3_made"], 1)

                    e.tensor_copy(wr_hi[:, :, :], wr_t[:, :, :]).then_inc(S["wr_split"], 1)
                    e.wait_ge(S["wr_split"], 1)
                    e.tensor_tensor(wr_lo[:, :, :], wr_t[:, :, :], wr_hi[:, :, :].bitcast(F32), ALU.subtract).then_inc(S["wr_split"], 1)
                    x3(0, 0)

                    def body(q, par, of):
                        if of(2):
                            x3(q + 2, par)
                        if of(1):
                            after(e, S["logits_made"], q - 1)
                            after(e, S["x3_hi"], q + 1)
                            e.tensor_tensor(X3L[:, 1 - par, :, :], TP[1 - par][:, :, :], X3H[:, 1 - par, :, :].bitcast(F32),
                                            ALU.subtract).then_inc(S["x3_lo"], 1)
                        if of(-1):
                            after(e, S["logits_turned"], q - 1)
                            e.tensor_copy(LG[:, bass.ds(q * RT - RT, RT), :], LP[1 - par][:, :, :]).then_inc(S["logits_copied"], 1)
                    all_rounds(e, body)
                    e.wait_ge(S["logits_copied"], NR)
                    n_ = [0]

                    def link(ins):
                        n_[0] += 1
                        ins.then_inc(S["route_chain"], 1)
                        e.wait_ge(S["route_chain"], n_[0])

                    e.wait_ge(S["consts_made"], 13)
                    link(e.tensor_scalar(part_i[:, 1:2], part_i[:, 0:1], TL.bit_length() - 1, None, ALU.logical_shift_right))
                    link(e.tensor_copy(batch_f[:, 0:1], part_i[:, 1:2]))
                    link(e.tensor_scalar(batch_f[:, 1:2], batch_f[:, 0:1], float(TT + TX - TL * NTX), None, ALU.mult))
                    link(e.tensor_scalar(batch_f[:, 0:1], batch_f[:, 0:1], float(TT + TX - TL * NTT), None, ALU.mult))
                    for s, seg in enumerate((slice(0, NTT), slice(NTT, NT))):
                        link(e.tensor_scalar(meta[:, seg, 3], mx[:, seg], batch_f[:, s:s + 1], None, ALU.add))
                    link(e.tensor_reduce(mx[:, :], LG[:, :, :], AX, ALU.max))
                    mxb = mx[:, :].unsqueeze(2).broadcast_to([P, NT, NE])
                    link(e.tensor_tensor(LS[:, :, :], LG[:, :, :], mxb, ALU.subtract))
                    e.tensor_tensor(LG[:, :, :], LG[:, :, :], mxb, ALU.is_equal).then_inc(S["exp_route"], 1)
                    e.wait_ge(S["exp_route"], 2)
                    link(e.tensor_reduce(rank[:, :], LS[:, :, :], AX, ALU.add))
                    link(e.reciprocal(meta[:, :, 2], rank[:, :]))
                    iob = iota8[:, :].unsqueeze(1).broadcast_to([P, NT, NE])
                    link(e.tensor_scalar(LG[:, :, :], LG[:, :, :], -float(NE), float(NE), ALU.mult, ALU.add))
                    link(e.tensor_tensor(LG[:, :, :], LG[:, :, :], iob, ALU.add))
                    link(e.tensor_reduce(idx[:, :], LG[:, :, :], AX, ALU.min))
                    link(e.tensor_tensor(OHT[:, :, :].rearrange("p e t -> p t e"), iob,
                                         idx[:, :].unsqueeze(2).broadcast_to([P, NT, NE]), ALU.is_equal))
                    link(e.tensor_tensor_scan(CS[:, :, :].rearrange("p e t -> p (e t)"), go_on[:, :, :].rearrange("p e t -> p (e t)"),
                                              OHT[:, :, :].rearrange("p e t -> p (e t)"), 0.0, ALU.mult, ALU.add))
                    e.wait_ge(S["offsets_made"], 1)
                    link(e.tensor_copy(offs[:, :, :], OP[:, 0:3, :]))
                    for s, (a, b_) in enumerate(((0, NTT), (NTT, NT))):
                        link(e.tensor_tensor(CS[:, :, a:b_], CS[:, :, a:b_],
                                             offs[:, s, :].unsqueeze(2).broadcast_to([P, NE, b_ - a]), ALU.add))
                    link(e.tensor_tensor(CS[:, :, :], CS[:, :, :], OHT[:, :, :], ALU.mult))
                    link(e.tensor_reduce(rank[:, :], CS[:, :, :].rearrange("p e t -> p t e"), AX, ALU.add))
                    link(e.tensor_scalar(kept[:, :], rank[:, :], float(CAP), NOWHERE, ALU.is_gt, ALU.mult))
                    link(e.tensor_scalar(rank[:, :], rank[:, :], -1.0, None, ALU.add))
                    link(e.tensor_scalar(n_all[:, :], offs[:, 2, :], float(CAP), None, ALU.min))
                    link(e.tensor_tensor(over[:, :, :], n_all[:, :].unsqueeze(2).broadcast_to([P, NE, NBE]),
                                         limits[:, :].unsqueeze(1).broadcast_to([P, NE, NBE]), ALU.is_gt))
                    link(e.tensor_reduce(n_blocks[:, :], over[:, :, :], AX, ALU.add))
                    link(e.tensor_tensor_scan(last_block[:, :], before[:, 3, 0:NE], n_blocks[:, :], 0.0, ALU.mult, ALU.add))
                    link(e.tensor_tensor(base[:, :], last_block[:, :], n_blocks[:, :], ALU.subtract))
                    link(e.tensor_scalar(base[:, :], base[:, :], float(BLK), None, ALU.mult))
                    link(e.tensor_tensor(passed[:, :, :], block_iota[:, :].unsqueeze(2).broadcast_to([P, NB, NE]),
                                         last_block[:, :].unsqueeze(1).broadcast_to([P, NB, NE]), ALU.is_ge))
                    link(e.tensor_reduce(block_e[:, :], passed[:, :, :], AX, ALU.add))
                    link(e.tensor_scalar(block_e[:, :], block_e[:, :], float(NE - 1), None, ALU.min))
                    link(e.tensor_copy(blocks_used[:, :], last_block[:, NE - 1:]))
                    e.tensor_copy(block_expert[:, :], block_e[:, :]).then_inc(experts_known, 1)
                    link(e.tensor_tensor(CS[:, :, :], OHT[:, :, :], base[:, :].unsqueeze(2).broadcast_to([P, NE, NT]), ALU.mult))
                    link(e.tensor_reduce(idx[:, :], CS[:, :, :].rearrange("p e t -> p t e"), AX, ALU.add))
                    link(e.tensor_tensor(idx[:, :], idx[:, :], rank[:, :], ALU.add))
                    link(e.tensor_tensor(idx[:, :], idx[:, :], kept[:, :], ALU.add))
                    link(e.tensor_copy(slot_i[:, :], idx[:, :]))
                    link(e.tensor_copy(meta[:, :, 0], st[:, 0, :]))
                    link(e.tensor_copy(meta[:, :, 1], r3))

                    def rows(n, par):
                        e.tensor_copy(R[:, par, :, 0:D], H[:, bass.ds(n * RT, RT), :]).then_inc(S["rows_made"], 1)
                        e.tensor_copy(R[:, par, :, D:], meta[:, bass.ds(n * RT, RT), :]).then_inc(S["rows_made"], 1)
                        e.tensor_copy(RI[:, par, :], slot_i[:, bass.ds(n * RT, RT)]).then_inc(S["rows_made"], 1)
                    rows(0, 0)
                    rows(1, 1)
                    with e.Fori(1, NR // 2) as n:
                        for u in range(2):
                            after(e, S["row_gate"], n * 2 + (u - 2))
                            e.wait_ge(rows_sent[u], n * (16 * RT))
                            rows(n * 2 + u, u)
                    for k in range(PIECES):
                        split_piece(e, main_signals, k, 0, 0)

                @block.tensor
                def _(e):
                    e.wait_ge(S["wr_split"], 2)

                    def body(q, par, of):
                        if of(1):
                            after(e, S["x3_lo"], q - 1)
                            after(e, S["x3_made"], q + 1)
                            for c_ in range(KC):
                                for j in range(RT):
                                    m = e.transpose(TP[1 - par][:, c_, j * P:(j + 1) * P], X3[:, 1 - par, j, c_ * P:(c_ + 1) * P],
                                                    ident[:, :])
                            m.then_inc(S["x3_transposed"], 1)
                        if of(0):
                            after(e, S["logits_t_copied"], q - 2)
                            after(e, S["x3_lo"], q)
                            n_ = 0
                            for k in range(KC):
                                for w, a in ((wr_hi, X3H), (wr_lo, X3H), (wr_hi, X3L)):
                                    m = e.matmul(LTP[par][0:NE, :], w[:, k, :], a[:, par, k, :],
                                                 start=(n_ == 0), stop=(n_ == 3 * KC - 1))
                                    n_ += 1
                            m.then_inc(S["logits_made"], 1)
                        if of(-1):
                            after(e, S["logits_copied"], q - 3)
                            after(e, S["logits_t_copied"], q - 1)
                            for j in range(RT):
                                m = e.matmul(LP[1 - par][:, j, :], LGT[:, 1 - par, j * P:(j + 1) * P], ident[0:NE, 0:NE],
                                             start=True, stop=True)
                            m.then_inc(S["logits_turned"], 1)
                    all_rounds(e, body)
                    e.wait_ge(S["route_chain"], 15)
                    tok, text = CS[:, :, NTT - 1], CS[:, :, NT - 1]
                    for s, (m_tok, m_text) in enumerate(((0, 1), (2, 0))):
                        e.matmul(OP[:, s, :], before[:, m_tok, :], tok, start=True, stop=False)
                        e.matmul(OP[:, s, :], before[:, m_text, :], text, start=False, stop=True)
                    e.matmul(OP[:, 2, :], before[:, 3, :], tok, start=True, stop=False)
                    m = e.matmul(OP[:, 2, :], before[:, 3, :], text, start=False, stop=True)
                    m.then_inc(S["offsets_made"], 1)

        def expert_buffers(c, W1, W2):
            weight_slot(c, W1, W2)
            XE = H[:, 0:BT, :]
            Y1 = H[:, BT:2 * BT, :]
            Y = H[:, 2 * BT:4 * BT, :].rearrange("p (s t) d -> p s t d", s=2)
            b2_b = H[:, 4 * BT:4 * BT + 2, :]
            b1_e = sbt(c, "b1_e", [P, 2, FC])
            X = sbt(c, "X", [P, 2, BT, ROW])
            XEH = sbt(c, "XEH", [P, KC, BLK], F32R)
            XEL = sbt(c, "XEL", [P, KC, BLK], F32R)
            G = sbt(c, "G", [P, 2, BLK])
            GH = sbt(c, "GH", [P, FC, BLK], F32R)
            GL = sbt(c, "GL", [P, FC, BLK], F32R)
            YI = sbt(c, "YI", [P, 2, BT], I32)
            XP = [pst(c, f"xe_bank{i}", [P, 512]) for i in range(KC)]
            GP = [pst(c, f"hidden_bank{i}", [P, 512]) for i in range(2)]
            YP = [pst(c, f"y_bank{i}", [P, 512]) for i in range(BT)]
            return X, XE, XEH, XEL, G, GH, GL, Y1, Y, YI, b1_e, b2_b, XP, GP, YP

        def experts_phase(buffers, ws, n_blocks, tag, W1, W2, expert_of, load_piece, round_piece, split_piece):
            X, XE, XEH, XEL, G, GH, GL, Y1, Y, YI, b1_e, b2_b, XP, GP, YP = buffers
            first = ws.first
            tail = first > 0
            S = {n: sem(n + tag) for n in ("xe_made", "xe_transposed", "xe_hi", "xe_lo", "hidden_made", "gelu_made",
                                     "g_split", "y_made", "y_added", "store_gate", "g_rounded", "y_biased")}
            x_rows_in = [sem(f"x_rows_in{par}{tag}") for par in range(2)]
            biases_in = [sem(f"biases_in{par}{tag}") for par in range(2)]
            stored = [sem(f"stored{par}{tag}") for par in range(2)]

            def blocks(e, body):
                for g in range(2):
                    body(g, g % 2, 0, 2)
                if n_blocks > 4:
                    with e.Fori(1, n_blocks // 2 - 1) as n:
                        for u in range(2):
                            body(n * 2 + u, u, n, 2)
                for g in range(n_blocks - 2, n_blocks):
                    body(g, g % 2, g // 2, n_blocks - 1 - g)

            def where_used(program):
                if not tail:
                    return program

                def conditional(e):
                    used = e.value_load(blocks_used[0:1, 0:1], min_val=0, max_val=NB)
                    with e.If(used > first):
                        program(e)
                return conditional

            with nc.Block() as block:
                @block.sync
                @where_used
                def _(e):
                    def rows(g, par, ex):
                        e.dma_start(X[:, par, :, :], slots_v[g + first]).then_inc(x_rows_in[par], 16)
                        e.dma_start(b1_e[:, par, :], b1_t[:, bass.ds(ex * FC, FC)]).then_inc(biases_in[par], 16)
                        e.dma_start(b2_b[:, par, :], b2[ex].unsqueeze(0).broadcast_to([P, D])).then_inc(biases_in[par], 16)

                    def piece_of(k, g, ex):
                        after(e, ws.split, g - 1, PIECES, k + 1)
                        load_piece(e, ws, k, ex)

                    ex = expert_of(e, first)
                    if tail:
                        for k in range(PIECES):
                            load_piece(e, ws, k, ex)
                    rows(0, 0, ex)
                    ex = expert_of(e, first + 1)
                    for k in range(2):
                        piece_of(k, 1, ex)

                    def body(g, par, rounds, more):
                        if more >= 1:
                            ex = expert_of(e, g + (first + 1))
                            after(e, S["y_added"], g - 1, BT)
                            rows(g + 1, 1 - par, ex)
                            for k in range(2, PIECES):
                                piece_of(k, g + 1, ex)
                        if more >= 2:
                            ex = expert_of(e, g + (first + 2))
                            for k in range(2):
                                piece_of(k, g + 2, ex)
                    blocks(e, body)

                @block.gpsimd
                @where_used
                def _(e):
                    def body(g, par, rounds, more):
                        if more:
                            for k in range(2):
                                split_piece(e, ws, k, g + 1, 1 - par)
                        for t in range(BT):
                            after(e, S["y_added"], g, BT, t + 1)
                            gate(e, S["store_gate"], par, t)
                            e.indirect_dma_start(out_rows, bass.IndirectOffsetOnAxis(ap=YI[:, par, t:t + 1], axis=0),
                                                 Y[:, par, t, :], None, bounds_check=NTOK - 1, oob_is_err=False
                                                 ).then_inc(stored[par], 16)
                        if more:
                            for k in range(2, PIECES):
                                split_piece(e, ws, k, g + 1, 1 - par)
                    blocks(e, body)
                    for par in range(2):
                        e.wait_ge(stored[par], 16 * BT * n_blocks // 2)

                @block.scalar
                @where_used
                def _(e):
                    def xe_hi(g):
                        after(e, S["hidden_made"], g - 1, FC)
                        after(e, S["xe_transposed"], g)
                        for c_ in range(KC):
                            e.activation(XEH[:, c_, :], XP[c_][:, 0:BLK], ACT.Copy).then_inc(S["xe_hi"], 1)

                    if tail:
                        for k in range(PIECES):
                            round_piece(e, ws, k, 0, 0)
                    xe_hi(0)

                    def body(g, par, rounds, more):
                        e.wait_ge(biases_in[par], (rounds + 1) * 32)
                        for f in range(FC):
                            after(e, S["hidden_made"], g, FC, f + 1)
                            after(e, S["g_split"], g, FC, f - 1)
                            e.activation(G[:, f % 2, :], GP[f % 2][:, 0:BLK], ACT.Gelu,
                                         bias=b1_e[:, par, f:f + 1]).then_inc(S["gelu_made"], 1)
                        if more:
                            xe_hi(g + 1)
                            after(e, S["y_made"], g - 1, BT)
                            for k in range(PIECES):
                                round_piece(e, ws, k, g + 1, 1 - par)
                    blocks(e, body)

                @block.vector
                @where_used
                def _(e):
                    def xe(g, par, rounds):
                        after(e, S["xe_transposed"], g - 1)
                        e.wait_ge(x_rows_in[par], (rounds + 1) * 16)
                        for t in range(BT):
                            m = e.tensor_scalar(XE[:, t, :], X[:, par, t, 0:D], X[:, par, t, D:D + 1], X[:, par, t, D + 1:D + 2],
                                                ALU.subtract, ALU.mult)
                        m.then_inc(S["xe_made"], 1)

                    def xe_lo(g):
                        for c_ in range(KC):
                            after(e, S["xe_hi"], g, KC, c_ + 1)
                            e.tensor_tensor(XEL[:, c_, :], XP[c_][:, 0:BLK], XEH[:, c_, :].bitcast(F32),
                                            ALU.subtract).then_inc(S["xe_lo"], 1)

                    if tail:
                        for k in range(PIECES):
                            split_piece(e, ws, k, 0, 0)
                    xe(0, 0, 0)
                    xe_lo(0)

                    def body(g, par, rounds, more):
                        after(e, S["y_made"], g - 1, BT)
                        for f in range(FC):
                            after(e, S["gelu_made"], g, FC, f + 1)
                            e.tensor_copy(GH[:, f, :], G[:, f % 2, :]).then_inc(S["g_rounded"], 1)
                            after(e, S["g_rounded"], g, FC, f + 1)
                            e.tensor_tensor(GL[:, f, :], G[:, f % 2, :], GH[:, f, :].bitcast(F32), ALU.subtract
                                            ).then_inc(S["g_split"], 1)
                            if f == FC // 2 and more:
                                xe(g + 1, 1 - par, rounds + par)
                        if more:
                            xe_lo(g + 1)
                        e.wait_ge(biases_in[par], (rounds + 1) * 32)
                        for t in range(BT):
                            after(e, S["y_made"], g, BT, t + 1)
                            if t == 0:
                                after(e, S["store_gate"], g - 2, BT)
                                after(e, stored[par], rounds - 1, 16 * BT)
                            e.tensor_tensor(Y1[:, t, :], YP[t][:, 0:D], b2_b[:, par, :], ALU.add).then_inc(S["y_biased"], 1)
                            if t == 0:
                                e.tensor_copy(YI[:, par, :], X[:, par, :, D + 3]).then_inc(S["y_biased"], 1)
                            after(e, S["y_biased"], g, BT + 1, t + 2)
                            e.scalar_tensor_tensor(out=Y[:, par, t, :], in0=Y1[:, t, :], scalar=X[:, par, t, D + 2:D + 3],
                                                   in1=X[:, par, t, 0:D], op0=ALU.mult, op1=ALU.add).then_inc(S["y_added"], 1)
                    blocks(e, body)

                @block.tensor
                @where_used
                def _(e):
                    def transposes(g):
                        after(e, S["xe_lo"], g - 1, KC)
                        after(e, S["xe_made"], g)
                        for c_ in range(KC):
                            for t in range(BT):
                                m = e.transpose(XP[c_][:, t * P:(t + 1) * P], XE[:, t, c_ * P:(c_ + 1) * P], ident[:, :])
                        m.then_inc(S["xe_transposed"], 1)

                    transposes(0)

                    def body(g, par, rounds, more):
                        after(e, ws.split, g, PIECES, 2)
                        after(e, S["xe_lo"], g, KC)
                        for f in range(FC):
                            after(e, S["gelu_made"], g, FC, f - 1)
                            n_ = 0
                            for k in range(KC):
                                for w, a in ((W1[par][0], XEH), (W1[par][1], XEH), (W1[par][0], XEL)):
                                    m = e.matmul(GP[f % 2][:, 0:BLK], w[:, k, f * P:(f + 1) * P], a[:, k, :],
                                                 start=(n_ == 0), stop=(n_ == 3 * KC - 1))
                                    n_ += 1
                            m.then_inc(S["hidden_made"], 1)
                        if more:
                            transposes(g + 1)
                        after(e, ws.split, g, PIECES)
                        for t in range(BT):
                            after(e, S["y_added"], g - 1, BT, t + 1)
                            n_ = 0
                            for f in range(FC):
                                if t == 0:
                                    after(e, S["g_split"], g, FC, f + 1)
                                for a, w in ((GH, W2[par][0]), (GH, W2[par][1]), (GL, W2[par][0])):
                                    m = e.matmul(YP[t][:, 0:D], a[:, f, t * P:(t + 1) * P], w[:, f, :],
                                                 start=(n_ == 0), stop=(n_ == 3 * FC - 1))
                                    n_ += 1
                            m.then_inc(S["y_made"], 1)
                    blocks(e, body)

        with ExitStack() as ac:
            attn_w = [(sbt(ac, n + "_hi", [P, KC, D], F32R), sbt(ac, n + "_lo", [P, KC, D], F32R))
                      for n in ("wq", "wk", "wv", "wo")]
            bq_c = sbt(ac, "bq_c", [P, KC])
            bk_c = sbt(ac, "bk_c", [P, KC])
            bo_b = sbt(ac, "bo_b", [P, D])
            with ExitStack() as c:
                tok_phase(c, attn_w, bq_c, bk_c, bo_b)
            with ExitStack() as c:
                attention_phase(c, attn_w, bq_c, bk_c, bo_b)
        with ExitStack() as wc:
            W1, W2, *weights = weight_buffers(wc)
            with ExitStack() as c:
                router_phase(c, *weights)
            with ExitStack() as c:
                buffers = expert_buffers(c, W1, W2)
                experts_phase(buffers, main_signals, NB_MAIN, "", W1, W2, *weights)
                experts_phase(buffers, tail_signals, NB - NB_MAIN, "_tail", W1, W2, *weights)


_INS = ["x", "txt", "L0_tok_weight", "L0_tok_weighted_sum", "L0_attn_ln_g", "L0_attn_ln_b", "L0_attn_Wq", "L0_attn_bq",
        "L0_attn_Wk", "L0_attn_bk", "L0_attn_Wv", "L0_attn_bv", "L0_attn_Wo", "L0_attn_bo", "L0_ffn_router_w",
        "L0_ffn_w1", "L0_ffn_b1", "L0_ffn_w2", "L0_ffn_b2"]
_OUTS = [((B, TT + TX, D), "float32")]


def kernel(**inputs):
    import numpy as _np
    import concourse.bacc as _bacc
    from concourse import mybir as _mybir
    from concourse.bass_utils import run_bass_kernel_spmd as _run

    nc = _bacc.Bacc("TRN2", target_bir_lowering=False, num_devices=1)
    arrays, args = {}, []
    for name in _INS:
        a = _np.ascontiguousarray(inputs[name])
        arrays[f"in_{name}_dram"] = a
        args.append(nc.dram_tensor(f"in_{name}_dram", a.shape, _mybir.dt.from_np(a.dtype), kind="ExternalInput").ap())
    for i, (shape, dtype) in enumerate(_OUTS):
        dt = _mybir.dt.from_np(_np.dtype(dtype))
        args.append(nc.dram_tensor(f"out_{i}_dram", shape, dt, kind="ExternalOutput").ap())
    fusion_kernel(nc, *args)
    r = _run(nc, [arrays], core_ids=[0])
    return r.results[0]["out_0_dram"]
```
